# Optimizing a Trainium2 kernel written in Bass

```python
import numpy as np
import jax
import jax.numpy as jnp

def _softmax(x, axis=-1):
    return jax.nn.softmax(x, axis=axis)

def _gelu(x):
    return jax.nn.gelu(x, approximate=True)

def _silu(x):
    return jax.nn.silu(x)

def _sigmoid(x):
    return jax.nn.sigmoid(x)

def _layernorm(x, axis=-1, eps=1e-05):
    m = jnp.mean(x, axis=axis, keepdims=True)
    v = jnp.var(x, axis=axis, keepdims=True)
    return (x - m) / jnp.sqrt(v + eps)

def _scatter_add(tgt, idx, src, axis=0):
    return tgt.at[idx].add(src)

def _segment_sum(src, seg, n):
    return jax.ops.segment_sum(src, seg, n)
kernel_name = 'mk_flamingo_gated_d1_seqx_r2_1c6727'

def setup_inputs(seed: int=0):
    np.random.seed(seed)
    _w = jnp.asarray

    def _rec_inputs():
        import jax
        import jax.numpy as jnp
        _rk = jax.random.key(seed)
        x = -0.0002928 + 1 * jax.random.normal(jax.random.fold_in(_rk, 1), (4, 1024, 512), jnp.float32)
        _lenS = 1024 - jax.random.randint(jax.random.fold_in(_rk, 7), (4,), 0, max(1, 1024 // 4) + 1, jnp.int32)
        _lenS2 = 64 - jax.random.randint(jax.random.fold_in(_rk, 8), (4,), 0, max(1, 64 // 4) + 1, jnp.int32)
        _ctx_1024P = jax.random.normal(jax.random.fold_in(_rk, 11), (4, 16, 512), jnp.float32)
        _ctx_1024c = jax.random.dirichlet(jax.random.fold_in(_rk, 511), 0.3 * jnp.ones((16,), jnp.float32), (4, 64))
        _ctx_1024t = jnp.einsum('bsk,bkd->bsd', _ctx_1024c, _ctx_1024P)
        _ctx_1024t = _ctx_1024t * jax.lax.rsqrt(jnp.mean(jnp.square(_ctx_1024t)) + 1e-12) * 0.953939
        ctx_1024 = -1.39393e-06 + 0.999914 * (_ctx_1024t + 0.3 * jax.random.normal(jax.random.fold_in(_rk, 611), (4, 64, 512), jnp.float32))
        _g = jax.random.normal(jax.random.fold_in(_rk, 9001), (2, 1), jnp.float32)
        _g = jnp.sign(_g) * jnp.maximum(jnp.abs(_g), 1.0) + (_g == 0) * 1.0
        g_xattn = _g[0]
        g_ffn = _g[1]
        return (x, ctx_1024, g_xattn, g_ffn)
    x, ctx_1024, g_xattn, g_ffn = _rec_inputs()

    def _L0_xattn_setup():
        import jax, jax.numpy as jnp
        import numpy as np
        HIDDEN, HEADS, HEAD_DIM = (512, 16, 64)
        BSZ, SEQ = (2, 1024)
        SCALE = HEAD_DIM ** (-0.5)
        CAUSAL = True
        key = jax.random.key(seed)
        ks = jax.random.split(key, 7)
        inner = HEADS * HEAD_DIM
        init = lambda k, shape: jax.random.normal(k, shape, dtype=jnp.float32) * shape[0] ** (-0.5)
        return {'query': jax.random.normal(ks[0], (BSZ, SEQ, HIDDEN), dtype=jnp.float32), 'key': jax.random.normal(ks[1], (BSZ, SEQ, HIDDEN), dtype=jnp.float32), 'value': jax.random.normal(ks[2], (BSZ, SEQ, HIDDEN), dtype=jnp.float32), 'w_q': init(ks[3], (HIDDEN, inner)), 'w_k': init(ks[4], (HIDDEN, inner)), 'w_v': init(ks[5], (HIDDEN, inner)), 'w_o': init(ks[6], (inner, HIDDEN))}
    _L0_xattn_all = _L0_xattn_setup()
    _L0_xattn_in = {k: v for k, v in _L0_xattn_all.items() if k in ('w_q', 'w_k', 'w_v', 'w_o')}
    del _L0_xattn_all

    def _L0_ffn_setup():
        import jax, jax.numpy as jnp
        import numpy as np
        BLOCK = 32
        W_BITS = 4
        ACT_BITS = 16

        def act_qdq(x):
            qmax = 2.0 ** (ACT_BITS - 1) - 1.0
            scale = jnp.maximum(jnp.max(jnp.abs(x)) / qmax, 1e-12)
            return jnp.clip(jnp.round(x / scale), -qmax - 1.0, qmax) * scale

        def fixed_qdq_u16(x):
            scale = 1.0 / 65536.0
            return jnp.clip(jnp.round(x / scale), 0.0, 65535.0) * scale

        def lpbq_dequant(w):
            O, I = w.shape
            qmax = 2.0 ** (W_BITS - 1) - 1.0
            wb = w.reshape(O, I // BLOCK, BLOCK)
            s = jnp.maximum(jnp.max(jnp.abs(wb), axis=-1, keepdims=True) / qmax, 1e-12)
            wq = jnp.clip(jnp.round(wb / s), -qmax - 1.0, qmax) * s
            return wq.reshape(O, I)
        key = jax.random.key(seed)
        k1, k2, k3, k4 = jax.random.split(key, 4)
        B, S, H, I = (2, 2048, 512, 1536)
        x = jax.random.normal(k1, (B, S, H), jnp.float32)
        w_gate = jax.random.normal(k2, (I, H), jnp.float32) * 0.02
        w_up = jax.random.normal(k3, (I, H), jnp.float32) * 0.02
        w_down = jax.random.normal(k4, (H, I), jnp.float32) * 0.02
        return {'x': x, 'w_gate': w_gate, 'w_up': w_up, 'w_down': w_down}
    _L0_ffn_all = _L0_ffn_setup()
    _L0_ffn_in = {k: v for k, v in _L0_ffn_all.items() if k in ('w_gate', 'w_up', 'w_down')}
    del _L0_ffn_all
    return {'x': x, 'ctx_1024': ctx_1024, 'g_xattn': g_xattn, 'g_ffn': g_ffn, 'L0_xattn_w_q': _L0_xattn_in['w_q'], 'L0_xattn_w_k': _L0_xattn_in['w_k'], 'L0_xattn_w_v': _L0_xattn_in['w_v'], 'L0_xattn_w_o': _L0_xattn_in['w_o'], 'L0_ffn_w_gate': _L0_ffn_in['w_gate'], 'L0_ffn_w_up': _L0_ffn_in['w_up'], 'L0_ffn_w_down': _L0_ffn_in['w_down']}

def reference(x, ctx_1024, g_xattn, g_ffn, L0_xattn_w_q, L0_xattn_w_k, L0_xattn_w_v, L0_xattn_w_o, L0_ffn_w_gate, L0_ffn_w_up, L0_ffn_w_down):
    import jax
    import jax.numpy as jnp

    def _L0_xattn_ref(query, key, value, w_q, w_k, w_v, w_o):
        import jax, jax.numpy as jnp
        import numpy as np
        HIDDEN, HEADS, HEAD_DIM = (512, 16, 64)
        BSZ, SEQ = (2, 1024)
        SCALE = HEAD_DIM ** (-0.5)
        CAUSAL = True
        bsz, q_len, _ = query.shape
        k_len = key.shape[1]

        def split_heads(x):
            return x.reshape(x.shape[0], x.shape[1], HEADS, HEAD_DIM).transpose(0, 2, 1, 3)
        q = split_heads(query @ w_q)
        k = split_heads(key @ w_k)
        v = split_heads(value @ w_v)
        scores = jnp.einsum('bhqd,bhkd->bhqk', q, k) * SCALE
        if CAUSAL:
            q_pos = jnp.arange(q_len)
            k_pos = jnp.arange(k_len)
            mask = (k_pos[None, :] <= q_pos[:, None]).astype(scores.dtype)
            scores = scores + (1.0 - mask)[None, None, :, :] * -10000.0
        weights = jax.nn.softmax(scores, axis=-1)
        out = jnp.einsum('bhqk,bhkd->bhqd', weights, v)
        out = out.transpose(0, 2, 1, 3).reshape(bsz, q_len, HEADS * HEAD_DIM)
        return out @ w_o

    def _L0_ffn_ref(x, w_gate, w_up, w_down):
        import jax, jax.numpy as jnp
        import numpy as np
        BLOCK = 32
        W_BITS = 4
        ACT_BITS = 16

        def act_qdq(x):
            qmax = 2.0 ** (ACT_BITS - 1) - 1.0
            scale = jnp.maximum(jnp.max(jnp.abs(x)) / qmax, 1e-12)
            return jnp.clip(jnp.round(x / scale), -qmax - 1.0, qmax) * scale

        def fixed_qdq_u16(x):
            scale = 1.0 / 65536.0
            return jnp.clip(jnp.round(x / scale), 0.0, 65535.0) * scale

        def lpbq_dequant(w):
            O, I = w.shape
            qmax = 2.0 ** (W_BITS - 1) - 1.0
            wb = w.reshape(O, I // BLOCK, BLOCK)
            s = jnp.maximum(jnp.max(jnp.abs(wb), axis=-1, keepdims=True) / qmax, 1e-12)
            wq = jnp.clip(jnp.round(wb / s), -qmax - 1.0, qmax) * s
            return wq.reshape(O, I)
        x = act_qdq(x)
        up = act_qdq(x @ lpbq_dequant(w_up).T)
        gate = act_qdq(x @ lpbq_dequant(w_gate).T)
        sig = fixed_qdq_u16(jax.nn.sigmoid(gate))
        gate = act_qdq(gate * sig)
        o = act_qdq(gate * up)
        return o @ lpbq_dequant(w_down).T
    x = x + jnp.tanh(g_xattn[0]) * _L0_xattn_ref(_layernorm(x, axis=-1), ctx_1024, ctx_1024, L0_xattn_w_q, L0_xattn_w_k, L0_xattn_w_v, L0_xattn_w_o)
    x = x + jnp.tanh(g_ffn[0]) * _L0_ffn_ref(_layernorm(x, axis=-1), L0_ffn_w_gate, L0_ffn_w_up, L0_ffn_w_down)
    return x

_drawn_inputs = setup_inputs


def setup_inputs(seed=0):
    import zlib

    import numpy as np

    out = dict(_drawn_inputs(seed))
    spreads = {}
    factors = {}
    for name, (base, spread) in spreads.items():
        noise = np.random.default_rng([zlib.crc32(name.encode()), seed]).standard_normal(out[name].shape)
        drawn = base * np.exp(spread * noise) if base else spread * noise
        out[name] = jnp.asarray(drawn.astype(out[name].dtype))
    for name, factor in factors.items():
        out[name] = (out[name] * factor).astype(out[name].dtype)
    return out
```

```python
from contextlib import ExitStack

import concourse.bass as bass
from concourse import mybir

F32 = mybir.dt.float32
F32R = mybir.dt.float32r
I16 = mybir.dt.int16
U16 = mybir.dt.uint16
ALU = mybir.AluOpType
ACT = mybir.ActivationFunctionType
X = mybir.AxisListType.X
RMAX = bass.bass_isa.ReduceOp.max

P = 128
B, S, H = 4, 1024, 512
CK = 64
HEADS, HD = 16, 64
INNER = HEADS * HD
I = 1536
TOK = B * S
KT = H // P
PAIRS = HEADS // 2
IT = I // P
QT = TOK // P
BQ = S // P
FT = TOK // 512
BLK = 32
NBLK = 512 // BLK
LN_EPS = 1e-5
TINY = 1e-12
QMAX = 32767.0
SIG_ONE = 65536.0
SCALE = HD ** -0.5


def flamingo_block(nc, x, ctx, g_xattn, g_ffn, w_q, w_k, w_v, w_o, w_gate, w_up, w_down, out):
    xf = x.rearrange("b s d -> (b s) d")
    cf = ctx.rearrange("b s d -> (b s) d")
    of = out.rearrange("b s d -> (b s) d")

    wsc = [[nc.dram_tensor(f"w{n}_{part}", (P, IT * 512), F32).ap() for part in ("hi", "lo")]
           for n in ("gate", "up", "down")]
    x1_d = nc.dram_tensor("x1_d", (TOK, H), F32).ap()
    xn_d = nc.dram_tensor("xn_d", (TOK, H), F32).ap()
    xq_d = nc.dram_tensor("xq_d", (FT, P, KT * 512), I16).ap()
    gate_d = nc.dram_tensor("gate_d", (QT, P, IT * P), F32).ap()
    up_d = nc.dram_tensor("up_d", (QT, P, IT * P), F32).ap()

    with ExitStack() as top:
        def sb(scope, name, shape, dt):
            return scope.enter_context(nc.sbuf_tensor(name, shape, dt))

        def pb(scope, name, n=512):
            return scope.enter_context(nc.psum_tensor(name, [P, n], F32))

        phase_sems = []

        def sem(name):
            phase_sems.append(nc.alloc_semaphore(name=name))
            return phase_sems[-1]

        def release_sems():
            nc.clear_and_free_semaphores(phase_sems)
            nc.all_engine_barrier()
            phase_sems.clear()

        ident = sb(top, "ident", [P, P], F32)
        mask = sb(top, "mask", [P, CK], F32)
        half = sb(top, "half", [P, 2], F32)
        sc = sb(top, "sc", [P, 32], F32)
        xmx = sb(top, "xmx", [P, QT], F32)
        gmx = sb(top, "gmx", [P, 2, FT * IT], F32)
        umx = sb(top, "umx", [P, FT * IT], F32)
        fmx = sb(top, "fmx", [P, QT], F32)
        pmx = sb(top, "pmx", [P, QT], F32)
        sci = sb(top, "sci", [P, 2], I16)
        scu = sb(top, "scu", [P, 2], U16)

        def col(n):
            return sc[:, n:n + 1]

        (TG_X, TG_F, RAW_X, RAW_F, S_X, INV_X, S_G, INV_G, S_U, INV_U, C_F, S_F2, S_O, C_O, C_OUT,
         PMAX, AMAX, T0, T1, T2, T3, T4, GPOS, GNEG, AP2, AN2) = [col(n) for n in range(26)]

        with ExitStack() as att:
            wqT = sb(att, "wqT", [P, PAIRS, H], F32)
            wo = sb(att, "wo", [P, PAIRS, H], F32)
            kT = sb(att, "kT", [P, PAIRS, B * CK], F32)
            vT = sb(att, "vT", [P, PAIRS, B * CK], F32)
            prepare(nc, sb, pb, sem, cf, w_q, w_k, w_v, w_o, w_gate, w_up, w_down, g_xattn, g_ffn,
                    wsc, ident, mask, half, TG_X, TG_F, RAW_X, RAW_F, wqT, wo, kT, vT)
            release_sems()
            attend(nc, sb, pb, sem, xf, x1_d, xn_d, ident, mask, half, xmx, TG_X,
                   (S_X, INV_X, T0, T1), wqT, wo, kT, vT)
            release_sems()
        gate_phase(nc, sb, pb, sem, xn_d, xq_d, gate_d, wsc[0], ident, gmx,
                   S_X, INV_X, (GPOS, GNEG, AP2, AN2, AMAX, S_G, INV_G, T0))
        with ExitStack() as ff:
            nq = sb(ff, "nq", [P, QT, I], I16)
            up_phase(nc, sb, pb, sem, xq_d, gate_d, up_d, wsc[1], nq, umx, fmx, sci, scu, S_X,
                     (S_G, INV_G, AP2, S_F2, C_F, S_U, INV_U), (T0, T1, T2, T3, T4))
            down_phase(nc, sb, pb, sem, up_d, x1_d, of, wsc[2], nq, pmx,
                       (S_F2, S_U, INV_U, S_O, C_O, C_OUT, TG_F), (T0, T1, T2, T3))


def prepare(nc, sb, pb, sem, cf, w_q, w_k, w_v, w_o, w_gate, w_up, w_down, g_xattn, g_ffn,
            wsc, ident, mask, half, TG_X, TG_F, RAW_X, RAW_F, wqT, wo, kT, vT):
    with ExitStack() as ph:
        wq = sb(ph, "wq", [P, KT, INNER], F32)
        wk = sb(ph, "wk", [P, KT, INNER], F32)
        wv = sb(ph, "wv", [P, KT, INNER], F32)
        cx = sb(ph, "cx", [P, 2, H], F32)
        cT = sb(ph, "cT", [P, KT, B * CK], F32)
        NJ = 3
        wj = [sb(ph, f"wj{n}", [P, 512], F32) for n in range(NJ)]
        qj = [sb(ph, f"qj{n}", [P, 512], I16) for n in range(NJ)]
        dj = [sb(ph, f"dj{n}", [P, 512], F32) for n in range(NJ)]
        hj = [sb(ph, f"hj{n}", [P, 512], F32R) for n in range(NJ)]
        lj = [sb(ph, f"lj{n}", [P, 512], F32R) for n in range(NJ)]
        bm = sb(ph, "bm", [P, NJ, NBLK], F32)
        bs = sb(ph, "bs", [P, NJ, NBLK], F32)
        bi = sb(ph, "bi", [P, NJ, NBLK], F32)
        pj = [pb(ph, f"pj{n}") for n in range(NJ)]
        pw = [pb(ph, f"pw{n}") for n in range(2)]
        pk = pb(ph, "pk")
        pv = pb(ph, "pv")

        ctx_in = sem("ctx_in")
        wq_in, wk_in, wv_in, wo_in, g_in = (sem(n) for n in ("wq_in", "wk_in", "wv_in", "wo_in", "g_in"))
        wj_in = [sem(f"wj_in{n}") for n in range(NJ)]
        id_set, const_set, half_set, tanh_done = sem("id_set"), sem("const_set"), sem("half_set"), sem("tanh_done")
        ctxT_ps, ctxT_sb = sem("ctxT_ps"), sem("ctxT_sb")
        wqT_ps, wqT_sb, k_ps, k_sb, v_ps, v_sb = (sem(n) for n in ("wqT_ps", "wqT_sb", "k_ps", "k_sb", "v_ps", "v_sb"))
        bmax_done, bscale_done, binv_done = sem("bmax_done"), sem("bscale_done"), sem("binv_done")
        wdiv_done = sem("wdiv_done")
        wint_done, wdeq_done, wT_ps, whi_done, wlo_done = (sem(n) for n in ("wint_done", "wdeq_done", "wT_ps", "whi_done", "wlo_done"))
        wst = [sem(f"wst{n}") for n in range(NJ)]
        block = ph.enter_context(nc.Block())

        RJ = 9
        ROUNDS = 4
        jobs = [(kind, c) for c in range(3) for kind in range(3)]
        src = [w_gate.rearrange("(r c p) k -> r c p k", r=ROUNDS, p=P),
               w_up.rearrange("(r c p) k -> r c p k", r=ROUNDS, p=P),
               w_down.rearrange("(r p) (c k) -> r c p k", p=P, c=3)]

        def store(sp, r, j, kind, c):
            n = j % NJ
            sp.wait_ge(whi_done, r * RJ + j + 1)
            sp.wait_ge(wlo_done, r * RJ + j + 1)
            for part, t in enumerate((hj[n], lj[n])):
                if kind < 2:
                    dst = wsc[kind][part][:, bass.ds(r * (3 * 512) + c * 512, 512)]
                    sp.dma_start(dst, t[:, :].bitcast(F32)).then_inc(wst[n], 16)
                else:
                    dst = wsc[2][part].rearrange("p (i h) -> p i h", h=H)[:, 4 * c:4 * c + 4, bass.ds(r * P, P)]
                    sp.dma_start(dst, t[:, :].bitcast(F32).rearrange("p (i h) -> p i h", h=P)).then_inc(wst[n], 16)

        def hi_part(act, r, j):
            n = j % NJ
            act.wait_ge(wst[n], r * (RJ // NJ * 32) + 32 * (j // NJ))
            act.wait_ge(wT_ps, r * RJ + j + 1)
            act.activation(hj[n][:, :], pj[n][:, :], ACT.Copy).then_inc(whi_done, 1)

        @block.sync
        def _(sp):
            sp.dma_start(cx[:, :, :], cf.rearrange("(t p) d -> p t d", p=P)).then_inc(ctx_in, 16)
            sp.dma_start(wq[:, :, :], w_q.rearrange("(t p) n -> p t n", p=P)).then_inc(wq_in, 16)
            sp.dma_start(wk[:, :, :], w_k.rearrange("(t p) n -> p t n", p=P)).then_inc(wk_in, 16)
            sp.dma_start(wv[:, :, :], w_v.rearrange("(t p) n -> p t n", p=P)).then_inc(wv_in, 16)
            sp.dma_start(wo[:, :, :], w_o.rearrange("(t p) n -> p t n", p=P)).then_inc(wo_in, 16)
            sp.wait_ge(wo_in, 16)
            with sp.Fori(0, ROUNDS) as r:
                for j in range(RJ + 2):
                    if j < RJ:
                        kind, c = jobs[j]
                        if j >= NJ - 1:
                            sp.wait_ge(wdeq_done, r * RJ + j - NJ + 1)
                        sp.dma_start(wj[j % NJ][:, :], src[kind][bass.ds(r, 1), c, :, :].rearrange("a p k -> (a p) k"))\
                          .then_inc(wj_in[j % NJ], 16)
                    if j >= 2:
                        store(sp, r, j - 2, *jobs[j - 2])
            for n in range(NJ):
                sp.wait_ge(wst[n], 32 * (ROUNDS * RJ // NJ))

        @block.gpsimd
        def _(pool):
            pool.memset(ident[:, :], 0.0).then_inc(const_set, 1)
            pool.memset(mask[:, :], 0.0).then_inc(const_set, 1)
            pool.memset(half[:, 0:1], -0.5).then_inc(half_set, 1)
            pool.memset(half[:, 1:2], LN_EPS).then_inc(half_set, 1)
            pool.wait_ge(const_set, 2)
            pool.affine_select(out=ident[:, :], in_=ident[:, :], compare_op=ALU.not_equal, fill=1.0,
                               base=0, pattern=[[-1, P]], channel_multiplier=1).then_inc(id_set, 1)
            pool.affine_select(out=mask[:, :], in_=mask[:, :], compare_op=ALU.is_ge, fill=-10000.0,
                               base=0, pattern=[[-1, CK]], channel_multiplier=1).then_inc(id_set, 1)
            with pool.Fori(0, ROUNDS) as r:
                for j in range(RJ):
                    n = j % NJ
                    pool.wait_ge(binv_done, r * RJ + j + 1)
                    pool.tensor_tensor(wj[n][:, :].rearrange("p (b k) -> p b k", k=BLK),
                                       wj[n][:, :].rearrange("p (b k) -> p b k", k=BLK),
                                       bi[:, n, :].unsqueeze(2).to_broadcast([P, NBLK, BLK]),
                                       ALU.mult).then_inc(wdiv_done, 1)

        @block.scalar
        def _(act):
            act.dma_start(RAW_X, g_xattn.unsqueeze(0).to_broadcast([P, 1])).then_inc(g_in, 16)
            act.dma_start(RAW_F, g_ffn.unsqueeze(0).to_broadcast([P, 1])).then_inc(g_in, 16)
            for kt in range(2):
                act.wait_ge(ctxT_ps, kt + 1)
                act.activation(cT[:, 2 * kt:2 * kt + 2, :].rearrange("p a b -> p (a b)"), pw[kt][:, :],
                               ACT.Copy).then_inc(ctxT_sb, 1)
            act.wait_ge(g_in, 32)
            act.activation(TG_X, RAW_X, ACT.Tanh).then_inc(tanh_done, 1)
            act.activation(TG_F, RAW_F, ACT.Tanh).then_inc(tanh_done, 1)
            with act.Fori(0, ROUNDS) as r:
                for j in range(RJ):
                    if j == 0:
                        for a in range(2):
                            act.wait_ge(wqT_ps, 2 * r + a + 1)
                            act.activation(wqT[:, bass.ds(2 * r + a, 1), :].rearrange("p a b -> p (a b)"), pw[a][:, :],
                                           ACT.Copy).then_inc(wqT_sb, 1)
                    if j == 3:
                        act.wait_ge(k_ps, r + 1)
                        act.activation(kT[:, bass.ds(2 * r, 2), :].rearrange("p a b -> p (a b)"), pk[:, :],
                                       ACT.Copy).then_inc(k_sb, 1)
                    if j == 6:
                        act.wait_ge(v_ps, r + 1)
                        act.activation(vT[:, bass.ds(2 * r, 2), :].rearrange("p a b -> p (a b)"), pv[:, :],
                                       ACT.Copy).then_inc(v_sb, 1)
                    if j >= 1:
                        hi_part(act, r, j - 1)
                hi_part(act, r, RJ - 1)
            act.wait_ge(tanh_done, 2)

        @block.vector
        def _(dve):
            with dve.Fori(0, ROUNDS) as r:
                for j in range(RJ + 1):
                    n = j % NJ
                    if j < RJ:
                        dve.wait_ge(wj_in[n], r * (RJ // NJ * 16) + 16 * (j // NJ + 1))
                        dve.tensor_reduce(bm[:, n, :], wj[n][:, :].rearrange("p (b k) -> p b k", k=BLK), X, ALU.max,
                                          apply_absolute_value=True).then_inc(bmax_done, 1)
                        dve.wait_ge(bmax_done, r * RJ + j + 1)
                        dve.tensor_scalar(bs[:, n, :], bm[:, n, :], 1.0 / 7.0, TINY, ALU.mult, ALU.max).then_inc(bscale_done, 1)
                    if j >= 1:
                        m = (j - 1) % NJ
                        dve.wait_ge(wT_ps, r * RJ + max(j - NJ, 0))
                        dve.wait_ge(wdiv_done, r * RJ + j)
                        dve.tensor_scalar(qj[m][:, :], wj[m][:, :], 1.0, None, ALU.mult).then_inc(wint_done, 1)
                        dve.wait_ge(wint_done, r * RJ + j)
                        dve.tensor_tensor(dj[m][:, :].rearrange("p (b k) -> p b k", k=BLK),
                                          qj[m][:, :].rearrange("p (b k) -> p b k", k=BLK),
                                          bs[:, m, :].unsqueeze(2).to_broadcast([P, NBLK, BLK]),
                                          ALU.mult).then_inc(wdeq_done, 1)
                    if j < RJ:
                        dve.wait_ge(bscale_done, r * RJ + j + 1)
                        dve.reciprocal(bi[:, n, :], bs[:, n, :]).then_inc(binv_done, 1)
                    if j >= 1:
                        dve.wait_ge(wst[m], r * (RJ // NJ * 32) + 32 * ((j - 1) // NJ))
                        dve.wait_ge(whi_done, r * RJ + j)
                        dve.tensor_tensor(lj[m][:, :], pj[m][:, :], hj[m][:, :].bitcast(F32), ALU.subtract).then_inc(wlo_done, 1)
        @block.tensor
        def _(pe):
            pe.wait_ge(id_set, 1)
            pe.wait_ge(ctx_in, 16)
            for kt in range(KT):
                for t in range(2):
                    mm = pe.transpose(pw[kt // 2][:, (kt % 2) * 256 + t * P:(kt % 2) * 256 + (t + 1) * P],
                                      cx[:, t, kt * P:(kt + 1) * P], ident[:, :])
                if kt % 2:
                    mm.then_inc(ctxT_ps, 1)
            for r in range(ROUNDS):
                if r == 0:
                    pe.wait_ge(ctxT_sb, 2)
                    pe.wait_ge(wq_in, 16)
                for j in range(RJ):
                    n = j % NJ
                    if j == 0:
                        if r:
                            pe.wait_ge(wqT_sb, 2 * r)
                        for a in range(2):
                            for kt in range(KT):
                                mm = pe.transpose(pw[a][:, kt * P:(kt + 1) * P],
                                                  wq[:, kt, (2 * r + a) * P:(2 * r + a + 1) * P], ident[:, :])
                            mm.then_inc(wqT_ps, 1)
                    if j in (3, 6):
                        w, ps, s_in, s_ps, s_sb = (wk, pk, wk_in, k_ps, k_sb) if j == 3 else (wv, pv, wv_in, v_ps, v_sb)
                        pe.wait_ge(s_in, 16)
                        if r:
                            pe.wait_ge(s_sb, r)
                        for a in range(2):
                            for kt in range(KT):
                                mm = pe.matmul(ps[:, a * 256:(a + 1) * 256], w[:, kt, (2 * r + a) * P:(2 * r + a + 1) * P],
                                               cT[:, kt, :], start=(kt == 0), stop=(kt == KT - 1))
                        mm.then_inc(s_ps, 1)
                    g = r * RJ + j
                    if g >= NJ:
                        pe.wait_ge(wlo_done, g - NJ + 1)
                    pe.wait_ge(wdeq_done, g + 1)
                    for kt in range(4):
                        mm = pe.transpose(pj[n][:, kt * P:(kt + 1) * P], dj[n][:, kt * P:(kt + 1) * P], ident[:, :])
                    mm.then_inc(wT_ps, 1)


def attend(nc, sb, pb, sem, xf, x1_d, xn_d, ident, mask, half, xmx, TG_X, cols, wqT, wo, kT, vT):
    S_X, INV_X, T0, T1 = cols
    with ExitStack() as ph:
        kbd = sb(ph, "kbd", [P, PAIRS, P], F32)
        vbd = sb(ph, "vbd", [P, PAIRS, P], F32)
        Ah = sb(ph, "Ah", [P, KT, INNER], F32R)
        Al = sb(ph, "Al", [P, KT, INNER], F32R)
        Vh = sb(ph, "Vh", [P, PAIRS, H], F32R)
        Vl = sb(ph, "Vl", [P, PAIRS, H], F32R)
        NX = BQ
        xin = [sb(ph, f"xin{n}", [P, H], F32) for n in range(NX)]
        xn = [sb(ph, f"xn{n}", [P, H], F32) for n in range(2)]
        xh = [sb(ph, f"xh{n}", [P, H], F32R) for n in range(2)]
        xl = [sb(ph, f"xl{n}", [P, H], F32R) for n in range(2)]
        pr = [sb(ph, f"pr{n}", [P, INNER], F32) for n in range(2)]
        pTh = sb(ph, "pTh", [P, INNER], F32R)
        pTl = sb(ph, "pTl", [P, INNER], F32R)
        x1 = [sb(ph, f"x1{n}", [P, H], F32) for n in range(2)]
        x2 = [sb(ph, f"x2{n}", [P, H], F32) for n in range(2)]
        st = sb(ph, "st", [P, 2, 6], F32)
        mv = sb(ph, "mv", [P, 2, 2], F32)
        rs = sb(ph, "rs", [P, 2, 2], F32)
        st2 = sb(ph, "st2", [P, 2, 6], F32)
        mv2 = sb(ph, "mv2", [P, 2, 2], F32)
        rs2 = sb(ph, "rs2", [P, 2, 2], F32)
        smx = sb(ph, "smx", [P, 2, HEADS], F32)
        ssum = sb(ph, "ssum", [P, 2, HEADS], F32)
        srec = sb(ph, "srec", [P, 2, HEADS], F32)
        pS = [pb(ph, f"pS{n}", 1024) for n in range(2)]
        pT = pb(ph, "pT", 1024)
        pX = pb(ph, "pX")
        pO = pb(ph, "pO")
        chunk = [pS[0][:, 0:512], pS[0][:, 512:1024], pS[1][:, 0:512], pS[1][:, 512:1024]]

        names = """bd_zero kbd_set vbd_set ch_ps ch_hi ch_lo
            stats_done mean_done eps_done rstd_done xn_done xT_ps xh_done xl_done
            s_ps masked max_done sub_done exp_done sum_done rec_done prob_done pT_ps pTh_done pTl_done
            o_ps x1_done stats2_done mean2_done eps2_done rstd2_done x2_done x2max_done
            sx_red sx_all sx_scale apart""".split()
        sems = {n: sem(n) for n in names}
        (bd_zero, kbd_set, vbd_set, ch_ps, ch_hi, ch_lo,
         stats_done, mean_done, eps_done, rstd_done, xn_done, xT_ps, xh_done, xl_done,
         s_ps, masked, max_done, sub_done, exp_done, sum_done, rec_done, prob_done, pT_ps, pTh_done, pTl_done,
         o_ps, x1_done, stats2_done, mean2_done, eps2_done, rstd2_done, x2_done, x2max_done,
         sx_red, sx_all, sx_scale, apart) = [sems[n] for n in names]
        x_in = [sem(f"x_in{n}") for n in range(NX)]
        x1_out = [sem(f"x1_out{n}") for n in range(2)]
        x2_out = [sem(f"x2_out{n}") for n in range(2)]
        block = ph.enter_context(nc.Block())

        STEPS = range(-2, BQ + 3)
        NCH = 16

        def tile_wait(eng, s, b, j):
            if j + 1 >= 0:
                eng.wait_ge(s, b * BQ + (j + 1))

        def have(j):
            return 0 <= j < BQ

        def rstd(pool, b, j, mv_, rs_, mean_s, eps_s, rstd_s):
            tile_wait(pool, mean_s, b, j)
            if j >= 2:
                tile_wait(pool, xn_done if rs_ is rs else x2_done, b, j - 2)
            pool.tensor_tensor(rs_[:, j % 2, 0:1], mv_[:, j % 2, 1:2], half[:, 1:2], ALU.add).then_inc(eps_s, 1)
            tile_wait(pool, eps_s, b, j)
            pool.tensor_tensor(rs_[:, j % 2, 1:2], rs_[:, j % 2, 0:1], half[:, 0:1], ALU.pow).then_inc(rstd_s, 1)

        def stored(eng, s, b, j):
            if j // 2 >= 0:
                eng.wait_ge(s, b * (16 * BQ // 2) + 16 * (j // 2))

        def scores_down(dve, b, j):
            n = j % 2
            s3 = pS[n][:, :].rearrange("p (h c) -> p h c", c=CK)
            p3 = pr[n][:, :].rearrange("p (h c) -> p h c", c=CK)
            tile_wait(dve, s_ps, b, j)
            tile_wait(dve, pT_ps, b, j - 2)
            src = s3
            if j == 0:
                dve.tensor_tensor(p3, s3, mask[:, :].unsqueeze(1).to_broadcast([P, HEADS, CK]), ALU.add).then_inc(masked, 1)
                dve.wait_ge(masked, b + 1)
                src = p3
            dve.tensor_reduce(smx[:, n, :], src, X, ALU.max).then_inc(max_done, 1)
            tile_wait(dve, max_done, b, j)
            dve.tensor_tensor(p3, src, smx[:, n, :].unsqueeze(2).to_broadcast([P, HEADS, CK]), ALU.subtract).then_inc(sub_done, 1)

        def sums(dve, b, j):
            n = j % 2
            tile_wait(dve, exp_done, b, j)
            dve.tensor_reduce(ssum[:, n, :], pr[n][:, :].rearrange("p (h c) -> p h c", c=CK), X, ALU.add).then_inc(sum_done, 1)
            tile_wait(dve, sum_done, b, j)
            tile_wait(dve, prob_done, b, j - 2)
            dve.reciprocal(srec[:, n, :], ssum[:, n, :]).then_inc(rec_done, 1)

        def statistics(dve, b, j):
            n = j % 2
            dve.wait_ge(x_in[j], b * 16 + 16)
            tile_wait(dve, mean_done, b, j - 2)
            dve.bn_stats(st[:, n, :], xin[j][:, :]).then_inc(stats_done, 1)
            tile_wait(dve, stats_done, b, j)
            tile_wait(dve, xn_done, b, j - 2)
            dve.sem_inc(apart, 1)
            dve.bn_aggr(mv[:, n, :], st[:, n, :]).then_inc(mean_done, 1)

        def residual(dve, b, j):
            n = j % 2
            tile_wait(dve, o_ps, b, j)
            stored(dve, x1_out[n], b, j)
            tile_wait(dve, x2_done, b, j - 2)
            dve.scalar_tensor_tensor(out=x1[n][:, :], in0=pO[:, :], scalar=TG_X, in1=xin[j][:, :],
                                     op0=ALU.mult, op1=ALU.add).then_inc(x1_done, 1)
            tile_wait(dve, x1_done, b, j)
            dve.bn_stats(st2[:, n, :], x1[n][:, :]).then_inc(stats2_done, 1)
            tile_wait(dve, stats2_done, b, j)
            dve.sem_inc(apart, 1)
            dve.bn_aggr(mv2[:, n, :], st2[:, n, :]).then_inc(mean2_done, 1)

        @block.sync
        def _(sp):
            with sp.Fori(0, B) as b:
                for j in range(BQ):
                    if j == 0:
                        sp.wait_ge(x1_done, b * BQ)
                    sp.dma_start(xin[j][:, :], xf[bass.ds(b * S + j * P, P), :]).then_inc(x_in[j], 16)
                for j in range(BQ):
                    tile_wait(sp, x1_done, b, j)
                    sp.dma_start(x1_d[bass.ds(b * S + j * P, P), :], x1[j % 2][:, :]).then_inc(x1_out[j % 2], 16)
                    tile_wait(sp, x2_done, b, j)
                    sp.dma_start(xn_d[bass.ds(b * S + j * P, P), :], x2[j % 2][:, :]).then_inc(x2_out[j % 2], 16)
            for n in range(2):
                sp.wait_ge(x1_out[n], 16 * QT // 2)
                sp.wait_ge(x2_out[n], 16 * QT // 2)

        @block.gpsimd
        def _(pool):
            pool.memset(kbd[:, :, :], 0.0).then_inc(bd_zero, 1)
            pool.memset(vbd[:, :, :], 0.0).then_inc(bd_zero, 1)
            with pool.Fori(0, B) as b:
                for k in STEPS:
                    if have(k + 2):
                        rstd(pool, b, k + 2, mv, rs, mean_done, eps_done, rstd_done)
                    if have(k - 3):
                        rstd(pool, b, k - 3, mv2, rs2, mean2_done, eps2_done, rstd2_done)
                    if have(k - 1):
                        j = k - 1
                        tile_wait(pool, rec_done, b, j)
                        p3 = pr[j % 2][:, :].rearrange("p (h c) -> p h c", c=CK)
                        pool.tensor_tensor(p3, p3, srec[:, j % 2, :].unsqueeze(2).to_broadcast([P, HEADS, CK]),
                                           ALU.mult).then_inc(prob_done, 1)
            pool.wait_ge(sx_red, 1)
            pool.partition_all_reduce(T1, T0, P, RMAX).then_inc(sx_all, 1)

        @block.scalar
        def _(act):
            act.wait_ge(bd_zero, 2)
            with act.Fori(0, B) as b:
                for bd, t, s in ((kbd, kT, kbd_set), (vbd, vT, vbd_set)):
                    for a in range(2):
                        rows = slice(a * 64, a * 64 + 64)
                        act.activation(bd[rows, :, a * 64:a * 64 + 64], t[rows, :, bass.ds(b * CK, CK)], ACT.Copy).then_inc(s, 1)
                for n in range(NCH):
                    act.wait_ge(ch_ps, b * NCH + n + 1)
                    dst = Ah[:, n // 2, (n % 2) * 512:(n % 2 + 1) * 512] if n < 8 else Vh[:, n - 8, :]
                    act.activation(dst, chunk[n % 4], ACT.Copy, scale=SCALE if n < 8 else 1.0).then_inc(ch_hi, 1)
                for k in STEPS:
                    if have(k - 2):
                        tile_wait(act, o_ps, b, k - 3)
                        tile_wait(act, pT_ps, b, k - 2)
                        act.activation(pTh[:, :], pT[:, :], ACT.Copy).then_inc(pTh_done, 1)
                    if have(k - 1):
                        j = k - 1
                        tile_wait(act, sub_done, b, j)
                        act.activation(pr[j % 2][:, :], pr[j % 2][:, :], ACT.Exp).then_inc(exp_done, 1)
                    if have(k + 1):
                        j = k + 1
                        tile_wait(act, xT_ps, b, j)
                        if j >= 2:
                            tile_wait(act, s_ps, b, j - 2)
                        act.activation(xh[j % 2][:, :], pX[:, :], ACT.Copy).then_inc(xh_done, 1)

        @block.vector
        def _(dve):
            with dve.Fori(0, B) as b:
                for n in range(NCH):
                    dve.wait_ge(ch_hi, b * NCH + n + 1)
                    if n < 8:
                        cols_ = slice((n % 2) * 512, (n % 2 + 1) * 512)
                        dve.scalar_tensor_tensor(out=Al[:, n // 2, cols_], in0=chunk[n % 4], scalar=SCALE,
                                                 in1=Ah[:, n // 2, cols_].bitcast(F32), op0=ALU.mult,
                                                 op1=ALU.subtract).then_inc(ch_lo, 1)
                    else:
                        dve.tensor_tensor(Vl[:, n - 8, :], chunk[n % 4], Vh[:, n - 8, :].bitcast(F32),
                                          ALU.subtract).then_inc(ch_lo, 1)
                for k in STEPS:
                    if have(k - 2):
                        tile_wait(dve, pTh_done, b, k - 2)
                        dve.tensor_tensor(pTl[:, :], pT[:, :], pTh[:, :].bitcast(F32), ALU.subtract).then_inc(pTl_done, 1)
                    if have(k - 1):
                        scores_down(dve, b, k - 1)
                    if have(k + 2):
                        statistics(dve, b, k + 2)
                    if have(k - 3):
                        residual(dve, b, k - 3)
                    if have(k - 1):
                        sums(dve, b, k - 1)
                    if have(k + 2):
                        j = k + 2
                        tile_wait(dve, rstd_done, b, j)
                        if j >= 2:
                            tile_wait(dve, xT_ps, b, j - 2)
                        dve.tensor_scalar(xn[j % 2][:, :], xin[j][:, :], mv[:, j % 2, 0:1], rs[:, j % 2, 1:2],
                                          ALU.subtract, ALU.mult).then_inc(xn_done, 1)
                    if have(k - 3):
                        j = k - 3
                        tile_wait(dve, rstd2_done, b, j)
                        stored(dve, x2_out[j % 2], b, j)
                        tile_wait(dve, x2max_done, b, j - 2)
                        dve.tensor_scalar(x2[j % 2][:, :], x1[j % 2][:, :], mv2[:, j % 2, 0:1], rs2[:, j % 2, 1:2],
                                          ALU.subtract, ALU.mult).then_inc(x2_done, 1)
                        tile_wait(dve, x2_done, b, j)
                        dve.tensor_reduce(xmx[:, bass.ds(b * BQ + j, 1)], x2[j % 2][:, :], X, ALU.max,
                                          apply_absolute_value=True).then_inc(x2max_done, 1)
                    if have(k + 1):
                        j = k + 1
                        tile_wait(dve, xh_done, b, j)
                        if j >= 2:
                            tile_wait(dve, s_ps, b, j - 2)
                        dve.tensor_tensor(xl[j % 2][:, :], pX[:, :], xh[j % 2][:, :].bitcast(F32), ALU.subtract).then_inc(xl_done, 1)
            dve.wait_ge(x2max_done, QT)
            dve.tensor_reduce(T0, xmx[:, :], X, ALU.max).then_inc(sx_red, 1)
            dve.wait_ge(sx_all, 1)
            dve.tensor_scalar(S_X, T1, 1.0 / QMAX, TINY, ALU.mult, ALU.max).then_inc(sx_scale, 1)
            dve.wait_ge(sx_scale, 1)
            dve.reciprocal(INV_X, S_X).then_inc(sx_scale, 1)
            dve.wait_ge(sx_scale, 2)

        @block.tensor
        def _(pe):
            with pe.Fori(0, B) as b:
                for n in range(NCH):
                    if n >= 4:
                        pe.wait_ge(ch_lo, b * NCH + n - 3)
                    else:
                        pe.wait_ge(sub_done, b * BQ)
                    if n < 8:
                        if n == 0:
                            pe.wait_ge(kbd_set, 2 * b + 2)
                        for q in range(4):
                            pair = (n % 2) * 4 + q
                            mm = pe.matmul(chunk[n % 4][:, q * P:(q + 1) * P], wqT[:, pair, (n // 2) * P:(n // 2 + 1) * P],
                                           kbd[:, pair, :], start=True, stop=True)
                    else:
                        if n == 8:
                            pe.wait_ge(vbd_set, 2 * b + 2)
                        mm = pe.matmul(chunk[n % 4], vbd[:, n - 8, :], wo[:, n - 8, :], start=True, stop=True)
                    mm.then_inc(ch_ps, 1)
                for k in STEPS:
                    if have(k - 2):
                        j = k - 2
                        tile_wait(pe, prob_done, b, j)
                        tile_wait(pe, pTl_done, b, j - 1)
                        for p in range(PAIRS):
                            mm = pe.transpose(pT[:, p * P:(p + 1) * P], pr[j % 2][:, p * P:(p + 1) * P], ident[:, :])
                        mm.then_inc(pT_ps, 1)
                    if have(k):
                        if k == 0:
                            pe.wait_ge(ch_lo, (b + 1) * NCH)
                        tile_wait(pe, xl_done, b, k)
                        tile_wait(pe, sub_done, b, k - 2)
                        for kt in range(KT):
                            cs = slice(kt * P, (kt + 1) * P)
                            for xs, As in ((xh, Ah), (xh, Al), (xl, Ah)):
                                for hf in range(2):
                                    mm = pe.matmul(pS[k % 2][:, hf * 512:(hf + 1) * 512], xs[k % 2][:, cs],
                                                   As[:, kt, hf * 512:(hf + 1) * 512],
                                                   start=(kt == 0 and xs is xh and As is Ah),
                                                   stop=(kt == KT - 1 and xs is xl))
                        mm.then_inc(s_ps, 1)
                    if have(k + 1):
                        j = k + 1
                        tile_wait(pe, xn_done, b, j)
                        tile_wait(pe, xl_done, b, j - 1)
                        for kt in range(KT):
                            mm = pe.transpose(pX[:, kt * P:(kt + 1) * P], xn[j % 2][:, kt * P:(kt + 1) * P], ident[:, :])
                        mm.then_inc(xT_ps, 1)
                    if have(k - 2):
                        j = k - 2
                        tile_wait(pe, pTl_done, b, j)
                        tile_wait(pe, x1_done, b, j - 1)
                        for p in range(PAIRS):
                            cs = slice(p * P, (p + 1) * P)
                            for ps_, vs in ((pTh, Vh), (pTh, Vl), (pTl, Vh)):
                                mm = pe.matmul(pO[:, :], ps_[:, cs], vs[:, p, :],
                                               start=(p == 0 and ps_ is pTh and vs is Vh),
                                               stop=(p == PAIRS - 1 and ps_ is pTl))
                        mm.then_inc(o_ps, 1)


def gate_phase(nc, sb, pb, sem, xn_d, xq_d, gate_d, w_d, ident, gmx, S_X, INV_X, cols):
    GPOS, GNEG, AP2, AN2, AMAX, S_G, INV_G, T0 = cols
    with ExitStack() as ph:
        Wh = sb(ph, "gWh", [P, IT, 512], F32R)
        Wl = sb(ph, "gWl", [P, IT, 512], F32R)
        xr = [sb(ph, f"xr{n}", [P, 4, H], F32) for n in range(2)]
        xq = [sb(ph, f"gxq{n}", [P, KT, 512], I16) for n in range(2)]
        xh = [sb(ph, f"gxh{n}", [P, KT, 512], F32R) for n in range(2)]
        xl = [sb(ph, f"gxl{n}", [P, KT, 512], F32R) for n in range(2)]
        NS = 4
        stage = [sb(ph, f"gst{n}", [P, 512], F32) for n in range(NS)]
        pX = [pb(ph, f"gpX{n}") for n in range(4)]
        pG = [pb(ph, f"gpG{n}") for n in range(3)]
        w_in = [sem(f"g_w_in{n}") for n in range(4)]
        xr_in = [sem(f"g_xr_in{n}") for n in range(2)]
        xq_out = [sem(f"g_xq_out{n}") for n in range(2)]
        st_out = [sem(f"g_st_out{n}") for n in range(NS)]
        xT_ps, xq_done, xh_done, xl_done, g_ps, g_sb, g_pos, g_neg = (sem(f"g_{n}") for n in
            ("xT_ps", "xq_done", "xh_done", "xl_done", "ps", "sb", "pos", "neg"))
        red, all_, scl = sem("g_red"), sem("g_all"), sem("g_scl")
        block = ph.enter_context(nc.Block())

        def xn_pad(d, i, t):
            nxt = (i + 1) % (FT // 2)
            return d[bass.ds(nxt * 1024 + t * 512, 512), :].rearrange("(q p) d -> p q d", p=P)

        def parts(act, i, t):
            T = 2 * i + t
            for kt in range(KT):
                act.wait_ge(xT_ps, KT * T + kt + 1)
                if kt == 0:
                    act.wait_ge(xq_out[t], 16 * i)
                act.activation(xq[t][:, kt, :], pX[kt][:, :], ACT.Copy, scale=INV_X).then_inc(xq_done, 1)
            act.wait_ge(xq_done, KT * T + KT)
            act.activation(xh[t][:, :, :], xq[t][:, :, :], ACT.Copy).then_inc(xh_done, 1)

        @block.sync
        def _(sp):
            for t in range(2):
                sp.dma_start(xr[t][:, :, :], xn_d[t * 512:(t + 1) * 512, :].rearrange("(q p) d -> p q d", p=P)).then_inc(xr_in[t], 16)
                for c in (0, 1) if t == 0 else (2, 3):
                    for W, d in ((Wh, w_d[0]), (Wl, w_d[1])):
                        sp.dma_start(W[:, 3 * c:3 * c + 3, :].bitcast(F32),
                                     d.rearrange("p (i k) -> p i k", k=512)[:, 3 * c:3 * c + 3, :]).then_inc(w_in[c], 16)
            with sp.Fori(0, FT // 2) as i:
                for t in range(2):
                    T = 2 * i + t
                    sp.wait_ge(xq_done, KT * T + KT)
                    sp.dma_start(xq_d[bass.ds(T, 1), :, :].rearrange("a p k -> (a p) k"),
                                 xq[t][:, :, :].rearrange("p k n -> p (k n)")).then_inc(xq_out[t], 16)
                    nxt = (T + 2) if t < 2 else T
                    sp.wait_ge(xT_ps, KT * T + KT)
                    sp.dma_start(xr[t][:, :, :], xn_pad(xn_d, i, t)).then_inc(xr_in[t], 16)
                    for it in range(IT):
                        n = it % NS
                        sp.wait_ge(g_sb, IT * T + it + 1)
                        sp.dma_start(gate_d[bass.ds(4 * T, 4), :, it * P:(it + 1) * P].rearrange("q p n -> p q n"),
                                     stage[n][:, :].rearrange("p (q n) -> p q n", q=4)).then_inc(st_out[n], 16)
            for n in range(NS):
                sp.wait_ge(st_out[n], 16 * FT * IT // NS)
            for t in range(2):
                sp.wait_ge(xq_out[t], 16 * FT // 2)
                sp.wait_ge(xr_in[t], 16 * (FT // 2 + 1))

        @block.scalar
        def _(act):
            with act.Fori(0, FT // 2) as i:
                for t in range(2):
                    T = 2 * i + t
                    for it in range(IT):
                        if it == 0 and t == 0:
                            parts(act, i, 0)
                        n = it % NS
                        act.wait_ge(g_ps, IT * T + it + 1)
                        act.wait_ge(st_out[n], (16 * IT // NS) * T + 16 * (it // NS))
                        act.wait_ge(g_pos, IT * 2 * i + max(IT * t + it - NS + 1, 0))
                        act.activation(stage[n][:, :], pG[it % 3][:, :], ACT.Copy, scale=S_X).then_inc(g_sb, 1)
                        if it == 5 and t == 0:
                            parts(act, i, 1)

        @block.vector
        def _(dve):
            def low(i, t):
                T = 2 * i + t
                dve.wait_ge(xh_done, T + 1)
                dve.tensor_tensor(xl[t][:, :, :], xq[t][:, :, :], xh[t][:, :, :].bitcast(F32), ALU.subtract).then_inc(xl_done, 1)

            with dve.Fori(0, FT // 2) as i:
                for t in range(2):
                    T = 2 * i + t
                    if t == 0:
                        low(i, 0)
                    for it in range(IT):
                        n = it % NS
                        dve.wait_ge(g_sb, IT * T + it + 1)
                        dve.tensor_reduce(gmx[:, 1, bass.ds(IT * T + it, 1)], stage[n][:, :], X, ALU.min).then_inc(g_neg, 1)
                        dve.tensor_reduce(gmx[:, 0, bass.ds(IT * T + it, 1)], stage[n][:, :], X, ALU.max).then_inc(g_pos, 1)
                        if it == 6 and t == 0:
                            low(i, 1)
            dve.wait_ge(g_pos, FT * IT)
            dve.wait_ge(g_neg, FT * IT)
            dve.tensor_reduce(GPOS, gmx[:, 0, :], X, ALU.max).then_inc(red, 1)
            dve.tensor_reduce(GNEG, gmx[:, 1, :], X, ALU.min, negate=True).then_inc(red, 1)
            dve.wait_ge(all_, 2)
            dve.tensor_tensor(AMAX, AP2, AN2, ALU.max).then_inc(scl, 1)
            dve.wait_ge(scl, 1)
            dve.tensor_scalar(S_G, AMAX, 1.0 / QMAX, TINY, ALU.mult, ALU.max).then_inc(scl, 1)
            dve.wait_ge(scl, 2)
            dve.reciprocal(INV_G, S_G).then_inc(scl, 1)
            dve.wait_ge(scl, 3)

        @block.gpsimd
        def _(pool):
            pool.wait_ge(red, 2)
            pool.partition_all_reduce(AP2, GPOS, P, RMAX).then_inc(all_, 1)
            pool.partition_all_reduce(AN2, GNEG, P, RMAX).then_inc(all_, 1)

        @block.tensor
        def _(pe):
            def transposes(i, t):
                T = 2 * i + t
                pe.wait_ge(xr_in[t], 16 * i + 16)
                for kt in range(KT):
                    pe.wait_ge(xq_done, KT * (T - 1) + kt + 1) if t else pe.wait_ge(xq_done, KT * T)
                    for q in range(4):
                        mm = pe.transpose(pX[kt][:, q * P:(q + 1) * P], xr[t][:, q, kt * P:(kt + 1) * P], ident[:, :])
                    mm.then_inc(xT_ps, 1)

            with pe.Fori(0, FT // 2) as i:
                transposes(i, 0)
                for t in range(2):
                    T = 2 * i + t
                    pe.wait_ge(xl_done, T + 1)
                    for it in range(IT):
                        if it % 3 == 0:
                            pe.wait_ge(w_in[it // 3], 32)
                        pe.wait_ge(g_sb, IT * 2 * i + max(IT * t + it - 2, 0))
                        product(pe, pG[it % 3], Wh, Wl, xh[t], xl[t], it).then_inc(g_ps, 1)
                        if it == 3 and t == 0:
                            transposes(i, 1)


def product(pe, ps, Wh, Wl, xh, xl, it):
    for kt in range(KT):
        for Ws, xs in ((Wh, xh), (Wh, xl), (Wl, xh)):
            mm = pe.matmul(ps[:, :], Ws[:, it, kt * P:(kt + 1) * P], xs[:, kt, :],
                           start=(kt == 0 and Ws is Wh and xs is xh), stop=(kt == KT - 1 and Ws is Wl))
    return mm


def up_phase(nc, sb, pb, sem, xq_d, gate_d, up_d, w_d, nq, umx, fmx, sci, scu, S_X, cols, tmp):
    S_G, INV_G, GMAX, S_F2, C_F, S_U, INV_U = cols
    T0, T1, T2, T3, T4 = tmp
    with ExitStack() as ph:
        Wh = sb(ph, "uWh", [P, IT, 512], F32R)
        Wl = sb(ph, "uWl", [P, IT, 512], F32R)
        xq = sb(ph, "uxq", [P, KT, 512], I16)
        xh = [sb(ph, f"uxh{n}", [P, KT, 512], F32R) for n in range(2)]
        xl = [sb(ph, f"uxl{n}", [P, KT, 512], F32R) for n in range(2)]
        NS = 3
        stage = [sb(ph, f"ust{n}", [P, 512], F32) for n in range(NS)]
        GW = I // 2
        NG = 4
        gb = [sb(ph, f"gb{n}", [P, GW], F32) for n in range(NG)]
        nb = [sb(ph, f"nb{n}", [P, GW], I16) for n in range(2)]
        mb = [sb(ph, f"mb{n}", [P, GW], U16) for n in range(2)]
        pU = [pb(ph, f"pU{n}") for n in range(4)]
        w_in = [sem(f"u_w_in{n}") for n in range(4)]
        xq_in = sem("u_xq_in")
        g_in = [sem(f"u_g_in{n}") for n in range(NG)]
        st_out = [sem(f"u_st_out{n}") for n in range(NS)]
        xh_done, xl_done, u_ps, u_sb, u_max = (sem(f"u_{n}") for n in ("xh_done", "xl_done", "ps", "sb", "max"))
        n_done, sig_done, m_done, f_done = (sem(f"u_{n}") for n in ("n_done", "sig_done", "m_done", "f_done"))
        kept, fmx_set, apart_p, apart_v = (sem(f"u_{n}") for n in ("kept", "fmx_set", "apart_p", "apart_v"))
        link_s, red, all_, pos_n, pos_sig, pos_m = (sem(f"u_{n}") for n in ("link", "red", "all", "pos_n", "pos_sig", "pos_m"))
        block = ph.enter_context(nc.Block())
        HT = FT // 2
        GROUPS = QT * I // GW
        GR = GROUPS // HT
        after = {it: [gr for gr in range(GR) if gr * IT // GR == it] for it in range(IT)}
        gate_g = gate_d.rearrange("q p (a k) -> q p a k", a=2)

        def sigmoid_int(pool, h, i, t, gr):
            g0 = GR * 2 * i + (GR * t + gr + GROUPS * h)
            pool.wait_ge(f_done, g0 - 1) if gr + t + h else pool.wait_ge(f_done, g0)
            pool.wait_ge(sig_done, g0 + 1)
            plain(pool)
            pool.tensor_scalar(mb[gr % 2][:, :], gb[gr % NG][:, :], SIG_ONE, 0.0, ALU.mult, ALU.add).then_inc(m_done, 1)

        def plain(pool):
            pool.sem_inc(apart_p, 1)

        def group(i, t, gr):
            return nq[:, bass.ds(GR * i + (GR // 2 * t + gr // 2), 1), (gr % 2) * GW:(gr % 2 + 1) * GW].rearrange("p a k -> p (a k)")

        @block.sync
        def _(sp):
            sp.dma_start(xq[:, :, :].rearrange("p k n -> p (k n)"), xq_d[0, :, :]).then_inc(xq_in, 16)
            for n in range(NG):
                sp.dma_start(gb[n][:, :], gate_g[n // 2, :, n % 2, :]).then_inc(g_in[n], 16)
            for c in range(4):
                for W, d in ((Wh, w_d[0]), (Wl, w_d[1])):
                    sp.dma_start(W[:, 3 * c:3 * c + 3, :].bitcast(F32),
                                 d.rearrange("p (i k) -> p i k", k=512)[:, 3 * c:3 * c + 3, :]).then_inc(w_in[c], 16)
            for h in range(2):
                with sp.Fori(0, HT // 2) as i:
                    for t in range(2):
                        T = 2 * i + (t + HT * h)
                        sp.wait_ge(xl_done, T + 1)
                        nxt = (2 * i + (t + 1 + HT * h)) % FT
                        sp.dma_start(xq[:, :, :].rearrange("p k n -> p (k n)"),
                                     xq_d[bass.ds(nxt, 1), :, :].rearrange("a p k -> (a p) k")).then_inc(xq_in, 16)
                        for it in range(IT):
                            n = it % NS
                            sp.wait_ge(u_sb, IT * T + it + 1)
                            sp.dma_start(up_d[bass.ds(4 * T, 4), :, it * P:(it + 1) * P].rearrange("q p n -> p q n"),
                                         stage[n][:, :].rearrange("p (q n) -> p q n", q=4)).then_inc(st_out[n], 16)
                            for gr in after[it] if h == 0 else ():
                                sp.wait_ge(f_done, GR * 2 * i + (GR * t + gr + 1))
                                nx = ((GR // 2) * 2 * i + (GR // 2 * t + (gr + NG) // 2)) % QT
                                sp.dma_start(gb[gr % NG][:, :], gate_g[bass.ds(nx, 1), :, gr % 2, :].rearrange("a p k -> (a p) k"))\
                                  .then_inc(g_in[gr % NG], 16)
            for n in range(NS):
                sp.wait_ge(st_out[n], 16 * FT * IT // NS)
            sp.wait_ge(xq_in, 16 * (FT + 1))
            for n in range(NG):
                sp.wait_ge(g_in[n], 16 * (GROUPS // NG + 1))

        @block.gpsimd
        def _(pool):
            for h in range(2):
                with pool.Fori(0, HT // 2) as i:
                    for t in range(2):
                        for gr in range(GR):
                            g0 = GR * 2 * i + (GR * t + gr)
                            n = gr % NG
                            if h == 0:
                                pool.wait_ge(kept, GR * 2 * i + (GR * t + gr - 1)) if gr + t else pool.wait_ge(kept, GR * 2 * i)
                                pool.wait_ge(g_in[n], (16 * GR // NG) * 2 * i + (16 * GR // NG * t + 16 * (gr // NG) + 16))
                                plain(pool)
                                pool.tensor_scalar(nb[gr % 2][:, :], gb[n][:, :], INV_G, 0.0, ALU.mult, ALU.add).then_inc(n_done, 1)
                            if gr >= 1:
                                sigmoid_int(pool, h, i, t, gr - 1)
                        sigmoid_int(pool, h, i, t, GR - 1)
                if h == 0:
                    pool.wait_ge(red, 1)
                    pool.partition_all_reduce(T1, T0, P, RMAX).then_inc(all_, 1)
            pool.wait_ge(red, 2)
            pool.partition_all_reduce(T1, T0, P, RMAX).then_inc(all_, 1)

        @block.scalar
        def _(act):
            act.wait_ge(pos_n, 1)
            act.activation(T3, sci[:, 0:1], ACT.Sigmoid, scale=S_G).then_inc(pos_sig, 1)
            act.wait_ge(xq_in, 16)
            act.activation(xh[0][:, :, :], xq[:, :, :], ACT.Copy).then_inc(xh_done, 1)
            for h in range(2):
                if h == 1:
                    for n in range(NG):
                        act.wait_ge(g_in[n], 16 * (GROUPS // NG + 1))
                with act.Fori(0, HT // 2) as i:
                    for t in range(2):
                        T = 2 * i + (t + HT * h)
                        for it in range(IT):
                            n = it % NS
                            act.wait_ge(u_ps, IT * T + it + 1)
                            act.wait_ge(st_out[n], (16 * IT // NS) * T + 16 * (it // NS))
                            act.wait_ge(u_max, IT * 2 * i + max(IT * (t + HT * h) + it - NS + 1, 0))
                            act.activation(stage[n][:, :], pU[it % 4][:, :], ACT.Copy, scale=S_X).then_inc(u_sb, 1)
                            for gr in after[it]:
                                g0 = GR * 2 * i + (GR * t + gr)
                                if h == 0:
                                    act.wait_ge(n_done, g0 + 1)
                                    src = nb[gr % 2][:, :]
                                else:
                                    act.wait_ge(m_done, g0 + GROUPS - NG + 1)
                                    src = group(i, t, gr)
                                act.activation(gb[gr % NG][:, :], src, ACT.Sigmoid, scale=S_G).then_inc(sig_done, 1)
                            if it == 4:
                                act.wait_ge(xq_in, 16 * T + 32)
                                act.activation(xh[(t + 1) % 2][:, :, :], xq[:, :, :], ACT.Copy).then_inc(xh_done, 1)

        @block.vector
        def _(dve):
            seq = [0]

            def link(ins):
                seq[0] += 1
                ins.then_inc(link_s, 1)
                dve.wait_ge(link_s, seq[0])

            dve.memset(fmx[:, 0:NG], 0.0).then_inc(fmx_set, 1)
            dve.wait_ge(fmx_set, 1)
            dve.tensor_scalar(sci[:, 0:1], GMAX, INV_G, None, ALU.mult).then_inc(pos_n, 1)
            dve.wait_ge(xh_done, 1)
            dve.tensor_tensor(xl[0][:, :, :], xq[:, :, :], xh[0][:, :, :].bitcast(F32), ALU.subtract).then_inc(xl_done, 1)
            dve.wait_ge(pos_sig, 1)
            dve.tensor_scalar(scu[:, 0:1], T3, SIG_ONE, None, ALU.mult).then_inc(pos_m, 1)
            for h in range(2):
                with dve.Fori(0, HT // 2) as i:
                    for t in range(2):
                        T = 2 * i + (t + HT * h)
                        for it in range(IT):
                            n = it % NS
                            dve.wait_ge(u_sb, IT * T + it + 1)
                            dve.tensor_reduce(umx[:, bass.ds(IT * T + it, 1)], stage[n][:, :], X, ALU.max,
                                              apply_absolute_value=True).then_inc(u_max, 1)
                            for gr in after[it]:
                                g0 = GR * 2 * i + (GR * t + gr)
                                dve.wait_ge(m_done, g0 + GROUPS * h + 1)
                                if h == 0:
                                    dve.wait_ge(kept, g0)
                                    dve.sem_inc(apart_v, 1)
                                    dve.tensor_tensor_reduce(out=gb[gr % NG][:, :], in0=nb[gr % 2][:, :], in1=mb[gr % 2][:, :],
                                                             scale=-1.0, scalar=fmx[:, gr % NG:gr % NG + 1], op0=ALU.mult, op1=ALU.max,
                                                             accum_out=fmx[:, gr % NG:gr % NG + 1]).then_inc(f_done, 1)
                                    dve.tensor_copy(group(i, t, gr), nb[gr % 2][:, :]).then_inc(kept, 1)
                                else:
                                    dve.scalar_tensor_tensor(out=group(i, t, gr), in0=group(i, t, gr), scalar=C_F, in1=mb[gr % 2][:, :],
                                                             op0=ALU.mult, op1=ALU.mult).then_inc(f_done, 1)
                            if it == 4:
                                dve.wait_ge(xh_done, T + 2)
                                dve.tensor_tensor(xl[(t + 1) % 2][:, :, :], xq[:, :, :], xh[(t + 1) % 2][:, :, :].bitcast(F32),
                                                  ALU.subtract).then_inc(xl_done, 1)
                if h == 0:
                    dve.wait_ge(f_done, GROUPS)
                    dve.tensor_reduce(T0, fmx[:, 0:NG], X, ALU.max).then_inc(red, 1)
                    dve.wait_ge(all_, 1)
                    dve.wait_ge(pos_m, 1)
                    link(dve.tensor_copy(T2, sci[:, 0:1]))
                    link(dve.tensor_copy(T3, scu[:, 0:1]))
                    link(dve.tensor_tensor(T4, T2, T3, ALU.mult))
                    link(dve.tensor_tensor(T2, T4, T1, ALU.max))
                    link(dve.tensor_scalar(T3, S_G, 1.0 / SIG_ONE, None, ALU.mult))
                    link(dve.tensor_tensor(T4, T2, T3, ALU.mult))
                    link(dve.tensor_scalar(S_F2, T4, 1.0 / QMAX, TINY, ALU.mult, ALU.max))
                    link(dve.reciprocal(T2, S_F2))
                    link(dve.tensor_tensor(C_F, T2, T3, ALU.mult))
            dve.wait_ge(u_max, FT * IT)
            dve.tensor_reduce(T0, umx[:, :], X, ALU.max).then_inc(red, 1)
            dve.wait_ge(all_, 2)
            link(dve.tensor_scalar(S_U, T1, 1.0 / QMAX, TINY, ALU.mult, ALU.max))
            link(dve.reciprocal(INV_U, S_U))

        @block.tensor
        def _(pe):
            for h in range(2):
                with pe.Fori(0, HT // 2) as i:
                    for t in range(2):
                        T = 2 * i + (t + HT * h)
                        pe.wait_ge(xl_done, T + 1)
                        for it in range(IT):
                            if it % 3 == 0:
                                pe.wait_ge(w_in[it // 3], 32)
                            pe.wait_ge(u_sb, IT * 2 * i + max(IT * (t + HT * h) + it - 3, 0))
                            product(pe, pU[it % 4], Wh, Wl, xh[t], xl[t], it).then_inc(u_ps, 1)


def down_phase(nc, sb, pb, sem, up_d, x1_d, of, w_d, nq, pmx, cols, tmp):
    S_F2, S_U, INV_U, S_O, C_O, C_OUT, TG_F = cols
    T0, T1, T2, T3 = tmp
    with ExitStack() as dn:
        Wh = sb(dn, "dWh", [P, IT, H], F32R)
        Wl = sb(dn, "dWl", [P, IT, H], F32R)
        w_in = sem("d_w_in")
        with ExitStack() as ph:
            NB_ = 4
            ub = [sb(ph, f"xub{n}", [P, I], F32) for n in range(NB_)]
            ui = [sb(ph, f"xui{n}", [P, I], I16) for n in range(2)]
            pp = sb(ph, "xpp", [P, I], F32)
            u_in = [sem(f"x_u_in{n}") for n in range(NB_)]
            ui_done, p_done, pmax_done, link_s, red, all_ = (sem(f"x_{n}") for n in ("ui", "p", "pmax", "link", "red", "all"))
            block = ph.enter_context(nc.Block())

            @block.sync
            def _(sp):
                with sp.Fori(0, QT // NB_) as i:
                    for n in range(NB_):
                        sp.wait_ge(ui_done, NB_ * i)
                        sp.dma_start(ub[n][:, :], up_d[bass.ds(NB_ * i + n, 1), :, :].rearrange("a p k -> (a p) k")).then_inc(u_in[n], 16)
                for W, d in ((Wh, w_d[0]), (Wl, w_d[1])):
                    sp.dma_start(W[:, :, :].bitcast(F32), d.rearrange("p (i k) -> p i k", k=H)).then_inc(w_in, 16)

            @block.scalar
            def _(act):
                with act.Fori(0, QT // NB_) as i:
                    for n in range(NB_):
                        act.wait_ge(u_in[n], 16 * i + 16)
                        act.wait_ge(p_done, NB_ * i + max(n - 1, 0))
                        act.activation(ui[n % 2][:, :], ub[n][:, :], ACT.Copy, scale=INV_U).then_inc(ui_done, 1)

            @block.vector
            def _(dve):
                seq = [0]

                def link(ins):
                    seq[0] += 1
                    ins.then_inc(link_s, 1)
                    dve.wait_ge(link_s, seq[0])

                with dve.Fori(0, QT // NB_) as i:
                    for n in range(NB_):
                        dve.wait_ge(ui_done, NB_ * i + n + 1)
                        dve.wait_ge(pmax_done, NB_ * i + n)
                        dve.tensor_tensor(pp[:, :], nq[:, bass.ds(NB_ * i + n, 1), :].rearrange("p a k -> p (a k)"), ui[n % 2][:, :],
                                          ALU.mult).then_inc(p_done, 1)
                        dve.wait_ge(p_done, NB_ * i + n + 1)
                        dve.tensor_reduce(pmx[:, bass.ds(NB_ * i + n, 1)], pp[:, :], X, ALU.max,
                                          apply_absolute_value=True).then_inc(pmax_done, 1)
                dve.wait_ge(pmax_done, QT)
                dve.tensor_reduce(T0, pmx[:, :], X, ALU.max).then_inc(red, 1)
                dve.wait_ge(all_, 1)
                link(dve.tensor_tensor(T2, S_F2, S_U, ALU.mult))
                link(dve.tensor_tensor(T3, T1, T2, ALU.mult))
                link(dve.tensor_scalar(S_O, T3, 1.0 / QMAX, TINY, ALU.mult, ALU.max))
                link(dve.reciprocal(T0, S_O))
                link(dve.tensor_tensor(C_O, T0, T2, ALU.mult))
                link(dve.tensor_tensor(C_OUT, S_O, TG_F, ALU.mult))

            @block.gpsimd
            def _(pool):
                pool.wait_ge(red, 1)
                pool.partition_all_reduce(T1, T0, P, RMAX).then_inc(all_, 1)

        with ExitStack() as ph:
            ub = [sb(ph, f"dub{n}", [P, I], F32) for n in range(2)]
            ui = sb(ph, "dui", [P, I], I16)
            oq = sb(ph, "doq", [P, I], I16)
            oh = [sb(ph, f"doh{n}", [P, I], F32R) for n in range(2)]
            ol = [sb(ph, f"dol{n}", [P, I], F32R) for n in range(2)]
            xr = [sb(ph, f"dxr{n}", [P, H], F32) for n in range(2)]
            yo = [sb(ph, f"dyo{n}", [P, H], F32) for n in range(2)]
            pD = [pb(ph, f"pD{n}") for n in range(2)]
            u_in = [sem(f"d_u_in{n}") for n in range(2)]
            x_in = [sem(f"d_x_in{n}") for n in range(2)]
            y_out = [sem(f"d_y_out{n}") for n in range(2)]
            ui_done, o_done, oh_done, ol_done, d_ps, y_done = (sem(f"d_{n}") for n in ("ui", "o", "oh", "ol", "ps", "y"))
            block = ph.enter_context(nc.Block())

            def output(act, i, n):
                act.wait_ge(y_done, 2 * i + n + 1)
                act.dma_start(of[bass.ds((2 * i + n) * P, P), :], yo[n][:, :]).then_inc(y_out[n], 16)

            @block.sync
            def _(sp):
                with sp.Fori(0, QT // 2) as i:
                    for n in range(2):
                        g = 2 * i + n
                        sp.wait_ge(ui_done, 2 * i)
                        sp.wait_ge(y_done, 2 * i)
                        sp.dma_start(ub[n][:, :], up_d[bass.ds(g, 1), :, :].rearrange("a p k -> (a p) k")).then_inc(u_in[n], 16)
                        sp.dma_start(xr[n][:, :], x1_d[bass.ds(g * P, P), :]).then_inc(x_in[n], 16)

            @block.scalar
            def _(act):
                with act.Fori(0, QT // 2) as i:
                    for n in range(2):
                        g = 2 * i + n
                        act.wait_ge(u_in[n], 16 * i + 16)
                        act.wait_ge(o_done, g)
                        act.activation(ui[:, :], ub[n][:, :], ACT.Copy, scale=INV_U).then_inc(ui_done, 1)
                        act.wait_ge(o_done, g + 1)
                        act.wait_ge(d_ps, 2 * i)
                        act.activation(oh[n][:, :], oq[:, :], ACT.Copy).then_inc(oh_done, 1)
                        if n:
                            output(act, i, 0)
                    output(act, i, 1)
                for n in range(2):
                    act.wait_ge(y_out[n], 16 * QT // 2)

            @block.vector
            def _(dve):
                def finish(i, n):
                    g = 2 * i + n
                    dve.wait_ge(d_ps, g + 1)
                    dve.wait_ge(x_in[n], 16 * i + 16)
                    dve.wait_ge(y_out[n], 16 * i)
                    dve.scalar_tensor_tensor(out=yo[n][:, :], in0=pD[n][:, :], scalar=C_OUT, in1=xr[n][:, :],
                                             op0=ALU.mult, op1=ALU.add).then_inc(y_done, 1)

                with dve.Fori(0, QT // 2) as i:
                    for n in range(2):
                        g = 2 * i + n
                        dve.wait_ge(ui_done, g + 1)
                        dve.wait_ge(ol_done, g)
                        dve.scalar_tensor_tensor(out=oq[:, :], in0=nq[:, bass.ds(g, 1), :].rearrange("p a k -> p (a k)"), scalar=C_O,
                                                 in1=ui[:, :], op0=ALU.mult, op1=ALU.mult).then_inc(o_done, 1)
                        dve.wait_ge(oh_done, g + 1)
                        dve.tensor_tensor(ol[n][:, :], oq[:, :], oh[n][:, :].bitcast(F32), ALU.subtract).then_inc(ol_done, 1)
                        if n:
                            finish(i, 0)
                    finish(i, 1)

            @block.tensor
            def _(pe):
                pe.wait_ge(w_in, 32)
                with pe.Fori(0, QT // 2) as i:
                    for n in range(2):
                        g = 2 * i + n
                        pe.wait_ge(ol_done, g + 1)
                        pe.wait_ge(y_done, 2 * i)
                        for it in range(IT):
                            cs = slice(it * P, (it + 1) * P)
                            for os_, Ws in ((oh[n], Wh), (oh[n], Wl), (ol[n], Wh)):
                                mm = pe.matmul(pD[n][:, :], os_[:, cs], Ws[:, it, :],
                                               start=(it == 0 and os_ is oh[n] and Ws is Wh),
                                               stop=(it == IT - 1 and os_ is ol[n]))
                        mm.then_inc(d_ps, 1)


_INS = ["x", "ctx_1024", "g_xattn", "g_ffn", "L0_xattn_w_q", "L0_xattn_w_k", "L0_xattn_w_v", "L0_xattn_w_o",
        "L0_ffn_w_gate", "L0_ffn_w_up", "L0_ffn_w_down"]


def kernel(**inputs):
    import numpy as _np
    import concourse.bacc as _bacc
    from concourse import mybir as _mybir
    from concourse.bass_utils import run_bass_kernel_spmd as _run

    nc = _bacc.Bacc("TRN2", target_bir_lowering=False, num_devices=1)
    arrays, args = {}, []
    for name in _INS:
        a = _np.ascontiguousarray(inputs[name])
        arrays[f"in_{name}"] = a
        args.append(nc.dram_tensor(f"in_{name}", a.shape, _mybir.dt.from_np(a.dtype), kind="ExternalInput").ap())
    out = nc.dram_tensor("out_0", (B, S, H), F32, kind="ExternalOutput").ap()
    flamingo_block(nc, *args, out)
    r = _run(nc, [arrays], core_ids=[0])
    return r.results[0]["out_0"]
```

```python
from contextlib import ExitStack

import concourse.bass as bass
from concourse import mybir

F32 = mybir.dt.float32
F32R = mybir.dt.float32r
I16 = mybir.dt.int16
U16 = mybir.dt.uint16
ALU = mybir.AluOpType
ACT = mybir.ActivationFunctionType
X = mybir.AxisListType.X
RMAX = bass.bass_isa.ReduceOp.max

P = 128
B, S, H = 4, 1024, 512
CK = 64
HEADS, HD = 16, 64
INNER = HEADS * HD
I = 1536
TOK = B * S
KT = H // P
PAIRS = HEADS // 2
IT = I // P
QT = TOK // P
BQ = S // P
FT = TOK // 512
BLK = 32
NBLK = 512 // BLK
LN_EPS = 1e-5
TINY = 1e-12
QMAX = 32767.0
SIG_ONE = 65536.0
SCALE = HD ** -0.5


LEAD = {}


def at(sem, base, n):
    assert n + LEAD[sem.name] >= 1, (sem.name, n)
    return sem, base + (n + LEAD[sem.name])


def head_starts(pool, sems):
    for s in sems:
        if LEAD[s.name]:
            pool.sem_inc(s, LEAD[s.name])


def flamingo_block(nc, x, ctx, g_xattn, g_ffn, w_q, w_k, w_v, w_o, w_gate, w_up, w_down, out):
    xf = x.rearrange("b s d -> (b s) d")
    cf = ctx.rearrange("b s d -> (b s) d")
    of = out.rearrange("b s d -> (b s) d")

    wsc = [[nc.dram_tensor(f"w{n}_{part}", (P, IT * 512), F32).ap() for part in ("hi", "lo")]
           for n in ("gate", "up", "down")]
    x1_d = nc.dram_tensor("x1_d", (TOK, H), F32).ap()
    xn_d = nc.dram_tensor("xn_d", (TOK, H), F32).ap()
    xq_d = nc.dram_tensor("xq_d", (FT, P, KT * 512), I16).ap()
    gate_d = nc.dram_tensor("gate_d", (QT, P, IT * P), F32).ap()
    up_d = nc.dram_tensor("up_d", (QT, P, IT * P), F32).ap()
    w_src = [w_gate.rearrange("(r c p) k -> r c p k", r=ROUNDS, p=P),
             w_up.rearrange("(r c p) k -> r c p k", r=ROUNDS, p=P),
             w_down.rearrange("(r p) (c k) -> r c p k", p=P, c=3)]

    with ExitStack() as top:
        phase_sems = []

        def sb(scope, name, shape, dt):
            return scope.enter_context(nc.sbuf_tensor(name, shape, dt))

        def pb(scope, name, n=512):
            return scope.enter_context(nc.psum_tensor(name, [P, n], F32))

        def sem(name, lead=0):
            s = nc.alloc_semaphore(name=name)
            LEAD[s.name] = lead
            phase_sems.append(s)
            return s

        def release_sems():
            nc.clear_and_free_semaphores(phase_sems)
            nc.all_engine_barrier()
            phase_sems.clear()

        mk = (nc, sb, pb, sem, phase_sems)
        ident = sb(top, "ident", [P, P], F32)
        mask = sb(top, "mask", [P, CK], F32)
        half = sb(top, "half", [P, 2], F32)
        sc = sb(top, "sc", [P, 32], F32)
        xmx = sb(top, "xmx", [P, QT], F32)
        gmx = sb(top, "gmx", [P, 2, FT * IT], F32)
        umx = sb(top, "umx", [P, FT * IT], F32)
        fmx = sb(top, "fmx", [P, 8], F32)
        pmx = sb(top, "pmx", [P, 16], F32)
        sci = sb(top, "sci", [P, 2], I16)
        scu = sb(top, "scu", [P, 2], U16)
        (TG_X, TG_F, RAW_X, RAW_F, S_X, INV_X, S_G, INV_G, S_U, INV_U, C_F, S_F2, S_O, C_O, C_OUT,
         T0, T1, T2, T3, T4, AMAX, GPOS, GNEG, AP2, AN2) = [sc[:, n:n + 1] for n in range(25)]

        with ExitStack() as att:
            wqT = sb(att, "wqT", [P, PAIRS, H], F32)
            wo = sb(att, "wo", [P, PAIRS, H], F32)
            kT = sb(att, "kT", [P, PAIRS, B * CK], F32)
            vT = sb(att, "vT", [P, PAIRS, B * CK], F32)
            prepare(mk, cf, w_q, w_k, w_v, w_o, g_xattn, g_ffn, w_src[0], wsc[0], ident, mask, half,
                    (TG_X, TG_F, RAW_X, RAW_F), wqT, wo, kT, vT)
            release_sems()
            attend(mk, xf, x1_d, xn_d, ident, mask, half, xmx, TG_X, (S_X, INV_X, T0, T1), wqT, wo, kT, vT)
            release_sems()
        gate_phase(mk, xn_d, xq_d, gate_d, wsc, w_src, ident, gmx, S_X, INV_X,
                   (GPOS, GNEG, AP2, AN2, AMAX, S_G, INV_G))
        with ExitStack() as ff:
            nq = sb(ff, "nq", [P, QT, I], I16)
            up_phase(mk, xq_d, gate_d, up_d, wsc[1], nq, umx, fmx, sci, scu, S_X,
                     (S_G, INV_G, AP2, S_F2, C_F, S_U, INV_U), (T0, T1, T2, T3, T4))
            down_phase(mk, up_d, x1_d, of, wsc[2], nq, pmx,
                       (S_F2, S_U, INV_U, S_O, C_O, C_OUT, TG_F), (T0, T1, T2, T3))



NJ = 3
ROUNDS = 4


class Jobs:

    def __init__(self, mk, ph, tag, R, banks):
        nc, sb, pb, sem, _ = mk
        self.R = R
        self.w = [sb(ph, f"{tag}w{n}", [P, 512], F32) for n in range(NJ)]
        self.q = [sb(ph, f"{tag}q{n}", [P, 512], I16) for n in range(NJ)]
        self.d = [sb(ph, f"{tag}d{n}", [P, 512], F32) for n in range(NJ)]
        self.hi = [sb(ph, f"{tag}hi{n}", [P, 512], F32R) for n in range(NJ)]
        self.lo = [sb(ph, f"{tag}lo{n}", [P, 512], F32R) for n in range(NJ)]
        self.mx = sb(ph, f"{tag}mx", [P, NJ, NBLK], F32)
        self.s = sb(ph, f"{tag}s", [P, NJ, NBLK], F32)
        self.inv = sb(ph, f"{tag}inv", [P, NJ, NBLK], F32)
        self.bank = [pb(ph, f"{tag}bank{n}") for n in range(banks)]
        self.loaded = [sem(f"{tag}_loaded{n}") for n in range(NJ)]
        self.stored = [sem(f"{tag}_stored{n}", 32) for n in range(NJ)]
        self.max_done, self.scale_done, self.inv_done, self.div_done, self.int_done, self.hi_done = (
            sem(f"{tag}_{n}") for n in ("max", "scale", "inv", "div", "int", "hi"))
        self.apart = sem(f"{tag}_apart")
        self.deq_done, self.turned, self.lo_done = sem(f"{tag}_deq", NJ), sem(f"{tag}_turned", NJ), sem(f"{tag}_lo", NJ)


def blocks(ap):
    return ap.rearrange("p (b k) -> p b k", k=BLK)


def spread(ap):
    return ap.unsqueeze(2).to_broadcast([P, NBLK, BLK])


def job_load(sp, J, i, q, src):
    sp.wait_ge(*at(J.deq_done, J.R * i, q - NJ + 1))
    sp.sem_inc(J.apart, 1)
    sp.dma_start(J.w[q % NJ][:, :], src).then_inc(J.loaded[q % NJ], 16)


def job_scale(dve, J, i, q):
    n = q % NJ
    dve.wait_ge(*at(J.loaded[n], 16 * (J.R // NJ) * i, 16 * (q // NJ + 1)))
    dve.tensor_reduce(J.mx[:, n, :], blocks(J.w[n][:, :]), X, ALU.max, apply_absolute_value=True).then_inc(J.max_done, 1)
    dve.wait_ge(*at(J.max_done, J.R * i, q + 1))
    dve.tensor_scalar(J.s[:, n, :], J.mx[:, n, :], 1.0 / 7.0, TINY, ALU.mult, ALU.max).then_inc(J.scale_done, 1)
    dve.wait_ge(*at(J.scale_done, J.R * i, q + 1))
    dve.reciprocal(J.inv[:, n, :], J.s[:, n, :]).then_inc(J.inv_done, 1)


def job_divide(pool, J, i, q):
    n = q % NJ
    pool.wait_ge(*at(J.inv_done, J.R * i, q + 1))
    pool.tensor_tensor(blocks(J.w[n][:, :]), blocks(J.w[n][:, :]), spread(J.inv[:, n, :]), ALU.mult).then_inc(J.div_done, 1)


def job_integer(dve, J, i, q):
    n = q % NJ
    dve.wait_ge(*at(J.div_done, J.R * i, q + 1))
    dve.tensor_scalar(J.q[n][:, :], J.w[n][:, :], 1.0, None, ALU.mult).then_inc(J.int_done, 1)
    dve.wait_ge(*at(J.int_done, J.R * i, q + 1))
    dve.wait_ge(*at(J.turned, J.R * i, q - NJ + 1))
    dve.tensor_tensor(blocks(J.d[n][:, :]), blocks(J.q[n][:, :]), spread(J.s[:, n, :]), ALU.mult).then_inc(J.deq_done, 1)


def job_turn(pe, J, i, q, ident):
    n, m = q % NJ, q % len(J.bank)
    pe.wait_ge(*at(J.lo_done, J.R * i, q - len(J.bank) + 1))
    pe.wait_ge(*at(J.deq_done, J.R * i, q + 1))
    for kt in range(4):
        mm = pe.transpose(J.bank[m][:, kt * P:(kt + 1) * P], J.d[n][:, kt * P:(kt + 1) * P], ident[:, :])
    mm.then_inc(J.turned, 1)


def job_hi(act, J, i, q):
    n, m = q % NJ, q % len(J.bank)
    act.wait_ge(*at(J.stored[n], 32 * (J.R // NJ) * i, 32 * (q // NJ)))
    act.wait_ge(*at(J.turned, J.R * i, q + 1))
    act.activation(J.hi[n][:, :], J.bank[m][:, :], ACT.Copy).then_inc(J.hi_done, 1)


def job_lo(dve, J, i, q):
    n, m = q % NJ, q % len(J.bank)
    dve.wait_ge(*at(J.stored[n], 32 * (J.R // NJ) * i, 32 * (q // NJ)))
    dve.wait_ge(*at(J.hi_done, J.R * i, q + 1))
    dve.tensor_tensor(J.lo[n][:, :], J.bank[m][:, :], J.hi[n][:, :].bitcast(F32), ALU.subtract).then_inc(J.lo_done, 1)


def job_store(sp, J, i, q, dsts):
    n = q % NJ
    sp.wait_ge(*at(J.lo_done, J.R * i, q + 1))
    for part, dst in zip((J.hi[n], J.lo[n]), dsts):
        src = part[:, :].bitcast(F32)
        if len(dst.shape) == 3:
            src = src.rearrange("p (i h) -> p i h", h=P)
        sp.dma_start(dst, src).then_inc(J.stored[n], 16)


def by_input(w, r, c):
    return [d[:, bass.ds(r * (3 * 512) + c * 512, 512)] for d in w]


def prepare(mk, cf, w_q, w_k, w_v, w_o, g_xattn, g_ffn, w_src, w_dst, ident, mask, half, cols, wqT, wo, kT, vT):
    nc, sb, pb, sem, sems = mk
    TG_X, TG_F, RAW_X, RAW_F = cols
    with ExitStack() as ph:
        wq = sb(ph, "wq", [P, KT, INNER], F32)
        wk = sb(ph, "wk", [P, KT, INNER], F32)
        wv = sb(ph, "wv", [P, KT, INNER], F32)
        cx = sb(ph, "cx", [P, 2, H], F32)
        cT = sb(ph, "cT", [P, KT, B * CK], F32)
        JR = 3
        NJOBS = JR * ROUNDS
        J = Jobs(mk, ph, "pj", JR, 3)
        pw = [pb(ph, f"pw{n}") for n in range(2)]
        pk = pb(ph, "pk")
        pv = pb(ph, "pv")
        ctx_in, wo_in, g_in = (sem(n) for n in ("ctx_in", "wo_in", "g_in"))
        wq_in, wk_in, wv_in = ([sem(f"{n}_in{r}") for r in range(2)] for n in ("wq", "wk", "wv"))
        const_set, id_set, ctxT_ps, ctxT_sb, wqT_ps, wqT_sb, k_ps, k_sb, v_ps, v_sb, tanh_done = (sem(n) for n in
            ("const_set", "id_set", "ctxT_ps", "ctxT_sb", "wqT_ps", "wqT_sb", "k_ps", "k_sb", "v_ps", "v_sb", "tanh_done"))
        block = ph.enter_context(nc.Block())
        HC = INNER // 2

        @block.sync
        def _(sp):
            sp.dma_start(cx[:, :, :], cf.rearrange("(t p) d -> p t d", p=P)).then_inc(ctx_in, 16)
            sp.dma_start(wq[:, :, 0:HC], w_q.rearrange("(t p) n -> p t n", p=P)[:, :, 0:HC]).then_inc(wq_in[0], 16)
            for q in range(NJ):
                job_load(sp, J, 0, q, w_src[0, q, :, :])
            for r in range(2):
                for w, d, s in ((wk, w_k, wk_in), (wv, w_v, wv_in), (wq, w_q, wq_in)):
                    if w is not wq or r == 0:
                        rr = 1 if w is wq else r
                        sp.dma_start(w[:, :, rr * HC:(rr + 1) * HC],
                                     d.rearrange("(t p) n -> p t n", p=P)[:, :, rr * HC:(rr + 1) * HC]).then_inc(s[rr], 16)
            sp.dma_start(wo[:, :, :], w_o.rearrange("(t p) n -> p t n", p=P)).then_inc(wo_in, 16)
            with sp.Fori(0, ROUNDS - 1) as r:
                for q in range(JR):
                    job_load(sp, J, r, q + NJ, w_src[bass.ds(r + 1, 1), q, :, :].rearrange("a p k -> (a p) k"))
                    job_store(sp, J, r, q, by_input(w_dst, r, q))
            for q in range(JR):
                job_store(sp, J, ROUNDS - 1, q, by_input(w_dst, ROUNDS - 1, q))
            for n in range(NJ):
                sp.wait_ge(*at(J.stored[n], 0, 32 * NJOBS // NJ))
            sp.wait_ge(wo_in, 16)

        @block.gpsimd
        def _(pool):
            head_starts(pool, sems)
            pool.memset(ident[:, :], 0.0).then_inc(const_set, 1)
            pool.memset(mask[:, :], 0.0).then_inc(const_set, 1)
            pool.memset(half[:, 0:1], -0.5).then_inc(const_set, 1)
            pool.memset(half[:, 1:2], LN_EPS).then_inc(const_set, 1)
            pool.wait_ge(const_set, 4)
            pool.affine_select(out=ident[:, :], in_=ident[:, :], compare_op=ALU.not_equal, fill=1.0,
                               base=0, pattern=[[-1, P]], channel_multiplier=1).then_inc(id_set, 1)
            pool.affine_select(out=mask[:, :], in_=mask[:, :], compare_op=ALU.is_ge, fill=-10000.0,
                               base=0, pattern=[[-1, CK]], channel_multiplier=1).then_inc(id_set, 1)
            with pool.Fori(0, ROUNDS) as r:
                for q in range(JR):
                    job_divide(pool, J, r, q)

        @block.scalar
        def _(act):
            act.dma_start(RAW_X, g_xattn.unsqueeze(0).to_broadcast([P, 1])).then_inc(g_in, 16)
            act.dma_start(RAW_F, g_ffn.unsqueeze(0).to_broadcast([P, 1])).then_inc(g_in, 16)
            for kt in range(2):
                act.wait_ge(ctxT_ps, kt + 1)
                act.activation(cT[:, 2 * kt:2 * kt + 2, :].rearrange("p a b -> p (a b)"), pw[kt][:, :],
                               ACT.Copy).then_inc(ctxT_sb, 1)
            act.wait_ge(g_in, 32)
            act.activation(TG_X, RAW_X, ACT.Tanh).then_inc(tanh_done, 1)
            act.activation(TG_F, RAW_F, ACT.Tanh).then_inc(tanh_done, 1)
            with act.Fori(0, ROUNDS) as r:
                for a in range(2):
                    act.wait_ge(wqT_ps, 2 * r + a + 1)
                    act.activation(wqT[:, bass.ds(2 * r + a, 1), :].rearrange("p a b -> p (a b)"), pw[a][:, :],
                                   ACT.Copy).then_inc(wqT_sb, 1)
                job_hi(act, J, r, 0)
                act.wait_ge(k_ps, r + 1)
                act.activation(kT[:, bass.ds(2 * r, 2), :].rearrange("p a b -> p (a b)"), pk[:, :],
                               ACT.Copy).then_inc(k_sb, 1)
                job_hi(act, J, r, 1)
                act.wait_ge(v_ps, r + 1)
                act.activation(vT[:, bass.ds(2 * r, 2), :].rearrange("p a b -> p (a b)"), pv[:, :],
                               ACT.Copy).then_inc(v_sb, 1)
                job_hi(act, J, r, 2)

        @block.vector
        def _(dve):
            def run(r, k, last=False):
                if not last:
                    job_scale(dve, J, r, k)
                if k >= 1 and not (last and k > JR):
                    job_integer(dve, J, r, k - 1)
                if k >= 2:
                    job_lo(dve, J, r, k - 2)

            run(0, 0)
            run(0, 1)
            with dve.Fori(0, ROUNDS - 1) as r:
                for k in range(2, 2 + JR):
                    run(r, k)
            run(ROUNDS - 1, 2)
            run(ROUNDS - 1, 3, last=True)
            run(ROUNDS - 1, 4, last=True)

        @block.tensor
        def _(pe):
            pe.wait_ge(id_set, 1)
            pe.wait_ge(ctx_in, 16)
            for kt in range(KT):
                for t in range(2):
                    mm = pe.transpose(pw[kt // 2][:, (kt % 2) * 256 + t * P:(kt % 2) * 256 + (t + 1) * P],
                                      cx[:, t, kt * P:(kt + 1) * P], ident[:, :])
                if kt % 2:
                    mm.then_inc(ctxT_ps, 1)
            pe.wait_ge(ctxT_sb, 2)
            for r in range(ROUNDS):
                pe.wait_ge(wq_in[r // 2], 16)
                if r:
                    pe.wait_ge(wqT_sb, 2 * r)
                for a in range(2):
                    for kt in range(KT):
                        mm = pe.transpose(pw[a][:, kt * P:(kt + 1) * P],
                                          wq[:, kt, (2 * r + a) * P:(2 * r + a + 1) * P], ident[:, :])
                    mm.then_inc(wqT_ps, 1)
                job_turn(pe, J, r, 0, ident)
                for n, (w, ps, s_in, s_ps, s_sb) in enumerate(((wk, pk, wk_in, k_ps, k_sb), (wv, pv, wv_in, v_ps, v_sb))):
                    pe.wait_ge(s_in[r // 2], 16)
                    if r:
                        pe.wait_ge(s_sb, r)
                    for a in range(2):
                        for kt in range(KT):
                            mm = pe.matmul(ps[:, a * 256:(a + 1) * 256], w[:, kt, (2 * r + a) * P:(2 * r + a + 1) * P],
                                           cT[:, kt, :], start=(kt == 0), stop=(kt == KT - 1))
                    mm.then_inc(s_ps, 1)
                    job_turn(pe, J, r, n + 1, ident)


def attend(mk, xf, x1_d, xn_d, ident, mask, half, xmx, TG_X, cols, wqT, wo, kT, vT):
    nc, sb, pb, sem, sems = mk
    S_X, INV_X, T0, T1 = cols
    with ExitStack() as ph:
        kbd = sb(ph, "kbd", [P, PAIRS, P], F32)
        vbd = sb(ph, "vbd", [P, PAIRS, P], F32)
        Ah = sb(ph, "Ah", [P, KT, INNER], F32R)
        Al = sb(ph, "Al", [P, KT, INNER], F32R)
        Vh = sb(ph, "Vh", [P, PAIRS, H], F32R)
        Vl = sb(ph, "Vl", [P, PAIRS, H], F32R)
        xin = [sb(ph, f"xin{n}", [P, H], F32) for n in range(BQ)]
        xn = [sb(ph, f"xn{n}", [P, H], F32) for n in range(2)]
        xh = [sb(ph, f"xh{n}", [P, H], F32R) for n in range(2)]
        xl = [sb(ph, f"xl{n}", [P, H], F32R) for n in range(2)]
        pr = [sb(ph, f"pr{n}", [P, INNER], F32) for n in range(2)]
        pTh = sb(ph, "pTh", [P, INNER], F32R)
        pTl = sb(ph, "pTl", [P, INNER], F32R)
        x1 = [sb(ph, f"x1{n}", [P, H], F32) for n in range(2)]
        x2 = [sb(ph, f"x2{n}", [P, H], F32) for n in range(2)]
        st = sb(ph, "st", [P, 2, 6], F32)
        mv = sb(ph, "mv", [P, 2, 2], F32)
        rs = sb(ph, "rs", [P, 2, 2], F32)
        st2 = sb(ph, "st2", [P, 2, 6], F32)
        mv2 = sb(ph, "mv2", [P, 2, 2], F32)
        rs2 = sb(ph, "rs2", [P, 2, 2], F32)
        smx = sb(ph, "smx", [P, 2, HEADS], F32)
        ssum = sb(ph, "ssum", [P, 2, HEADS], F32)
        srec = sb(ph, "srec", [P, 2, HEADS], F32)
        pS = [pb(ph, f"pS{n}", 1024) for n in range(2)]
        pT = pb(ph, "pT", 1024)
        pX = pb(ph, "pX")
        pO = pb(ph, "pO")

        (stats_done, mean_done, eps_done, rstd_done, xn_done, xT_ps, xh_done, xl_done,
         s_ps, max_done, sub_done, exp_done, sum_done, rec_done, prob_done, pT_ps, pTh_done, pTl_done,
         o_ps, x1_done, stats2_done, mean2_done, eps2_done, rstd2_done, x2_done, x2max_done) = (sem(n, 8) for n in
            """stats mean eps rstd xn xT_ps xh xl s_ps max sub exp sum rec prob pT_ps pTh pTl
               o_ps x1 stats2 mean2 eps2 rstd2 x2 x2max""".split())
        masked, kbd_set, vbd_set, bd_zero, apart, sx_red, sx_all, sx_scale = (sem(n) for n in
            ("masked", "kbd_set", "vbd_set", "bd_zero", "apart", "sx_red", "sx_all", "sx_scale"))
        ch_ps, ch_hi, ch_lo = sem("ch_ps"), sem("ch_hi"), sem("ch_lo", 2)
        x_in = [sem(f"x_in{n}") for n in range(BQ)]
        x1_out = [sem(f"x1_out{n}", 16) for n in range(2)]
        x2_out = [sem(f"x2_out{n}", 16) for n in range(2)]
        block = ph.enter_context(nc.Block())
        NCH = 16

        def schedule(eng, step):
            for k in range(-2, 3):
                step(0, k, lambda j: j >= 0)
            with eng.Fori(0, B - 1) as b:
                for k in range(3, BQ + 3):
                    step(b, k, lambda j: True)
            for k in range(3, BQ + 3):
                step(B - 1, k, lambda j: j < BQ)

        def matrices(k, have):
            if k in (0, 1):
                return k, 0
            if k in (BQ, BQ + 1) and have(k):
                return k - BQ, 1
            return None, 0

        def tile(s, b, j):
            return at(s, BQ * b, j + 1)

        @block.sync
        def _(sp):
            for j in range(BQ):
                sp.dma_start(xin[j][:, :], xf[j * P:(j + 1) * P, :]).then_inc(x_in[j], 16)

            def step(b, k, have):
                j = k - 3
                if have(j):
                    n = j % 2
                    sp.wait_ge(*tile(x1_done, b, j))
                    sp.dma_start(x1_d[bass.ds(S * b + j * P, P), :], x1[n][:, :]).then_inc(x1_out[n], 16)
                    if have(j + BQ):
                        sp.dma_start(xin[j % BQ][:, :], xf[bass.ds(S * b + (j + BQ) * P, P), :]).then_inc(x_in[j % BQ], 16)
                    sp.wait_ge(*tile(x2_done, b, j))
                    sp.dma_start(xn_d[bass.ds(S * b + j * P, P), :], x2[n][:, :]).then_inc(x2_out[n], 16)

            schedule(sp, step)
            for n in range(2):
                sp.wait_ge(*at(x1_out[n], 0, 16 * QT // 2))
                sp.wait_ge(*at(x2_out[n], 0, 16 * QT // 2))

        @block.gpsimd
        def _(pool):
            head_starts(pool, sems)
            pool.memset(kbd[:, :, :], 0.0).then_inc(bd_zero, 1)
            pool.memset(vbd[:, :, :], 0.0).then_inc(bd_zero, 1)

            def rstd(b, j, mv_, rs_, mean_s, eps_s, rstd_s, used):
                pool.wait_ge(*tile(mean_s, b, j))
                pool.wait_ge(*tile(used, b, j - 2))
                pool.tensor_tensor(rs_[:, j % 2, 0:1], mv_[:, j % 2, 1:2], half[:, 1:2], ALU.add).then_inc(eps_s, 1)
                pool.wait_ge(*tile(eps_s, b, j))
                pool.tensor_tensor(rs_[:, j % 2, 1:2], rs_[:, j % 2, 0:1], half[:, 0:1], ALU.pow).then_inc(rstd_s, 1)

            def step(b, k, have):
                if have(k + 2):
                    rstd(b, k + 2, mv, rs, mean_done, eps_done, rstd_done, xn_done)
                if have(k - 3):
                    rstd(b, k - 3, mv2, rs2, mean2_done, eps2_done, rstd2_done, x2_done)
                if have(k - 1):
                    j = k - 1
                    pool.wait_ge(*tile(rec_done, b, j))
                    p3 = pr[j % 2][:, :].rearrange("p (h c) -> p h c", c=CK)
                    pool.tensor_tensor(p3, p3, srec[:, j % 2, :].unsqueeze(2).to_broadcast([P, HEADS, CK]),
                                       ALU.mult).then_inc(prob_done, 1)

            schedule(pool, step)
            pool.wait_ge(sx_red, 1)
            pool.partition_all_reduce(T1, T0, P, RMAX).then_inc(sx_all, 1)

        @block.scalar
        def _(act):
            def diagonal(b, ahead):
                for bd, t, s in ((kbd, kT, kbd_set), (vbd, vT, vbd_set)):
                    for a in range(2):
                        rows = slice(a * 64, a * 64 + 64)
                        act.activation(bd[rows, :, a * 64:a * 64 + 64], t[rows, :, bass.ds(CK * b + CK * ahead, CK)],
                                       ACT.Copy).then_inc(s, 1)

            def step(b, k, have):
                which, ahead = matrices(k, have)
                if k == 5 and have(BQ):
                    diagonal(b, 1)
                if have(k - 2):
                    j = k - 2
                    act.wait_ge(*tile(o_ps, b, j - 1))
                    act.wait_ge(*tile(pT_ps, b, j))
                    act.activation(pTh[:, :], pT[:, :], ACT.Copy).then_inc(pTh_done, 1)
                if have(k - 1):
                    j = k - 1
                    act.wait_ge(*tile(sub_done, b, j))
                    act.activation(pr[j % 2][:, :], pr[j % 2][:, :], ACT.Exp).then_inc(exp_done, 1)

                def high():
                    if have(k + 1):
                        j = k + 1
                        act.wait_ge(*tile(xT_ps, b, j))
                        act.wait_ge(*tile(s_ps, b, j - 2))
                        act.activation(xh[j % 2][:, :], pX[:, :], ACT.Copy).then_inc(xh_done, 1)

                if which != 0:
                    high()
                for n in range(8) if which is not None else ():
                    act.wait_ge(*at(ch_ps, NCH * b, NCH * ahead + 8 * which + n + 1))
                    if which == 0:
                        act.activation(Ah[:, n // 2, (n % 2) * 512:(n % 2 + 1) * 512], pT[:, (n % 2) * 512:(n % 2 + 1) * 512],
                                       ACT.Copy, scale=SCALE).then_inc(ch_hi, 1)
                    else:
                        act.activation(Vh[:, n, :], pT[:, (n % 2) * 512:(n % 2 + 1) * 512], ACT.Copy).then_inc(ch_hi, 1)
                if which == 0:
                    high()

            act.wait_ge(bd_zero, 2)
            diagonal(0, 0)
            schedule(act, step)

        @block.vector
        def _(dve):
            def chunk_low(b, ahead, which, n):
                dve.wait_ge(*at(ch_hi, NCH * b, NCH * ahead + 8 * which + n + 1))
                bank = pT[:, (n % 2) * 512:(n % 2 + 1) * 512]
                if which == 0:
                    cs = slice((n % 2) * 512, (n % 2 + 1) * 512)
                    dve.scalar_tensor_tensor(out=Al[:, n // 2, cs], in0=bank, scalar=SCALE, in1=Ah[:, n // 2, cs].bitcast(F32),
                                             op0=ALU.mult, op1=ALU.subtract).then_inc(ch_lo, 1)
                else:
                    dve.tensor_tensor(Vl[:, n, :], bank, Vh[:, n, :].bitcast(F32), ALU.subtract).then_inc(ch_lo, 1)

            def scores_down(b, j):
                n = j % 2
                s3 = pS[n][:, :].rearrange("p (h c) -> p h c", c=CK)
                p3 = pr[n][:, :].rearrange("p (h c) -> p h c", c=CK)
                dve.wait_ge(*tile(s_ps, b, j))
                dve.wait_ge(*tile(pT_ps, b, j - 2))
                src = s3
                if j % BQ == 0:
                    dve.tensor_tensor(p3, s3, mask[:, :].unsqueeze(1).to_broadcast([P, HEADS, CK]), ALU.add).then_inc(masked, 1)
                    dve.wait_ge(masked, b + (j // BQ + 1))
                    src = p3
                dve.tensor_reduce(smx[:, n, :], src, X, ALU.max).then_inc(max_done, 1)
                dve.wait_ge(*tile(max_done, b, j))
                dve.tensor_tensor(p3, src, smx[:, n, :].unsqueeze(2).to_broadcast([P, HEADS, CK]), ALU.subtract).then_inc(sub_done, 1)

            def statistics(b, j):
                n = j % 2
                dve.wait_ge(*at(x_in[j % BQ], 16 * b, 16 * (j // BQ + 1)))
                dve.wait_ge(*tile(mean_done, b, j - 2))
                dve.bn_stats(st[:, n, :], xin[j % BQ][:, :]).then_inc(stats_done, 1)
                dve.wait_ge(*tile(stats_done, b, j))
                dve.wait_ge(*tile(xn_done, b, j - 2))
                dve.sem_inc(apart, 1)
                dve.bn_aggr(mv[:, n, :], st[:, n, :]).then_inc(mean_done, 1)

            def residual(b, j):
                n = j % 2
                dve.wait_ge(*tile(o_ps, b, j))
                dve.wait_ge(*at(x1_out[n], 8 * BQ * b, 16 * (j // 2)))
                dve.wait_ge(*tile(x2_done, b, j - 2))
                dve.scalar_tensor_tensor(out=x1[n][:, :], in0=pO[:, :], scalar=TG_X, in1=xin[j % BQ][:, :],
                                         op0=ALU.mult, op1=ALU.add).then_inc(x1_done, 1)
                dve.wait_ge(*tile(x1_done, b, j))
                dve.bn_stats(st2[:, n, :], x1[n][:, :]).then_inc(stats2_done, 1)
                dve.wait_ge(*tile(stats2_done, b, j))
                dve.sem_inc(apart, 1)
                dve.bn_aggr(mv2[:, n, :], st2[:, n, :]).then_inc(mean2_done, 1)

            def sums(b, j):
                n = j % 2
                dve.wait_ge(*tile(exp_done, b, j))
                dve.tensor_reduce(ssum[:, n, :], pr[n][:, :].rearrange("p (h c) -> p h c", c=CK), X, ALU.add).then_inc(sum_done, 1)
                dve.wait_ge(*tile(sum_done, b, j))
                dve.wait_ge(*tile(prob_done, b, j - 2))
                dve.reciprocal(srec[:, n, :], ssum[:, n, :]).then_inc(rec_done, 1)

            def normal(b, j):
                dve.wait_ge(*tile(rstd_done, b, j))
                dve.wait_ge(*tile(xT_ps, b, j - 2))
                dve.tensor_scalar(xn[j % 2][:, :], xin[j % BQ][:, :], mv[:, j % 2, 0:1], rs[:, j % 2, 1:2],
                                  ALU.subtract, ALU.mult).then_inc(xn_done, 1)

            def normal2(b, j):
                n = j % 2
                dve.wait_ge(*tile(rstd2_done, b, j))
                dve.wait_ge(*at(x2_out[n], 8 * BQ * b, 16 * (j // 2)))
                dve.wait_ge(*tile(x2max_done, b, j - 2))
                dve.tensor_scalar(x2[n][:, :], x1[n][:, :], mv2[:, n, 0:1], rs2[:, n, 1:2],
                                  ALU.subtract, ALU.mult).then_inc(x2_done, 1)
                dve.wait_ge(*tile(x2_done, b, j))
                dve.tensor_reduce(xmx[:, bass.ds(BQ * b + j, 1)], x2[n][:, :], X, ALU.max,
                                  apply_absolute_value=True).then_inc(x2max_done, 1)

            def step(b, k, have):
                which, ahead = matrices(k, have)
                chunks = [lambda n=n: chunk_low(b, ahead, which, n) for n in range(8)] if which is not None else []

                def some(n):
                    for _ in range(min(n, len(chunks))):
                        chunks.pop(0)()

                if have(k - 2):
                    j = k - 2
                    dve.wait_ge(*tile(pTh_done, b, j))
                    dve.tensor_tensor(pTl[:, :], pT[:, :], pTh[:, :].bitcast(F32), ALU.subtract).then_inc(pTl_done, 1)
                if have(k - 1):
                    scores_down(b, k - 1)
                if have(k - 3):
                    residual(b, k - 3)
                if which == 0:
                    some(2)
                if have(k + 2):
                    statistics(b, k + 2)
                if which == 0:
                    some(2)
                if have(k - 1):
                    sums(b, k - 1)
                if which == 0:
                    some(2)
                if have(k + 2):
                    normal(b, k + 2)
                if have(k - 3):
                    normal2(b, k - 3)
                if which == 0:
                    some(8)
                if have(k + 1):
                    j = k + 1
                    dve.wait_ge(*tile(xh_done, b, j))
                    dve.wait_ge(*tile(s_ps, b, j - 2))
                    dve.tensor_tensor(xl[j % 2][:, :], pX[:, :], xh[j % 2][:, :].bitcast(F32), ALU.subtract).then_inc(xl_done, 1)
                some(8)

            schedule(dve, step)
            dve.wait_ge(*at(x2max_done, 0, QT))
            dve.tensor_reduce(T0, xmx[:, :], X, ALU.max).then_inc(sx_red, 1)
            dve.wait_ge(sx_all, 1)
            dve.tensor_scalar(S_X, T1, 1.0 / QMAX, TINY, ALU.mult, ALU.max).then_inc(sx_scale, 1)
            dve.wait_ge(sx_scale, 1)
            dve.reciprocal(INV_X, S_X).then_inc(sx_scale, 1)
            dve.wait_ge(sx_scale, 2)

        @block.tensor
        def _(pe):
            def chunk(b, ahead, which, n):
                pe.wait_ge(*at(ch_lo, NCH * b, NCH * ahead + 8 * which + n - 1))
                bank = pT[:, (n % 2) * 512:(n % 2 + 1) * 512]
                if which == 0:
                    if n == 0:
                        pe.wait_ge(*at(kbd_set, 2 * b, 2 * ahead + 2))
                    for q in range(4):
                        pair = (n % 2) * 4 + q
                        mm = pe.matmul(bank[:, q * P:(q + 1) * P], wqT[:, pair, (n // 2) * P:(n // 2 + 1) * P],
                                       kbd[:, pair, :], start=True, stop=True)
                else:
                    if n == 0:
                        pe.wait_ge(*at(vbd_set, 2 * b, 2 * ahead + 2))
                    mm = pe.matmul(bank, vbd[:, n, :], wo[:, n, :], start=True, stop=True)
                mm.then_inc(ch_ps, 1)

            def values(b, k, have):
                which, ahead = matrices(k, have)
                j = k - 2
                if have(j):
                    pe.wait_ge(*tile(pTl_done, b, j))
                    pe.wait_ge(*tile(x1_done, b, j - 1))
                for p in range(PAIRS):
                    cs = slice(p * P, (p + 1) * P)
                    if have(j):
                        for ps_, vs in ((pTh, Vh), (pTh, Vl), (pTl, Vh)):
                            mm = pe.matmul(pO[:, :], ps_[:, cs], vs[:, p, :],
                                           start=(p == 0 and ps_ is pTh and vs is Vh),
                                           stop=(p == PAIRS - 1 and ps_ is pTl))
                        if p == PAIRS - 1:
                            mm.then_inc(o_ps, 1)
                    if which is not None:
                        chunk(b, ahead, which, p)

            def scores(b, k):
                pe.wait_ge(*tile(xl_done, b, k))
                pe.wait_ge(*tile(sub_done, b, k - 2))
                if k % BQ == 0:
                    pe.wait_ge(*at(ch_lo, NCH * b, NCH * (k // BQ) + 8))
                for kt in range(KT):
                    cs = slice(kt * P, (kt + 1) * P)
                    for xs, As in ((xh, Ah), (xh, Al), (xl, Ah)):
                        for hf in range(2):
                            mm = pe.matmul(pS[k % 2][:, hf * 512:(hf + 1) * 512], xs[k % 2][:, cs],
                                           As[:, kt, hf * 512:(hf + 1) * 512],
                                           start=(kt == 0 and xs is xh and As is Ah),
                                           stop=(kt == KT - 1 and xs is xl))
                mm.then_inc(s_ps, 1)

            def step(b, k, have):
                which, ahead = matrices(k, have)
                if have(k - 2):
                    j = k - 2
                    pe.wait_ge(*tile(prob_done, b, j))
                    pe.wait_ge(*tile(pTl_done, b, j - 1))
                    if k % BQ == 2:
                        pe.wait_ge(*at(ch_lo, NCH * b, NCH * (k // BQ) + NCH))
                    for p in range(PAIRS):
                        mm = pe.transpose(pT[:, p * P:(p + 1) * P], pr[j % 2][:, p * P:(p + 1) * P], ident[:, :])
                    mm.then_inc(pT_ps, 1)
                if which == 0:
                    values(b, k, have)
                elif have(k) and k >= 0:
                    scores(b, k)
                if have(k + 1):
                    j = k + 1
                    pe.wait_ge(*tile(xn_done, b, j))
                    pe.wait_ge(*tile(xl_done, b, j - 1))
                    for kt in range(KT):
                        mm = pe.transpose(pX[:, kt * P:(kt + 1) * P], xn[j % 2][:, kt * P:(kt + 1) * P], ident[:, :])
                    mm.then_inc(xT_ps, 1)
                if which == 0:
                    scores(b, k)
                else:
                    values(b, k, have)

            schedule(pe, step)


def gate_phase(mk, xn_d, xq_d, gate_d, wsc, w_src, ident, gmx, S_X, INV_X, cols):
    nc, sb, pb, sem, sems = mk
    GPOS, GNEG, AP2, AN2, AMAX, S_G, INV_G = cols
    with ExitStack() as ph:
        Wh = sb(ph, "gWh", [P, IT, 512], F32R)
        Wl = sb(ph, "gWl", [P, IT, 512], F32R)
        xr = [sb(ph, f"xr{n}", [P, 4, H], F32) for n in range(2)]
        xq = [sb(ph, f"gxq{n}", [P, KT, 512], I16) for n in range(2)]
        xh = [sb(ph, f"gxh{n}", [P, KT, 512], F32R) for n in range(2)]
        xl = [sb(ph, f"gxl{n}", [P, KT, 512], F32R) for n in range(2)]
        NS = 4
        stage = [sb(ph, f"gst{n}", [P, 512], F32) for n in range(NS)]
        JR = 6
        J = Jobs(mk, ph, "gj", JR, 1)
        pX = [pb(ph, f"gpX{n}") for n in range(4)]
        pG = [pb(ph, f"gpG{n}") for n in range(3)]
        w_in = [sem(f"g_w_in{n}") for n in range(4)]
        xr_in = [sem(f"g_xr_in{n}") for n in range(2)]
        xq_out = [sem(f"g_xq_out{n}", 16) for n in range(2)]
        st_out = [sem(f"g_st_out{n}", 16) for n in range(NS)]
        xT_ps, xq_done, xh_done, xl_done, g_ps, g_neg = (sem(f"g_{n}") for n in ("xT_ps", "xq", "xh", "xl", "ps", "neg"))
        g_sb, g_pos = sem("g_sb", 4), sem("g_pos", NS)
        red, all_, scl = sem("g_red"), sem("g_all"), sem("g_scl")
        block = ph.enter_context(nc.Block())
        JOB_AT = (0, 4, 8)

        def job_src(i, q):
            r = (i + q // JR) % ROUNDS
            q = q % JR
            if isinstance(r, int):
                return w_src[1 + q // 3][r, q % 3, :, :]
            return w_src[1 + q // 3][bass.ds(r, 1), q % 3, :, :].rearrange("a p k -> (a p) k")

        def job_dst(i, q):
            if q < 3:
                return by_input(wsc[1], i, q)
            return [d.rearrange("p (i h) -> p i h", h=H)[:, 4 * (q - 3):4 * (q - 3) + 4, bass.ds(i * P, P)] for d in wsc[2]]

        def rows(T):
            return xn_d[bass.ds(T * 512, 512), :].rearrange("(q p) d -> p q d", p=P)

        @block.sync
        def _(sp):
            sp.dma_start(xr[0][:, :, :], rows(0)).then_inc(xr_in[0], 16)
            for c in range(4):
                for W, d in ((Wh, wsc[0][0]), (Wl, wsc[0][1])):
                    sp.dma_start(W[:, 3 * c:3 * c + 3, :].bitcast(F32),
                                 d.rearrange("p (i k) -> p i k", k=512)[:, 3 * c:3 * c + 3, :]).then_inc(w_in[c], 16)
                if c == 0:
                    sp.dma_start(xr[1][:, :, :], rows(1)).then_inc(xr_in[1], 16)
            for q in range(2):
                job_load(sp, J, 0, q, job_src(0, q))
            sp.wait_ge(*at(xT_ps, 0, KT))
            sp.dma_start(xr[0][:, :, :], rows(2)).then_inc(xr_in[0], 16)
            with sp.Fori(0, FT // 2) as i:
                for t in range(2):
                    sp.wait_ge(*at(xq_done, 2 * KT * i, KT * t + KT))
                    sp.dma_start(xq_d[bass.ds(2 * i + t, 1), :, :].rearrange("a p k -> (a p) k"),
                                 xq[t][:, :, :].rearrange("p k n -> p (k n)")).then_inc(xq_out[t], 16)
                    for it in range(IT):
                        m = IT * t + it
                        n = m % NS
                        sp.wait_ge(*at(g_sb, 2 * IT * i, m + 1))
                        sp.dma_start(gate_d[bass.ds(8 * i + 4 * t, 4), :, it * P:(it + 1) * P].rearrange("q p n -> p q n"),
                                     stage[n][:, :].rearrange("p (q n) -> p q n", q=4)).then_inc(st_out[n], 16)
                        if it == 6:
                            src = rows((2 * i + (t + 3)) % FT)
                            sp.wait_ge(*at(xT_ps, 2 * KT * i, KT * t + 2 * KT))
                            sp.dma_start(xr[(t + 1) % 2][:, :, :], src).then_inc(xr_in[(t + 1) % 2], 16)
                        if it in (2, 6, 10):
                            q = 3 * t + it // 4
                            job_load(sp, J, i, q + 2, job_src(i, q + 2))
                        if it in (5, 9, 11):
                            q = 3 * t + (5, 9, 11).index(it)
                            job_store(sp, J, i, q, job_dst(i, q))
            for n in range(NS):
                sp.wait_ge(*at(st_out[n], 0, 16 * FT * IT // NS))
            for n in range(2):
                sp.wait_ge(*at(xq_out[n], 0, 16 * FT // 2))
                sp.wait_ge(*at(xr_in[n], 0, 16 * (FT // 2 + 1 + (n == 0))))
            for n in range(NJ):
                sp.wait_ge(*at(J.stored[n], 0, 32 * JR * ROUNDS // NJ))
                sp.wait_ge(*at(J.loaded[n], 0, 16 * (JR * ROUNDS // NJ + (n < 2))))

        @block.scalar
        def _(act):
            def parts(i, T):
                n = T % 2
                for kt in range(KT):
                    act.wait_ge(*at(xT_ps, 2 * KT * i, KT * T + kt + 1))
                    if kt == 0:
                        act.wait_ge(*at(xq_out[n], 16 * i, 16 * (T // 2)))
                    act.activation(xq[n][:, kt, :], pX[kt][:, :], ACT.Copy, scale=INV_X).then_inc(xq_done, 1)
                act.wait_ge(*at(xq_done, 2 * KT * i, KT * T + KT))
                act.activation(xh[n][:, :, :], xq[n][:, :, :], ACT.Copy).then_inc(xh_done, 1)

            parts(0, 0)
            with act.Fori(0, FT // 2) as i:
                for t in range(2):
                    for it in range(IT):
                        m = IT * t + it
                        n = m % NS
                        act.wait_ge(*at(g_ps, 2 * IT * i, m + 1))
                        act.wait_ge(*at(st_out[n], 32 * IT // NS * i, 16 * (m // NS)))
                        act.wait_ge(*at(g_pos, 2 * IT * i, m - NS + 1))
                        act.activation(stage[n][:, :], pG[m % 3][:, :], ACT.Copy, scale=S_X).then_inc(g_sb, 1)
                        if it == 4:
                            parts(i, t + 1)
                        if it in (3, 7, 11):
                            job_hi(act, J, i, 3 * t + it // 4)

        @block.vector
        def _(dve):
            def low(i, T):
                n = T % 2
                dve.wait_ge(*at(xh_done, 2 * i, T + 1))
                dve.tensor_tensor(xl[n][:, :, :], xq[n][:, :, :], xh[n][:, :, :].bitcast(F32), ALU.subtract).then_inc(xl_done, 1)

            low(0, 0)
            with dve.Fori(0, FT // 2) as i:
                for t in range(2):
                    for it in range(IT):
                        m = IT * t + it
                        dve.wait_ge(*at(g_sb, 2 * IT * i, m + 1))
                        dve.tensor_reduce(gmx[:, 1, bass.ds(2 * IT * i + m, 1)], stage[m % NS][:, :], X, ALU.min).then_inc(g_neg, 1)
                        dve.tensor_reduce(gmx[:, 0, bass.ds(2 * IT * i + m, 1)], stage[m % NS][:, :], X, ALU.max).then_inc(g_pos, 1)
                        if it == 6:
                            low(i, t + 1)
                        q = 3 * t + it // 4
                        if it % 4 == 0:
                            job_scale(dve, J, i, q)
                        if it % 4 == 1:
                            job_integer(dve, J, i, q)
                        if it % 4 == 3:
                            job_lo(dve, J, i, q)
            dve.wait_ge(*at(g_pos, 0, FT * IT))
            dve.wait_ge(g_neg, FT * IT)
            dve.tensor_reduce(GPOS, gmx[:, 0, :], X, ALU.max).then_inc(red, 1)
            dve.tensor_reduce(GNEG, gmx[:, 1, :], X, ALU.min, negate=True).then_inc(red, 1)
            dve.wait_ge(all_, 2)
            dve.tensor_tensor(AMAX, AP2, AN2, ALU.max).then_inc(scl, 1)
            dve.wait_ge(scl, 1)
            dve.tensor_scalar(S_G, AMAX, 1.0 / QMAX, TINY, ALU.mult, ALU.max).then_inc(scl, 1)
            dve.wait_ge(scl, 2)
            dve.reciprocal(INV_G, S_G).then_inc(scl, 1)
            dve.wait_ge(scl, 3)

        @block.gpsimd
        def _(pool):
            head_starts(pool, sems)
            with pool.Fori(0, FT // 2) as i:
                for q in range(JR):
                    job_divide(pool, J, i, q)
            pool.wait_ge(red, 2)
            pool.partition_all_reduce(AP2, GPOS, P, RMAX).then_inc(all_, 1)
            pool.partition_all_reduce(AN2, GNEG, P, RMAX).then_inc(all_, 1)

        @block.tensor
        def _(pe):
            def transposes(i, T):
                n = T % 2
                pe.wait_ge(*at(xr_in[n], 16 * i, 16 * (T // 2 + 1)))
                for kt in range(KT):
                    if T:
                        pe.wait_ge(*at(xq_done, 2 * KT * i, KT * (T - 1) + kt + 1))
                    for q in range(4):
                        mm = pe.transpose(pX[kt][:, q * P:(q + 1) * P], xr[n][:, q, kt * P:(kt + 1) * P], ident[:, :])
                    mm.then_inc(xT_ps, 1)

            transposes(0, 0)
            with pe.Fori(0, FT // 2) as i:
                for t in range(2):
                    pe.wait_ge(*at(xl_done, 2 * i, t + 1))
                    for it in range(IT):
                        m = IT * t + it
                        if it % 3 == 0:
                            pe.wait_ge(w_in[it // 3], 32)
                        pe.wait_ge(*at(g_sb, 2 * IT * i, m - 2))
                        product(pe, pG[m % 3], Wh, Wl, xh[t], xl[t], it).then_inc(g_ps, 1)
                        if it == 3:
                            transposes(i, t + 1)
                        if it % 4 == 2:
                            job_turn(pe, J, i, 3 * t + it // 4, ident)


def product(pe, ps, Wh, Wl, xh, xl, it):
    for kt in range(KT):
        for Ws, xs in ((Wh, xh), (Wh, xl), (Wl, xh)):
            mm = pe.matmul(ps[:, :], Ws[:, it, kt * P:(kt + 1) * P], xs[:, kt, :],
                           start=(kt == 0 and Ws is Wh and xs is xh), stop=(kt == KT - 1 and Ws is Wl))
    return mm


def up_phase(mk, xq_d, gate_d, up_d, w_d, nq, umx, fmx, sci, scu, S_X, cols, tmp):
    nc, sb, pb, sem, sems = mk
    S_G, INV_G, GMAX, S_F2, C_F, S_U, INV_U = cols
    T0, T1, T2, T3, T4 = tmp
    with ExitStack() as ph:
        Wh = sb(ph, "uWh", [P, IT, 512], F32R)
        Wl = sb(ph, "uWl", [P, IT, 512], F32R)
        xq = sb(ph, "uxq", [P, KT, 512], I16)
        xh = [sb(ph, f"uxh{n}", [P, KT, 512], F32R) for n in range(2)]
        xl = [sb(ph, f"uxl{n}", [P, KT, 512], F32R) for n in range(2)]
        NS = 3
        stage = [sb(ph, f"ust{n}", [P, 512], F32) for n in range(NS)]
        GA = 3
        GW = I // GA
        NG, NN, NM = 6, 4, 3
        gb = [sb(ph, f"gb{n}", [P, GW], F32) for n in range(NG)]
        nb = [sb(ph, f"nb{n}", [P, GW], I16) for n in range(NN)]
        mb = [sb(ph, f"mb{n}", [P, GW], U16) for n in range(NM)]
        pU = [pb(ph, f"pU{n}") for n in range(4)]
        HT = FT // 2
        GROUPS = QT * I // GW
        GR = GROUPS // HT
        w_in = [sem(f"u_w_in{n}") for n in range(4)]
        xq_in = sem("u_xq_in")
        g_in = [sem(f"u_g_in{n}") for n in range(NG)]
        st_out = [sem(f"u_st_out{n}", 16) for n in range(NS)]
        xh_done, xl_done, u_ps = (sem(f"u_{n}") for n in ("xh", "xl", "ps"))
        u_sb, u_max = sem("u_sb", 4), sem("u_max", NS)
        n_done, sig_done = sem("u_n"), sem("u_sig")
        m_done, f_done, kept = sem("u_m", NG), sem("u_f", NG), sem("u_kept", NG)
        link_s, red, all_, pos_n, pos_sig, pos_m, fmx_set, apart_p, apart_v = (sem(f"u_{n}") for n in
            ("link", "red", "all", "pos_n", "pos_sig", "pos_m", "fmx_set", "apart_p", "apart_v"))
        block = ph.enter_context(nc.Block())
        sig_at = {it: [gr for gr in range(GR) if gr * (IT - 1) // GR == it] for it in range(IT)}
        end_at = {it: sig_at.get(it - 1, []) for it in range(IT)}
        gate_g = gate_d.rearrange("q p (a k) -> q p a k", a=GA)

        def group(i, t, gr):
            return nq[:, bass.ds(2 * GR // GA * i + (GR // GA * t + gr // GA), 1), (gr % GA) * GW:(gr % GA + 1) * GW].rearrange("p a k -> p (a k)")

        def refill(sp, i, t, gr):
            src = gate_g[bass.ds((2 * GR // GA * i + (GR // GA * t + (gr + NG) // GA)) % QT, 1), :, gr % GA, :].rearrange("a p k -> (a p) k")
            sp.wait_ge(*at(f_done, 2 * GR * i, GR * t + gr + 1))
            sp.dma_start(gb[gr % NG][:, :], src)\
              .then_inc(g_in[gr % NG], 16)

        @block.sync
        def _(sp):
            sp.dma_start(xq[:, :, :].rearrange("p k n -> p (k n)"), xq_d[0, :, :]).then_inc(xq_in, 16)
            for c in range(4):
                for W, d in ((Wh, w_d[0]), (Wl, w_d[1])):
                    sp.dma_start(W[:, 3 * c:3 * c + 3, :].bitcast(F32),
                                 d.rearrange("p (i k) -> p i k", k=512)[:, 3 * c:3 * c + 3, :]).then_inc(w_in[c], 16)
                if c == 0:
                    for n in range(NG):
                        sp.dma_start(gb[n][:, :], gate_g[n // GA, :, n % GA, :]).then_inc(g_in[n], 16)
            for h in range(2):
                with sp.Fori(0, HT // 2) as i:
                    for t in range(2):
                        T = t + HT * h
                        src = xq_d[bass.ds((2 * i + (T + 1)) % FT, 1), :, :].rearrange("a p k -> (a p) k")
                        sp.wait_ge(*at(xl_done, 2 * i, T + 1))
                        sp.dma_start(xq[:, :, :].rearrange("p k n -> p (k n)"), src).then_inc(xq_in, 16)
                        for it in range(IT):
                            n = it % NS
                            sp.wait_ge(*at(u_sb, 2 * IT * i, IT * T + it + 1))
                            sp.dma_start(up_d[bass.ds(8 * i + 4 * T, 4), :, it * P:(it + 1) * P].rearrange("q p n -> p q n"),
                                         stage[n][:, :].rearrange("p (q n) -> p q n", q=4)).then_inc(st_out[n], 16)
                            for gr in end_at[it] if h == 0 else ():
                                refill(sp, i, t, gr)
            for n in range(NS):
                sp.wait_ge(*at(st_out[n], 0, 16 * FT * IT // NS))
            sp.wait_ge(xq_in, 16 * (FT + 1))
            for n in range(NG):
                sp.wait_ge(g_in[n], 16 * (GROUPS // NG + 1))

        @block.gpsimd
        def _(pool):
            head_starts(pool, sems)

            def integer(i, t, gr):
                n = gr % NG
                pool.wait_ge(*at(kept, 2 * GR * i, GR * t + gr - NN + 1))
                pool.wait_ge(*at(g_in[n], 32 * GR // NG * i, 16 * GR // NG * t + 16 * (gr // NG) + 16))
                pool.sem_inc(apart_p, 1)
                pool.tensor_scalar(nb[gr % NN][:, :], gb[n][:, :], INV_G, 0.0, ALU.mult, ALU.add).then_inc(n_done, 1)

            def sigmoid_int(h, i, t, gr):
                g0 = GR * t + gr + GROUPS * h
                pool.wait_ge(*at(f_done, 2 * GR * i, g0 - NM + 1))
                pool.wait_ge(*at(sig_done, 2 * GR * i, g0 + 1))
                pool.sem_inc(apart_p, 1)
                pool.tensor_scalar(mb[gr % NM][:, :], gb[gr % NG][:, :], SIG_ONE, 0.0, ALU.mult, ALU.add).then_inc(m_done, 1)

            for h in range(2):
                with pool.Fori(0, HT // 2) as i:
                    for t in range(2):
                        for gr in range(GR):
                            if h == 0:
                                integer(i, t, gr)
                            if gr >= 1:
                                sigmoid_int(h, i, t, gr - 1)
                        sigmoid_int(h, i, t, GR - 1)
                if h == 0:
                    pool.wait_ge(red, 1)
                    pool.partition_all_reduce(T1, T0, P, RMAX).then_inc(all_, 1)
            pool.wait_ge(red, 2)
            pool.partition_all_reduce(T1, T0, P, RMAX).then_inc(all_, 1)

        @block.scalar
        def _(act):
            act.wait_ge(pos_n, 1)
            act.activation(T3, sci[:, 0:1], ACT.Sigmoid, scale=S_G).then_inc(pos_sig, 1)
            act.wait_ge(xq_in, 16)
            act.activation(xh[0][:, :, :], xq[:, :, :], ACT.Copy).then_inc(xh_done, 1)
            for h in range(2):
                if h == 1:
                    for n in range(NG):
                        act.wait_ge(g_in[n], 16 * (GROUPS // NG + 1))
                with act.Fori(0, HT // 2) as i:
                    for t in range(2):
                        T = t + HT * h
                        for it in range(IT):
                            n = it % NS
                            m = IT * T + it
                            act.wait_ge(*at(u_ps, 2 * IT * i, m + 1))
                            act.wait_ge(*at(st_out[n], 32 * IT // NS * i, 16 * (m // NS)))
                            act.wait_ge(*at(u_max, 2 * IT * i, m - NS + 1))
                            act.activation(stage[n][:, :], pU[it % 4][:, :], ACT.Copy, scale=S_X).then_inc(u_sb, 1)
                            for gr in sig_at[it]:
                                g0 = GR * t + gr + GROUPS * h
                                if h == 0:
                                    act.wait_ge(*at(n_done, 2 * GR * i, g0 + 1))
                                    src = nb[gr % NN][:, :]
                                else:
                                    act.wait_ge(*at(m_done, 2 * GR * i, g0 - NG + 1))
                                    src = group(i, t, gr)
                                act.activation(gb[gr % NG][:, :], src, ACT.Sigmoid, scale=S_G).then_inc(sig_done, 1)
                            if it == 6:
                                act.wait_ge(*at(xq_in, 32 * i, 16 * T + 32))
                                act.activation(xh[(t + 1) % 2][:, :, :], xq[:, :, :], ACT.Copy).then_inc(xh_done, 1)

        @block.vector
        def _(dve):
            seq = [0]

            def link(ins):
                seq[0] += 1
                ins.then_inc(link_s, 1)
                dve.wait_ge(link_s, seq[0])

            dve.memset(fmx[:, 0:NG], 0.0).then_inc(fmx_set, 1)
            dve.wait_ge(fmx_set, 1)
            dve.tensor_scalar(sci[:, 0:1], GMAX, INV_G, None, ALU.mult).then_inc(pos_n, 1)
            dve.wait_ge(xh_done, 1)
            dve.tensor_tensor(xl[0][:, :, :], xq[:, :, :], xh[0][:, :, :].bitcast(F32), ALU.subtract).then_inc(xl_done, 1)
            dve.wait_ge(pos_sig, 1)
            dve.tensor_scalar(scu[:, 0:1], T3, SIG_ONE, None, ALU.mult).then_inc(pos_m, 1)
            for h in range(2):
                with dve.Fori(0, HT // 2) as i:
                    for t in range(2):
                        T = t + HT * h
                        for it in range(IT):
                            m = IT * T + it
                            dve.wait_ge(*at(u_sb, 2 * IT * i, m + 1))
                            dve.tensor_reduce(umx[:, bass.ds(2 * IT * i + m, 1)], stage[it % NS][:, :], X, ALU.max,
                                              apply_absolute_value=True).then_inc(u_max, 1)
                            for gr in end_at[it]:
                                g0 = GR * t + gr + GROUPS * h
                                dve.wait_ge(*at(m_done, 2 * GR * i, g0 + 1))
                                if h == 0:
                                    dve.wait_ge(*at(kept, 2 * GR * i, g0 - 1))
                                    dve.sem_inc(apart_v, 1)
                                    dve.tensor_tensor_reduce(out=gb[gr % NG][:, :], in0=nb[gr % NN][:, :], in1=mb[gr % NM][:, :],
                                                             scale=-1.0, scalar=fmx[:, gr % NG:gr % NG + 1], op0=ALU.mult, op1=ALU.max,
                                                             accum_out=fmx[:, gr % NG:gr % NG + 1]).then_inc(f_done, 1)
                                    dve.tensor_copy(group(i, t, gr), nb[gr % NN][:, :]).then_inc(kept, 1)
                                else:
                                    dve.scalar_tensor_tensor(out=group(i, t, gr), in0=group(i, t, gr), scalar=C_F, in1=mb[gr % NM][:, :],
                                                             op0=ALU.mult, op1=ALU.mult).then_inc(f_done, 1)
                            if it == 7:
                                dve.wait_ge(*at(xh_done, 2 * i, T + 2))
                                dve.tensor_tensor(xl[(t + 1) % 2][:, :, :], xq[:, :, :], xh[(t + 1) % 2][:, :, :].bitcast(F32),
                                                  ALU.subtract).then_inc(xl_done, 1)
                if h == 0:
                    dve.wait_ge(*at(f_done, 0, GROUPS))
                    dve.tensor_reduce(T0, fmx[:, 0:NG], X, ALU.max).then_inc(red, 1)
                    dve.wait_ge(all_, 1)
                    dve.wait_ge(pos_m, 1)
                    link(dve.tensor_copy(T2, sci[:, 0:1]))
                    link(dve.tensor_copy(T3, scu[:, 0:1]))
                    link(dve.tensor_tensor(T4, T2, T3, ALU.mult))
                    link(dve.tensor_tensor(T2, T4, T1, ALU.max))
                    link(dve.tensor_scalar(T3, S_G, 1.0 / SIG_ONE, None, ALU.mult))
                    link(dve.tensor_tensor(T4, T2, T3, ALU.mult))
                    link(dve.tensor_scalar(S_F2, T4, 1.0 / QMAX, TINY, ALU.mult, ALU.max))
                    link(dve.reciprocal(T2, S_F2))
                    link(dve.tensor_tensor(C_F, T2, T3, ALU.mult))
            dve.wait_ge(*at(u_max, 0, FT * IT))
            dve.tensor_reduce(T0, umx[:, :], X, ALU.max).then_inc(red, 1)
            dve.wait_ge(all_, 2)
            link(dve.tensor_scalar(S_U, T1, 1.0 / QMAX, TINY, ALU.mult, ALU.max))
            link(dve.reciprocal(INV_U, S_U))

        @block.tensor
        def _(pe):
            for h in range(2):
                with pe.Fori(0, HT // 2) as i:
                    for t in range(2):
                        T = t + HT * h
                        pe.wait_ge(*at(xl_done, 2 * i, T + 1))
                        for it in range(IT):
                            if it % 3 == 0:
                                pe.wait_ge(w_in[it // 3], 32)
                            pe.wait_ge(*at(u_sb, 2 * IT * i, IT * T + it - 3))
                            product(pe, pU[it % 4], Wh, Wl, xh[t], xl[t], it).then_inc(u_ps, 1)


def down_phase(mk, up_d, x1_d, of, w_d, nq, pmx, cols, tmp):
    nc, sb, pb, sem, sems = mk
    S_F2, S_U, INV_U, S_O, C_O, C_OUT, TG_F = cols
    T0, T1, T2, T3 = tmp
    with ExitStack() as dn:
        Wh = sb(dn, "dWh", [P, IT, H], F32R)
        Wl = sb(dn, "dWl", [P, IT, H], F32R)
        w_in = sem("d_w_in")

        def row_tile(g):
            return nq[:, bass.ds(g, 1), :].rearrange("p a k -> p (a k)")

        with ExitStack() as ph:
            NB = 4
            BY_ABS = 3
            ub = [sb(ph, f"xub{n}", [P, I], F32) for n in range(NB)]
            ui = [sb(ph, f"xui{n}", [P, I], I16) for n in range(NB)]
            ga = [sb(ph, f"xga{n}", [P, I], I16) for n in range(BY_ABS)]
            pp = sb(ph, "xpp", [P, I], F32)
            u_in = [sem(f"x_u_in{n}") for n in range(NB)]
            ui_done, p_done = sem("x_ui", NB), sem("x_p", NB)
            ga_done, prod, pmx_set, apart, link_s, red, all_ = (sem(f"x_{n}") for n in
                ("ga", "prod", "pmx_set", "apart", "link", "red", "all"))
            x_sems = [*u_in, ui_done, p_done]
            block = ph.enter_context(nc.Block())

            @block.sync
            def _(sp):
                with sp.Fori(0, QT // NB) as i:
                    for n in range(NB):
                        sp.wait_ge(*at(ui_done, NB * i, n - NB + 1))
                        sp.dma_start(ub[n][:, :], up_d[bass.ds(NB * i + n, 1), :, :].rearrange("a p k -> (a p) k")).then_inc(u_in[n], 16)
                for W, d in ((Wh, w_d[0]), (Wl, w_d[1])):
                    sp.dma_start(W[:, :, :].bitcast(F32), d.rearrange("p (i k) -> p i k", k=H)).then_inc(w_in, 16)

            @block.scalar
            def _(act):
                with act.Fori(0, QT // NB) as i:
                    for n in range(NB):
                        act.wait_ge(*at(p_done, NB * i, n - NB + 1))
                        act.wait_ge(*at(u_in[n], 16 * i, 16))
                        act.activation(ui[n][:, :], ub[n][:, :], ACT.Abs if n < BY_ABS else ACT.Copy, scale=INV_U).then_inc(ui_done, 1)
                        if n < BY_ABS:
                            act.activation(ga[n][:, :], row_tile(NB * i + n), ACT.Abs).then_inc(ga_done, 1)

            @block.vector
            def _(dve):
                seq = [0]

                def link(ins):
                    seq[0] += 1
                    ins.then_inc(link_s, 1)
                    dve.wait_ge(link_s, seq[0])

                dve.memset(pmx[:, :], 0.0).then_inc(pmx_set, 1)
                dve.wait_ge(pmx_set, 1)
                with dve.Fori(0, QT // NB) as i:
                    for n in range(NB):
                        dve.wait_ge(*at(p_done, NB * i, n))
                        if n < BY_ABS:
                            dve.wait_ge(*at(ga_done, BY_ABS * i, n + 1))
                            dve.sem_inc(apart, 1)
                            dve.tensor_tensor_reduce(out=pp[:, :], in0=ga[n][:, :], in1=ui[n][:, :], scale=1.0,
                                                     scalar=pmx[:, n:n + 1], op0=ALU.mult, op1=ALU.max,
                                                     accum_out=pmx[:, n:n + 1]).then_inc(p_done, 1)
                        else:
                            dve.wait_ge(*at(ui_done, NB * i, n + 1))
                            dve.tensor_tensor(pp[:, :], row_tile(NB * i + n), ui[n][:, :], ALU.mult).then_inc(prod, 1)
                            dve.wait_ge(*at(prod, i, 1))
                            dve.tensor_reduce(pmx[:, bass.ds(i + NB, 1)], pp[:, :], X, ALU.max,
                                              apply_absolute_value=True).then_inc(p_done, 1)
                dve.wait_ge(*at(p_done, 0, QT))
                dve.tensor_reduce(T0, pmx[:, :], X, ALU.max).then_inc(red, 1)
                dve.wait_ge(all_, 1)
                link(dve.tensor_tensor(T2, S_F2, S_U, ALU.mult))
                link(dve.tensor_tensor(T3, T1, T2, ALU.mult))
                link(dve.tensor_scalar(S_O, T3, 1.0 / QMAX, TINY, ALU.mult, ALU.max))
                link(dve.reciprocal(T0, S_O))
                link(dve.tensor_tensor(C_O, T0, T2, ALU.mult))
                link(dve.tensor_tensor(C_OUT, S_O, TG_F, ALU.mult))

            @block.gpsimd
            def _(pool):
                head_starts(pool, x_sems)
                pool.wait_ge(red, 1)
                pool.partition_all_reduce(T1, T0, P, RMAX).then_inc(all_, 1)

        with ExitStack() as ph:
            ub = [sb(ph, f"dub{n}", [P, I], F32) for n in range(2)]
            ui = [sb(ph, f"dui{n}", [P, I], I16) for n in range(2)]
            oq = [sb(ph, f"doq{n}", [P, I], I16) for n in range(2)]
            oh = [sb(ph, f"doh{n}", [P, I], F32R) for n in range(2)]
            ol = [sb(ph, f"dol{n}", [P, I], F32R) for n in range(2)]
            xr = [sb(ph, f"dxr{n}", [P, H], F32) for n in range(2)]
            yo = [sb(ph, f"dyo{n}", [P, H], F32) for n in range(2)]
            pD = [pb(ph, f"pD{n}") for n in range(4)]
            u_in = [sem(f"d_u_in{n}") for n in range(2)]
            x_in = [sem(f"d_x_in{n}") for n in range(2)]
            y_out = [sem(f"d_y_out{n}", 16) for n in range(2)]
            ui_done, o_done, oh_done, ol_done, d_ps, y_done = (sem(f"d_{n}", 4) for n in ("ui", "o", "oh", "ol", "ps", "y"))
            d_sems = [*y_out, ui_done, o_done, oh_done, ol_done, d_ps, y_done]
            block = ph.enter_context(nc.Block())
            NU = 4

            def load_up(sp, i, g):
                src = up_d[bass.ds(NU * i + g, 1), :, :].rearrange("a p k -> (a p) k")
                sp.wait_ge(*at(ui_done, NU * i, g - 1))
                sp.dma_start(ub[g % 2][:, :], src).then_inc(u_in[g % 2], 16)

            def load_x(sp, i, g):
                src = x1_d[bass.ds(NU * P * i + g * P, P), :]
                sp.wait_ge(*at(y_done, NU * i, g - 1))
                sp.dma_start(xr[g % 2][:, :], src).then_inc(x_in[g % 2], 16)

            def output(sp, i, g):
                y_dst = of[bass.ds(NU * P * i + g * P, P), :]
                sp.wait_ge(*at(y_done, NU * i, g + 1))
                sp.dma_start(y_dst, yo[g % 2][:, :]).then_inc(y_out[g % 2], 16)

            @block.sync
            def _(sp):
                for g in range(2):
                    load_up(sp, 0, g)
                    load_x(sp, 0, g)
                load_up(sp, 0, 2)
                with sp.Fori(0, QT // NU - 1) as i:
                    for g in range(NU):
                        load_up(sp, i, g + 3)
                        output(sp, i, g)
                        load_x(sp, i, g + 2)
                for g in range(NU):
                    if g < 1:
                        load_up(sp, QT // NU - 1, g + 3)
                    output(sp, QT // NU - 1, g)
                    if g < 2:
                        load_x(sp, QT // NU - 1, g + 2)
                for n in range(2):
                    sp.wait_ge(*at(y_out[n], 0, 16 * QT // 2))

            @block.gpsimd
            def _(pool):
                head_starts(pool, d_sems)

            @block.scalar
            def _(act):
                with act.Fori(0, QT // NU) as i:
                    for g in range(NU):
                        n = g % 2
                        act.wait_ge(*at(u_in[n], 16 * NU // 2 * i, 16 * (g // 2 + 1)))
                        act.wait_ge(*at(o_done, NU * i, g - 1))
                        act.activation(ui[n][:, :], ub[n][:, :], ACT.Copy, scale=INV_U).then_inc(ui_done, 1)
                        act.wait_ge(*at(o_done, NU * i, g + 1))
                        act.wait_ge(*at(d_ps, NU * i, g - 1))
                        act.activation(oh[n][:, :], oq[n][:, :], ACT.Copy).then_inc(oh_done, 1)

            @block.vector
            def _(dve):
                def finish(i, g):
                    n = g % 2
                    dve.wait_ge(*at(d_ps, NU * i, g + 1))
                    dve.wait_ge(*at(x_in[n], 16 * NU // 2 * i, 16 * (g // 2 + 1)))
                    dve.wait_ge(*at(y_out[n], 16 * NU // 2 * i, 16 * (g // 2)))
                    dve.scalar_tensor_tensor(out=yo[n][:, :], in0=pD[g % 4][:, :], scalar=C_OUT, in1=xr[n][:, :],
                                             op0=ALU.mult, op1=ALU.add).then_inc(y_done, 1)

                def quantize(i, g):
                    n = g % 2
                    dve.wait_ge(*at(ui_done, NU * i, g + 1))
                    dve.wait_ge(*at(ol_done, NU * i, g - 1))
                    dve.scalar_tensor_tensor(out=oq[n][:, :], in0=row_tile(NU * i + g), scalar=C_O,
                                             in1=ui[n][:, :], op0=ALU.mult, op1=ALU.mult).then_inc(o_done, 1)

                def low(i, g):
                    n = g % 2
                    dve.wait_ge(*at(oh_done, NU * i, g + 1))
                    dve.tensor_tensor(ol[n][:, :], oq[n][:, :], oh[n][:, :].bitcast(F32), ALU.subtract).then_inc(ol_done, 1)

                for g in range(2):
                    quantize(0, g)
                    low(0, g)
                with dve.Fori(0, QT // NU - 1) as i:
                    for g in range(NU):
                        quantize(i, g + 2)
                        finish(i, g)
                        low(i, g + 2)
                for g in range(NU):
                    if g < 2:
                        quantize(QT // NU - 1, g + 2)
                    finish(QT // NU - 1, g)
                    if g < 2:
                        low(QT // NU - 1, g + 2)

            @block.tensor
            def _(pe):
                pe.wait_ge(w_in, 32)
                with pe.Fori(0, QT // NU) as i:
                    for g in range(NU):
                        n = g % 2
                        pe.wait_ge(*at(ol_done, NU * i, g + 1))
                        pe.wait_ge(*at(y_done, NU * i, g - 3))
                        for it in range(IT):
                            cs = slice(it * P, (it + 1) * P)
                            for os_, Ws in ((oh[n], Wh), (oh[n], Wl), (ol[n], Wh)):
                                mm = pe.matmul(pD[g % 4][:, :], os_[:, cs], Ws[:, it, :],
                                               start=(it == 0 and os_ is oh[n] and Ws is Wh),
                                               stop=(it == IT - 1 and os_ is ol[n]))
                        mm.then_inc(d_ps, 1)


_INS = ["x", "ctx_1024", "g_xattn", "g_ffn", "L0_xattn_w_q", "L0_xattn_w_k", "L0_xattn_w_v", "L0_xattn_w_o",
        "L0_ffn_w_gate", "L0_ffn_w_up", "L0_ffn_w_down"]


def kernel(**inputs):
    import numpy as _np
    import concourse.bacc as _bacc
    from concourse import mybir as _mybir
    from concourse.bass_utils import run_bass_kernel_spmd as _run

    nc = _bacc.Bacc("TRN2", target_bir_lowering=False, num_devices=1)
    arrays, args = {}, []
    for name in _INS:
        a = _np.ascontiguousarray(inputs[name])
        arrays[f"in_{name}"] = a
        args.append(nc.dram_tensor(f"in_{name}", a.shape, _mybir.dt.from_np(a.dtype), kind="ExternalInput").ap())
    out = nc.dram_tensor("out_0", (B, S, H), F32, kind="ExternalOutput").ap()
    flamingo_block(nc, *args, out)
    r = _run(nc, [arrays], core_ids=[0])
    return r.results[0]["out_0"]
```

```python
from contextlib import ExitStack

import concourse.bass as bass
from concourse import mybir

F32 = mybir.dt.float32
F32R = mybir.dt.float32r
I16 = mybir.dt.int16
U16 = mybir.dt.uint16
ALU = mybir.AluOpType
ACT = mybir.ActivationFunctionType
X = mybir.AxisListType.X
RMAX = bass.bass_isa.ReduceOp.max

P = 128
B, S, H = 4, 1024, 512
CK = 64
HEADS, HD = 16, 64
INNER = HEADS * HD
I = 1536
TOK = B * S
KT = H // P
PAIRS = HEADS // 2
IT = I // P
QT = TOK // P
BQ = S // P
FT = TOK // 512
BLK = 32
NBLK = 512 // BLK
LN_EPS = 1e-5
TINY = 1e-12
QMAX = 32767.0
SIG_ONE = 65536.0
SCALE = HD ** -0.5


LEAD = {}


def at(sem, base, n):
    assert n + LEAD[sem.name] >= 1, (sem.name, n)
    return sem, base + (n + LEAD[sem.name])


def head_starts(pool, sems):
    for s in sems:
        if LEAD[s.name]:
            pool.sem_inc(s, LEAD[s.name])


def flamingo_block(nc, x, ctx, g_xattn, g_ffn, w_q, w_k, w_v, w_o, w_gate, w_up, w_down, out):
    xf = x.rearrange("b s d -> (b s) d")
    cf = ctx.rearrange("b s d -> (b s) d")
    of = out.rearrange("b s d -> (b s) d")

    wsc = [[nc.dram_tensor(f"w{n}_{part}", (P, IT * 512), F32).ap() for part in ("hi", "lo")]
           for n in ("gate", "up", "down")]
    x1_d = nc.dram_tensor("x1_d", (TOK, H), F32).ap()
    xn_d = nc.dram_tensor("xn_d", (TOK, H), F32).ap()
    xq_d = nc.dram_tensor("xq_d", (FT, P, KT * 512), I16).ap()
    gate_d = nc.dram_tensor("gate_d", (QT, P, IT * P), F32).ap()
    up_d = nc.dram_tensor("up_d", (QT, P, IT * P), F32).ap()
    w_src = [w_gate.rearrange("(r c p) k -> r c p k", r=ROUNDS, p=P),
             w_up.rearrange("(r c p) k -> r c p k", r=ROUNDS, p=P),
             w_down.rearrange("(r p) (c k) -> r c p k", p=P, c=3)]

    with ExitStack() as top:
        phase_sems = []

        def sb(scope, name, shape, dt):
            return scope.enter_context(nc.sbuf_tensor(name, shape, dt))

        def pb(scope, name, n=512):
            return scope.enter_context(nc.psum_tensor(name, [P, n], F32))

        def sem(name, lead=0):
            s = nc.alloc_semaphore(name=name)
            LEAD[s.name] = lead
            phase_sems.append(s)
            return s

        def lasting(name):
            s = nc.alloc_semaphore(name=name)
            LEAD[s.name] = 0
            return s

        def release_sems():
            nc.clear_and_free_semaphores(phase_sems)
            nc.all_engine_barrier()
            phase_sems.clear()

        mk = (nc, sb, pb, sem, phase_sems)
        ident = sb(top, "ident", [P, P], F32)
        mask = sb(top, "mask", [P, CK], F32)
        half = sb(top, "half", [P, 2], F32)
        sc = sb(top, "sc", [P, 32], F32)
        xmx = sb(top, "xmx", [P, QT], F32)
        gmx = sb(top, "gmx", [P, 2, FT * IT], F32)
        umx = sb(top, "umx", [P, FT * IT], F32)
        fmx = sb(top, "fmx", [P, 8], F32)
        pmx = sb(top, "pmx", [P, 16], F32)
        sci = sb(top, "sci", [P, 2], I16)
        scu = sb(top, "scu", [P, 2], U16)
        (TG_X, TG_F, RAW_X, RAW_F, S_X, INV_X, S_G, INV_G, S_U, INV_U, C_F, S_F2, S_O, C_O, C_OUT,
         T0, T1, T2, T3, T4, AMAX, GPOS, GNEG, AP2, AN2) = [sc[:, n:n + 1] for n in range(25)]

        with ExitStack() as att:
            wqT = sb(att, "wqT", [P, PAIRS, H], F32)
            wo = sb(att, "wo", [P, PAIRS, H], F32)
            kT = sb(att, "kT", [P, PAIRS, B * CK], F32)
            vT = sb(att, "vT", [P, PAIRS, B * CK], F32)
            kbd = sb(att, "kbd", [P, PAIRS, P], F32)
            vbd = sb(att, "vbd", [P, PAIRS, P], F32)
            xin = [sb(att, f"xin{n}", [P, H], F32) for n in range(BQ)]
            x_in = [lasting(f"x_in{n}") for n in range(BQ)]
            prepare(mk, xf, xin, x_in, cf, w_q, w_k, w_v, w_o, g_xattn, g_ffn, w_src[0], wsc[0], ident, mask, half,
                    (TG_X, TG_F, RAW_X, RAW_F), wqT, wo, kT, vT, kbd, vbd)
            release_sems()
            attend(mk, xin, x_in, xf, x1_d, xn_d, ident, mask, half, xmx, TG_X, (S_X, INV_X, T0, T1), wqT, wo, kT, vT, kbd, vbd)
            release_sems()
        with ExitStack() as ff:
            W = [sb(ff, f"W{part}", [P, IT, 512], F32R) for part in ("h", "l")]
            w_in = [[sem(f"w_{n}_in{c}") for c in range(4)] for n in ("gate", "up", "down")]
            uxq, uxq_in = sb(ff, "uxq", [P, KT, 512], I16), sem("u_xq_in")
            load_w = [lambda eng, c, d=d, s=s: load_weights(eng, W, d, s, c) for d, s in zip(wsc, w_in)]
            gate_phase(mk, xn_d, xq_d, uxq, uxq_in, gate_d, wsc, w_src, W, w_in[0], load_w, ident, gmx, S_X, INV_X,
                       (GPOS, GNEG, AP2, AN2, AMAX, S_G, INV_G))
            nq = sb(ff, "nq", [P, QT, I], I16)
            up_phase(mk, xq_d, uxq, uxq_in, gate_d, up_d, W, w_in[1], load_w, nq, umx, fmx, sci, scu, S_X,
                     (S_G, INV_G, AP2, S_F2, C_F, S_U, INV_U), (T0, T1, T2, T3, T4))
            down_phase(mk, up_d, x1_d, of, W, w_in[2], load_w[2], nq, pmx,
                       (S_F2, S_U, INV_U, S_O, C_O, C_OUT, TG_F), (T0, T1, T2, T3))



NJ = 3
ROUNDS = 4


def load_weights(eng, W, d, w_in, c):
    for part, src in zip(W, d):
        eng.dma_start(part[:, 3 * c:3 * c + 3, :].bitcast(F32),
                      src.rearrange("p (i k) -> p i k", k=512)[:, 3 * c:3 * c + 3, :]).then_inc(w_in[c], 16)


class Jobs:

    def __init__(self, mk, ph, tag, R, banks):
        nc, sb, pb, sem, _ = mk
        self.R = R
        self.w = [sb(ph, f"{tag}w{n}", [P, 512], F32) for n in range(NJ)]
        self.q = [sb(ph, f"{tag}q{n}", [P, 512], I16) for n in range(NJ)]
        self.d = [sb(ph, f"{tag}d{n}", [P, 512], F32) for n in range(NJ)]
        self.hi = [sb(ph, f"{tag}hi{n}", [P, 512], F32R) for n in range(NJ)]
        self.lo = [sb(ph, f"{tag}lo{n}", [P, 512], F32R) for n in range(NJ)]
        self.mx = sb(ph, f"{tag}mx", [P, NJ, NBLK], F32)
        self.s = sb(ph, f"{tag}s", [P, NJ, NBLK], F32)
        self.inv = sb(ph, f"{tag}inv", [P, NJ, NBLK], F32)
        self.bank = [pb(ph, f"{tag}bank{n}") for n in range(banks)]
        self.loaded = [sem(f"{tag}_loaded{n}") for n in range(NJ)]
        self.stored = [sem(f"{tag}_stored{n}", 32) for n in range(NJ)]
        self.max_done, self.scale_done, self.inv_done, self.div_done, self.int_done, self.hi_done = (
            sem(f"{tag}_{n}") for n in ("max", "scale", "inv", "div", "int", "hi"))
        self.apart = sem(f"{tag}_apart")
        self.deq_done, self.turned, self.lo_done = sem(f"{tag}_deq", NJ), sem(f"{tag}_turned", NJ), sem(f"{tag}_lo", NJ)


def blocks(ap):
    return ap.rearrange("p (b k) -> p b k", k=BLK)


def spread(ap):
    return ap.unsqueeze(2).to_broadcast([P, NBLK, BLK])


def job_load(sp, J, i, q, src):
    sp.wait_ge(*at(J.deq_done, J.R * i, q - NJ + 1))
    sp.sem_inc(J.apart, 1)
    sp.dma_start(J.w[q % NJ][:, :], src).then_inc(J.loaded[q % NJ], 16)


def job_scale(dve, J, i, q):
    n = q % NJ
    dve.wait_ge(*at(J.loaded[n], 16 * (J.R // NJ) * i, 16 * (q // NJ + 1)))
    dve.tensor_reduce(J.mx[:, n, :], blocks(J.w[n][:, :]), X, ALU.max, apply_absolute_value=True).then_inc(J.max_done, 1)
    dve.wait_ge(*at(J.max_done, J.R * i, q + 1))
    dve.tensor_scalar(J.s[:, n, :], J.mx[:, n, :], 1.0 / 7.0, TINY, ALU.mult, ALU.max).then_inc(J.scale_done, 1)
    dve.wait_ge(*at(J.scale_done, J.R * i, q + 1))
    dve.reciprocal(J.inv[:, n, :], J.s[:, n, :]).then_inc(J.inv_done, 1)


def job_divide(pool, J, i, q):
    n = q % NJ
    pool.wait_ge(*at(J.inv_done, J.R * i, q + 1))
    pool.tensor_tensor(blocks(J.w[n][:, :]), blocks(J.w[n][:, :]), spread(J.inv[:, n, :]), ALU.mult).then_inc(J.div_done, 1)


def job_integer(dve, J, i, q):
    n = q % NJ
    dve.wait_ge(*at(J.div_done, J.R * i, q + 1))
    dve.tensor_scalar(J.q[n][:, :], J.w[n][:, :], 1.0, None, ALU.mult).then_inc(J.int_done, 1)
    dve.wait_ge(*at(J.int_done, J.R * i, q + 1))
    dve.wait_ge(*at(J.turned, J.R * i, q - NJ + 1))
    dve.tensor_tensor(blocks(J.d[n][:, :]), blocks(J.q[n][:, :]), spread(J.s[:, n, :]), ALU.mult).then_inc(J.deq_done, 1)


def job_turn(pe, J, i, q, ident):
    n, m = q % NJ, q % len(J.bank)
    pe.wait_ge(*at(J.lo_done, J.R * i, q - len(J.bank) + 1))
    pe.wait_ge(*at(J.deq_done, J.R * i, q + 1))
    for kt in range(4):
        mm = pe.transpose(J.bank[m][:, kt * P:(kt + 1) * P], J.d[n][:, kt * P:(kt + 1) * P], ident[:, :])
    mm.then_inc(J.turned, 1)


def job_hi(act, J, i, q):
    n, m = q % NJ, q % len(J.bank)
    act.wait_ge(*at(J.stored[n], 32 * (J.R // NJ) * i, 32 * (q // NJ)))
    act.wait_ge(*at(J.turned, J.R * i, q + 1))
    act.activation(J.hi[n][:, :], J.bank[m][:, :], ACT.Copy).then_inc(J.hi_done, 1)


def job_lo(dve, J, i, q):
    n, m = q % NJ, q % len(J.bank)
    dve.wait_ge(*at(J.stored[n], 32 * (J.R // NJ) * i, 32 * (q // NJ)))
    dve.wait_ge(*at(J.hi_done, J.R * i, q + 1))
    dve.tensor_tensor(J.lo[n][:, :], J.bank[m][:, :], J.hi[n][:, :].bitcast(F32), ALU.subtract).then_inc(J.lo_done, 1)


def job_store(sp, J, i, q, dsts):
    n = q % NJ
    sp.wait_ge(*at(J.lo_done, J.R * i, q + 1))
    for part, dst in zip((J.hi[n], J.lo[n]), dsts):
        src = part[:, :].bitcast(F32)
        if len(dst.shape) == 3:
            src = src.rearrange("p (i h) -> p i h", h=P)
        sp.dma_start(dst, src).then_inc(J.stored[n], 16)


def by_input(w, r, c):
    return [d[:, bass.ds(r * (3 * 512) + c * 512, 512)] for d in w]


def diagonal(act, kT, vT, kbd, vbd, b, kbd_set, vbd_set):
    for bd, t, s in ((kbd, kT, kbd_set), (vbd, vT, vbd_set)):
        for a in range(2):
            rows = slice(a * 64, a * 64 + 64)
            act.activation(bd[rows, :, a * 64:a * 64 + 64], t[rows, :, bass.ds(CK * b, CK)], ACT.Copy).then_inc(s, 1)


def prepare(mk, xf, xin, x_in, cf, w_q, w_k, w_v, w_o, g_xattn, g_ffn, w_src, w_dst, ident, mask, half, cols,
            wqT, wo, kT, vT, kbd, vbd):
    nc, sb, pb, sem, sems = mk
    TG_X, TG_F, RAW_X, RAW_F = cols
    with ExitStack() as ph:
        wq = sb(ph, "wq", [P, KT, INNER], F32)
        wk = sb(ph, "wk", [P, KT, INNER], F32)
        wv = sb(ph, "wv", [P, KT, INNER], F32)
        cx = sb(ph, "cx", [P, 2, H], F32)
        cT = sb(ph, "cT", [P, KT, B * CK], F32)
        JR = 3
        NJOBS = JR * ROUNDS
        J = Jobs(mk, ph, "pj", JR, 3)
        pw = [pb(ph, f"pw{n}") for n in range(2)]
        pk = pb(ph, "pk")
        pv = pb(ph, "pv")
        ctx_in, wo_in, g_in = (sem(n) for n in ("ctx_in", "wo_in", "g_in"))
        wq_in, wk_in, wv_in = ([sem(f"{n}_in{r}") for r in range(2)] for n in ("wq", "wk", "wv"))
        const_set, id_set, ctxT_ps, ctxT_sb, wqT_ps, wqT_sb, k_ps, k_sb, v_ps, v_sb, tanh_done, bd_zero, bd_set = (sem(n) for n in
            ("const_set", "id_set", "ctxT_ps", "ctxT_sb", "wqT_ps", "wqT_sb", "k_ps", "k_sb", "v_ps", "v_sb", "tanh_done", "bd_zero", "bd_set"))
        block = ph.enter_context(nc.Block())
        HC = INNER // 2

        @block.sync
        def _(sp):
            sp.dma_start(cx[:, :, :], cf.rearrange("(t p) d -> p t d", p=P)).then_inc(ctx_in, 16)
            sp.dma_start(wq[:, :, 0:HC], w_q.rearrange("(t p) n -> p t n", p=P)[:, :, 0:HC]).then_inc(wq_in[0], 16)
            for q in range(NJ):
                job_load(sp, J, 0, q, w_src[0, q, :, :])
            for r in range(2):
                for w, d, s in ((wk, w_k, wk_in), (wv, w_v, wv_in), (wq, w_q, wq_in)):
                    if w is not wq or r == 0:
                        rr = 1 if w is wq else r
                        sp.dma_start(w[:, :, rr * HC:(rr + 1) * HC],
                                     d.rearrange("(t p) n -> p t n", p=P)[:, :, rr * HC:(rr + 1) * HC]).then_inc(s[rr], 16)
                    if r == 1:
                        q = [n for n, v in enumerate((wk, wv, wq)) if v is w][0]
                        job_load(sp, J, 0, q + NJ, w_src[1, q, :, :])

            def load_wo(r):
                pairs = bass.ds(2 * r, 2)
                sp.dma_start(wo[:, pairs, :], w_o.rearrange("(t p) n -> p t n", p=P)[:, pairs, :]).then_inc(wo_in, 16)

            for q in range(JR):
                job_store(sp, J, 0, q, by_input(w_dst, 0, q))
            with sp.Fori(1, ROUNDS - 1) as r:
                for q in range(JR):
                    job_load(sp, J, r, q + NJ, w_src[bass.ds(r + 1, 1), q, :, :].rearrange("a p k -> (a p) k"))
                    job_store(sp, J, r, q, by_input(w_dst, r, q))
                load_wo(r)
            for r in (0, ROUNDS - 1):
                load_wo(r)
            for q in range(JR):
                job_store(sp, J, ROUNDS - 1, q, by_input(w_dst, ROUNDS - 1, q))
            for j in range(BQ):
                sp.dma_start(xin[j][:, :], xf[j * P:(j + 1) * P, :]).then_inc(x_in[j], 16)
            for n in range(NJ):
                sp.wait_ge(*at(J.stored[n], 0, 32 * NJOBS // NJ))
            sp.wait_ge(wo_in, 16 * ROUNDS)

        @block.gpsimd
        def _(pool):
            head_starts(pool, sems)
            pool.memset(ident[:, :], 0.0).then_inc(const_set, 1)
            pool.memset(mask[:, :], 0.0).then_inc(const_set, 1)
            pool.memset(half[:, 0:1], -0.5).then_inc(const_set, 1)
            pool.memset(half[:, 1:2], LN_EPS).then_inc(const_set, 1)
            pool.wait_ge(const_set, 4)
            pool.affine_select(out=ident[:, :], in_=ident[:, :], compare_op=ALU.not_equal, fill=1.0,
                               base=0, pattern=[[-1, P]], channel_multiplier=1).then_inc(id_set, 1)
            pool.affine_select(out=mask[:, :], in_=mask[:, :], compare_op=ALU.is_ge, fill=-10000.0,
                               base=0, pattern=[[-1, CK]], channel_multiplier=1).then_inc(id_set, 1)
            pool.memset(kbd[:, :, :], 0.0).then_inc(bd_zero, 1)
            pool.memset(vbd[:, :, :], 0.0).then_inc(bd_zero, 1)
            with pool.Fori(0, ROUNDS) as r:
                for q in range(JR):
                    job_divide(pool, J, r, q)

        @block.scalar
        def _(act):
            act.dma_start(RAW_X, g_xattn.unsqueeze(0).to_broadcast([P, 1])).then_inc(g_in, 16)
            act.dma_start(RAW_F, g_ffn.unsqueeze(0).to_broadcast([P, 1])).then_inc(g_in, 16)
            for kt in range(2):
                act.wait_ge(ctxT_ps, kt + 1)
                act.activation(cT[:, 2 * kt:2 * kt + 2, :].rearrange("p a b -> p (a b)"), pw[kt][:, :],
                               ACT.Copy).then_inc(ctxT_sb, 1)
            act.wait_ge(g_in, 32)
            act.activation(TG_X, RAW_X, ACT.Tanh).then_inc(tanh_done, 1)
            act.activation(TG_F, RAW_F, ACT.Tanh).then_inc(tanh_done, 1)
            with act.Fori(0, ROUNDS) as r:
                for a in range(2):
                    act.wait_ge(wqT_ps, 2 * r + a + 1)
                    act.activation(wqT[:, bass.ds(2 * r + a, 1), :].rearrange("p a b -> p (a b)"), pw[a][:, :],
                                   ACT.Copy).then_inc(wqT_sb, 1)
                job_hi(act, J, r, 0)
                act.wait_ge(k_ps, r + 1)
                act.activation(kT[:, bass.ds(2 * r, 2), :].rearrange("p a b -> p (a b)"), pk[:, :],
                               ACT.Copy).then_inc(k_sb, 1)
                job_hi(act, J, r, 1)
                act.wait_ge(v_ps, r + 1)
                act.activation(vT[:, bass.ds(2 * r, 2), :].rearrange("p a b -> p (a b)"), pv[:, :],
                               ACT.Copy).then_inc(v_sb, 1)
                job_hi(act, J, r, 2)
            act.wait_ge(bd_zero, 2)
            act.wait_ge(k_sb, ROUNDS)
            act.wait_ge(v_sb, ROUNDS)
            diagonal(act, kT, vT, kbd, vbd, 0, bd_set, bd_set)

        @block.vector
        def _(dve):
            def run(r, k, last=False):
                if not last:
                    job_scale(dve, J, r, k)
                if k >= 1 and not (last and k > JR):
                    job_integer(dve, J, r, k - 1)
                if k >= 2:
                    job_lo(dve, J, r, k - 2)

            run(0, 0)
            run(0, 1)
            with dve.Fori(0, ROUNDS - 1) as r:
                for k in range(2, 2 + JR):
                    run(r, k)
            run(ROUNDS - 1, 2)
            run(ROUNDS - 1, 3, last=True)
            run(ROUNDS - 1, 4, last=True)

        @block.tensor
        def _(pe):
            pe.wait_ge(id_set, 1)
            pe.wait_ge(ctx_in, 16)
            for kt in range(KT):
                for t in range(2):
                    mm = pe.transpose(pw[kt // 2][:, (kt % 2) * 256 + t * P:(kt % 2) * 256 + (t + 1) * P],
                                      cx[:, t, kt * P:(kt + 1) * P], ident[:, :])
                if kt % 2:
                    mm.then_inc(ctxT_ps, 1)
            pe.wait_ge(ctxT_sb, 2)
            for r in range(ROUNDS):
                pe.wait_ge(wq_in[r // 2], 16)
                if r:
                    pe.wait_ge(wqT_sb, 2 * r)
                for a in range(2):
                    for kt in range(KT):
                        mm = pe.transpose(pw[a][:, kt * P:(kt + 1) * P],
                                          wq[:, kt, (2 * r + a) * P:(2 * r + a + 1) * P], ident[:, :])
                    mm.then_inc(wqT_ps, 1)
                job_turn(pe, J, r, 0, ident)
                for n, (w, ps, s_in, s_ps, s_sb) in enumerate(((wk, pk, wk_in, k_ps, k_sb), (wv, pv, wv_in, v_ps, v_sb))):
                    pe.wait_ge(s_in[r // 2], 16)
                    if r:
                        pe.wait_ge(s_sb, r)
                    for a in range(2):
                        for kt in range(KT):
                            mm = pe.matmul(ps[:, a * 256:(a + 1) * 256], w[:, kt, (2 * r + a) * P:(2 * r + a + 1) * P],
                                           cT[:, kt, :], start=(kt == 0), stop=(kt == KT - 1))
                    mm.then_inc(s_ps, 1)
                    job_turn(pe, J, r, n + 1, ident)


def attend(mk, xin, x_in, xf, x1_d, xn_d, ident, mask, half, xmx, TG_X, cols, wqT, wo, kT, vT, kbd, vbd):
    nc, sb, pb, sem, sems = mk
    S_X, INV_X, T0, T1 = cols
    with ExitStack() as ph:
        Ah = sb(ph, "Ah", [P, KT, INNER], F32R)
        Al = sb(ph, "Al", [P, KT, INNER], F32R)
        Vh = sb(ph, "Vh", [P, PAIRS, H], F32R)
        Vl = sb(ph, "Vl", [P, PAIRS, H], F32R)
        xn = [sb(ph, f"xn{n}", [P, H], F32) for n in range(2)]
        xh = [sb(ph, f"xh{n}", [P, H], F32R) for n in range(2)]
        xl = [sb(ph, f"xl{n}", [P, H], F32R) for n in range(2)]
        pr = [sb(ph, f"pr{n}", [P, INNER], F32) for n in range(2)]
        pTh = sb(ph, "pTh", [P, INNER], F32R)
        pTl = sb(ph, "pTl", [P, INNER], F32R)
        x1 = [sb(ph, f"x1{n}", [P, H], F32) for n in range(2)]
        x2 = [sb(ph, f"x2{n}", [P, H], F32) for n in range(2)]
        st = sb(ph, "st", [P, 2, 6], F32)
        mv = sb(ph, "mv", [P, 2, 2], F32)
        rs = sb(ph, "rs", [P, 2, 2], F32)
        st2 = sb(ph, "st2", [P, 2, 6], F32)
        mv2 = sb(ph, "mv2", [P, 2, 2], F32)
        rs2 = sb(ph, "rs2", [P, 2, 2], F32)
        smx = sb(ph, "smx", [P, 2, HEADS], F32)
        ssum = sb(ph, "ssum", [P, 2, HEADS], F32)
        srec = sb(ph, "srec", [P, 2, HEADS], F32)
        pS = [pb(ph, f"pS{n}", 1024) for n in range(2)]
        pT = pb(ph, "pT", 1024)
        pX = pb(ph, "pX")
        pO = pb(ph, "pO")

        (stats_done, mean_done, eps_done, rstd_done, xn_done, xT_ps, xh_done, xl_done,
         s_ps, max_done, sub_done, exp_done, sum_done, rec_done, prob_done,
         o_ps, x1_done, stats2_done, mean2_done, eps2_done, rstd2_done, x2_done, x2max_done) = (sem(n, 8) for n in
            """stats mean eps rstd xn xT_ps xh xl s_ps max sub exp sum rec prob
               o_ps x1 stats2 mean2 eps2 rstd2 x2 x2max""".split())
        pT_ps, pTh_done, pTl_done = (sem(n, 16) for n in ("pT_ps", "pTh", "pTl"))
        kbd_set, vbd_set = sem("kbd_set", 2), sem("vbd_set", 2)
        masked, apart, sx_red, sx_all, sx_scale = (sem(n) for n in ("masked", "apart", "sx_red", "sx_all", "sx_scale"))
        ch_ps, ch_hi, ch_lo = sem("ch_ps"), sem("ch_hi"), sem("ch_lo", 2)
        x1_out = [sem(f"x1_out{n}", 16) for n in range(2)]
        x2_out = [sem(f"x2_out{n}", 16) for n in range(2)]
        block = ph.enter_context(nc.Block())
        NCH = 16

        def schedule(eng, step):
            for k in range(-2, 3):
                step(0, k, lambda j: j >= 0)
            with eng.Fori(0, B - 1) as b:
                for k in range(3, BQ + 3):
                    step(b, k, lambda j: True)
            for k in range(3, BQ + 3):
                step(B - 1, k, lambda j: j < BQ)

        def matrices(k, have):
            if k in (0, 1):
                return k, 0
            if k in (BQ, BQ + 1) and have(k):
                return k - BQ, 1
            return None, 0

        halves = [slice(h * 512, h * 512 + 512) for h in range(2)]

        def part(s, b, j, h):
            return at(s, 2 * BQ * b, 2 * j + h + 1)

        def tile(s, b, j):
            return at(s, BQ * b, j + 1)

        @block.sync
        def _(sp):
            def step(b, k, have):
                j = k - 3
                if have(j):
                    n = j % 2
                    sp.wait_ge(*tile(x1_done, b, j))
                    sp.dma_start(x1_d[bass.ds(S * b + j * P, P), :], x1[n][:, :]).then_inc(x1_out[n], 16)
                    if have(j + BQ):
                        sp.dma_start(xin[j % BQ][:, :], xf[bass.ds(S * b + (j + BQ) * P, P), :]).then_inc(x_in[j % BQ], 16)
                    sp.wait_ge(*tile(x2_done, b, j))
                    sp.dma_start(xn_d[bass.ds(S * b + j * P, P), :], x2[n][:, :]).then_inc(x2_out[n], 16)

            schedule(sp, step)
            for n in range(2):
                sp.wait_ge(*at(x1_out[n], 0, 16 * QT // 2))
                sp.wait_ge(*at(x2_out[n], 0, 16 * QT // 2))

        @block.gpsimd
        def _(pool):
            head_starts(pool, sems)

            def rstd(b, j, mv_, rs_, mean_s, eps_s, rstd_s, used):
                pool.wait_ge(*tile(mean_s, b, j))
                pool.wait_ge(*tile(used, b, j - 2))
                pool.tensor_tensor(rs_[:, j % 2, 0:1], mv_[:, j % 2, 1:2], half[:, 1:2], ALU.add).then_inc(eps_s, 1)
                pool.wait_ge(*tile(eps_s, b, j))
                pool.tensor_tensor(rs_[:, j % 2, 1:2], rs_[:, j % 2, 0:1], half[:, 0:1], ALU.pow).then_inc(rstd_s, 1)

            def step(b, k, have):
                if have(k + 2):
                    rstd(b, k + 2, mv, rs, mean_done, eps_done, rstd_done, xn_done)
                if have(k - 3):
                    rstd(b, k - 3, mv2, rs2, mean2_done, eps2_done, rstd2_done, x2_done)
                if have(k - 1):
                    j = k - 1
                    pool.wait_ge(*tile(rec_done, b, j))
                    p3 = pr[j % 2][:, :].rearrange("p (h c) -> p h c", c=CK)
                    pool.tensor_tensor(p3, p3, srec[:, j % 2, :].unsqueeze(2).to_broadcast([P, HEADS, CK]),
                                       ALU.mult).then_inc(prob_done, 1)

            schedule(pool, step)
            pool.wait_ge(sx_red, 1)
            pool.partition_all_reduce(T1, T0, P, RMAX).then_inc(sx_all, 1)

        @block.scalar
        def _(act):
            def step(b, k, have):
                which, ahead = matrices(k, have)
                if k == 5 and have(BQ):
                    diagonal(act, kT, vT, kbd, vbd, b + 1, kbd_set, vbd_set)
                if have(k - 2):
                    j = k - 2
                    act.wait_ge(*tile(o_ps, b, j - 1))
                    for h, cs in enumerate(halves):
                        act.wait_ge(*part(pT_ps, b, j, h))
                        act.activation(pTh[:, cs], pT[:, cs], ACT.Copy).then_inc(pTh_done, 1)

                def exponentials():
                    if have(k - 1):
                        j = k - 1
                        act.wait_ge(*tile(sub_done, b, j))
                        act.activation(pr[j % 2][:, :], pr[j % 2][:, :], ACT.Exp).then_inc(exp_done, 1)

                def high():
                    if have(k + 1):
                        j = k + 1
                        act.wait_ge(*tile(xT_ps, b, j))
                        act.wait_ge(*tile(s_ps, b, j - 2))
                        act.activation(xh[j % 2][:, :], pX[:, :], ACT.Copy).then_inc(xh_done, 1)

                if which != 0:
                    exponentials()
                    high()
                for n in range(8) if which is not None else ():
                    if which == 0 and n == 2:
                        exponentials()
                    act.wait_ge(*at(ch_ps, NCH * b, NCH * ahead + 8 * which + n + 1))
                    if which == 0:
                        act.activation(Ah[:, n // 2, (n % 2) * 512:(n % 2 + 1) * 512], pT[:, (n % 2) * 512:(n % 2 + 1) * 512],
                                       ACT.Copy, scale=SCALE).then_inc(ch_hi, 1)
                    else:
                        act.activation(Vh[:, n, :], pT[:, (n % 2) * 512:(n % 2 + 1) * 512], ACT.Copy).then_inc(ch_hi, 1)
                if which == 0:
                    high()

            schedule(act, step)

        @block.vector
        def _(dve):
            def chunk_low(b, ahead, which, n):
                dve.wait_ge(*at(ch_hi, NCH * b, NCH * ahead + 8 * which + n + 1))
                bank = pT[:, (n % 2) * 512:(n % 2 + 1) * 512]
                if which == 0:
                    cs = slice((n % 2) * 512, (n % 2 + 1) * 512)
                    dve.scalar_tensor_tensor(out=Al[:, n // 2, cs], in0=bank, scalar=SCALE, in1=Ah[:, n // 2, cs].bitcast(F32),
                                             op0=ALU.mult, op1=ALU.subtract).then_inc(ch_lo, 1)
                else:
                    dve.tensor_tensor(Vl[:, n, :], bank, Vh[:, n, :].bitcast(F32), ALU.subtract).then_inc(ch_lo, 1)

            def scores_down(b, j):
                n = j % 2
                s3 = pS[n][:, :].rearrange("p (h c) -> p h c", c=CK)
                p3 = pr[n][:, :].rearrange("p (h c) -> p h c", c=CK)
                dve.wait_ge(*tile(s_ps, b, j))
                dve.wait_ge(*part(pT_ps, b, j - 2, 1))
                src = s3
                if j % BQ == 0:
                    dve.tensor_tensor(p3, s3, mask[:, :].unsqueeze(1).to_broadcast([P, HEADS, CK]), ALU.add).then_inc(masked, 1)
                    dve.wait_ge(masked, b + (j // BQ + 1))
                    src = p3
                dve.tensor_reduce(smx[:, n, :], src, X, ALU.max).then_inc(max_done, 1)
                dve.wait_ge(*tile(max_done, b, j))
                dve.tensor_tensor(p3, src, smx[:, n, :].unsqueeze(2).to_broadcast([P, HEADS, CK]), ALU.subtract).then_inc(sub_done, 1)

            def statistics(b, j):
                n = j % 2
                dve.wait_ge(*at(x_in[j % BQ], 16 * b, 16 * (j // BQ + 1)))
                dve.wait_ge(*tile(mean_done, b, j - 2))
                dve.bn_stats(st[:, n, :], xin[j % BQ][:, :]).then_inc(stats_done, 1)
                dve.wait_ge(*tile(stats_done, b, j))
                dve.wait_ge(*tile(xn_done, b, j - 2))
                dve.sem_inc(apart, 1)
                dve.bn_aggr(mv[:, n, :], st[:, n, :]).then_inc(mean_done, 1)

            def residual(b, j):
                n = j % 2
                dve.wait_ge(*tile(o_ps, b, j))
                dve.wait_ge(*at(x1_out[n], 8 * BQ * b, 16 * (j // 2)))
                dve.wait_ge(*tile(x2_done, b, j - 2))
                dve.scalar_tensor_tensor(out=x1[n][:, :], in0=pO[:, :], scalar=TG_X, in1=xin[j % BQ][:, :],
                                         op0=ALU.mult, op1=ALU.add).then_inc(x1_done, 1)
                dve.wait_ge(*tile(x1_done, b, j))
                dve.bn_stats(st2[:, n, :], x1[n][:, :]).then_inc(stats2_done, 1)
                dve.wait_ge(*tile(stats2_done, b, j))
                dve.sem_inc(apart, 1)
                dve.bn_aggr(mv2[:, n, :], st2[:, n, :]).then_inc(mean2_done, 1)

            def sums(b, j):
                n = j % 2
                dve.wait_ge(*tile(exp_done, b, j))
                dve.tensor_reduce(ssum[:, n, :], pr[n][:, :].rearrange("p (h c) -> p h c", c=CK), X, ALU.add).then_inc(sum_done, 1)
                dve.wait_ge(*tile(sum_done, b, j))
                dve.wait_ge(*tile(prob_done, b, j - 2))
                dve.reciprocal(srec[:, n, :], ssum[:, n, :]).then_inc(rec_done, 1)

            def normal(b, j):
                dve.wait_ge(*tile(rstd_done, b, j))
                dve.wait_ge(*tile(xT_ps, b, j - 2))
                dve.tensor_scalar(xn[j % 2][:, :], xin[j % BQ][:, :], mv[:, j % 2, 0:1], rs[:, j % 2, 1:2],
                                  ALU.subtract, ALU.mult).then_inc(xn_done, 1)

            def normal2(b, j):
                n = j % 2
                dve.wait_ge(*tile(rstd2_done, b, j))
                dve.wait_ge(*at(x2_out[n], 8 * BQ * b, 16 * (j // 2)))
                dve.wait_ge(*tile(x2max_done, b, j - 2))
                dve.tensor_scalar(x2[n][:, :], x1[n][:, :], mv2[:, n, 0:1], rs2[:, n, 1:2],
                                  ALU.subtract, ALU.mult).then_inc(x2_done, 1)
                dve.wait_ge(*tile(x2_done, b, j))
                dve.tensor_reduce(xmx[:, bass.ds(BQ * b + j, 1)], x2[n][:, :], X, ALU.max,
                                  apply_absolute_value=True).then_inc(x2max_done, 1)

            def step(b, k, have):
                which, ahead = matrices(k, have)
                chunks = [lambda n=n: chunk_low(b, ahead, which, n) for n in range(8)] if which is not None else []

                def some(n):
                    for _ in range(min(n, len(chunks))):
                        chunks.pop(0)()

                if have(k - 2):
                    j = k - 2
                    for h, cs in enumerate(halves):
                        dve.wait_ge(*part(pTh_done, b, j, h))
                        dve.tensor_tensor(pTl[:, cs], pT[:, cs], pTh[:, cs].bitcast(F32), ALU.subtract).then_inc(pTl_done, 1)
                early = which is not None or not have(BQ)
                if early and have(k - 3):
                    residual(b, k - 3)
                if have(k - 1):
                    scores_down(b, k - 1)
                if not early and have(k - 3):
                    residual(b, k - 3)
                if which == 0:
                    some(2)
                if have(k + 2):
                    statistics(b, k + 2)
                some(2 if which == 0 else 1)
                if have(k - 1):
                    sums(b, k - 1)
                some(2 if which == 0 else 1)
                if have(k + 2):
                    normal(b, k + 2)
                some(1)
                if have(k - 3):
                    normal2(b, k - 3)
                some(1)
                if which == 0:
                    some(8)
                if have(k + 1):
                    j = k + 1
                    dve.wait_ge(*tile(xh_done, b, j))
                    dve.wait_ge(*tile(s_ps, b, j - 2))
                    dve.tensor_tensor(xl[j % 2][:, :], pX[:, :], xh[j % 2][:, :].bitcast(F32), ALU.subtract).then_inc(xl_done, 1)
                some(8)

            schedule(dve, step)
            dve.wait_ge(*at(x2max_done, 0, QT))
            dve.tensor_reduce(T0, xmx[:, :], X, ALU.max).then_inc(sx_red, 1)
            dve.wait_ge(sx_all, 1)
            dve.tensor_scalar(S_X, T1, 1.0 / QMAX, TINY, ALU.mult, ALU.max).then_inc(sx_scale, 1)
            dve.wait_ge(sx_scale, 1)
            dve.reciprocal(INV_X, S_X).then_inc(sx_scale, 1)
            dve.wait_ge(sx_scale, 2)

        @block.tensor
        def _(pe):
            def chunk(b, ahead, which, n):
                pe.wait_ge(*at(ch_lo, NCH * b, NCH * ahead + 8 * which + n - 1))
                bank = pT[:, (n % 2) * 512:(n % 2 + 1) * 512]
                if which == 0:
                    if n == 0:
                        pe.wait_ge(*at(kbd_set, 2 * b, 2 * ahead))
                    for q in range(4):
                        pair = (n % 2) * 4 + q
                        mm = pe.matmul(bank[:, q * P:(q + 1) * P], wqT[:, pair, (n // 2) * P:(n // 2 + 1) * P],
                                       kbd[:, pair, :], start=True, stop=True)
                else:
                    if n == 0:
                        pe.wait_ge(*at(vbd_set, 2 * b, 2 * ahead))
                    mm = pe.matmul(bank, vbd[:, n, :], wo[:, n, :], start=True, stop=True)
                mm.then_inc(ch_ps, 1)

            def values(b, k, have):
                which, ahead = matrices(k, have)
                j = k - 2
                if have(j):
                    pe.wait_ge(*tile(x1_done, b, j - 1))
                for p in range(PAIRS):
                    cs = slice(p * P, (p + 1) * P)
                    if have(j):
                        if p % 4 == 0:
                            pe.wait_ge(*part(pTl_done, b, j, p // 4))
                        for ps_, vs in ((pTh, Vh), (pTh, Vl), (pTl, Vh)):
                            mm = pe.matmul(pO[:, :], ps_[:, cs], vs[:, p, :],
                                           start=(p == 0 and ps_ is pTh and vs is Vh),
                                           stop=(p == PAIRS - 1 and ps_ is pTl))
                        if p == PAIRS - 1:
                            mm.then_inc(o_ps, 1)
                    if which is not None:
                        chunk(b, ahead, which, p)

            def scores(b, k):
                pe.wait_ge(*tile(xl_done, b, k))
                pe.wait_ge(*tile(sub_done, b, k - 2))
                for kt in range(KT):
                    cs = slice(kt * P, (kt + 1) * P)
                    if k % BQ == 0:
                        pe.wait_ge(*at(ch_lo, NCH * b, NCH * (k // BQ) + 2 * kt + 2))
                    for xs, As in ((xh, Ah), (xh, Al), (xl, Ah)):
                        for hf in range(2):
                            mm = pe.matmul(pS[k % 2][:, hf * 512:(hf + 1) * 512], xs[k % 2][:, cs],
                                           As[:, kt, hf * 512:(hf + 1) * 512],
                                           start=(kt == 0 and xs is xh and As is Ah),
                                           stop=(kt == KT - 1 and xs is xl))
                mm.then_inc(s_ps, 1)

            def step(b, k, have):
                which, ahead = matrices(k, have)
                if have(k - 2):
                    j = k - 2
                    pe.wait_ge(*tile(prob_done, b, j))
                    pe.wait_ge(*part(pTl_done, b, j - 1, 1))
                    for p in range(PAIRS):
                        if k % BQ == 2 and p % 4 == 0:
                            pe.wait_ge(*at(ch_lo, NCH * b, NCH * (k // BQ) + NCH - 1 + p // 4))
                        mm = pe.transpose(pT[:, p * P:(p + 1) * P], pr[j % 2][:, p * P:(p + 1) * P], ident[:, :])
                        if p % 4 == 3:
                            mm.then_inc(pT_ps, 1)
                if which != 0 and have(k) and k >= 0:
                    scores(b, k)
                if have(k + 1):
                    j = k + 1
                    pe.wait_ge(*tile(xn_done, b, j))
                    pe.wait_ge(*tile(xl_done, b, j - 1))
                    for kt in range(KT):
                        mm = pe.transpose(pX[:, kt * P:(kt + 1) * P], xn[j % 2][:, kt * P:(kt + 1) * P], ident[:, :])
                    mm.then_inc(xT_ps, 1)
                values(b, k, have)
                if which == 0:
                    scores(b, k)

            schedule(pe, step)


def gate_phase(mk, xn_d, xq_d, uxq, uxq_in, gate_d, wsc, w_src, W, w_in, load_w, ident, gmx, S_X, INV_X, cols):
    nc, sb, pb, sem, sems = mk
    GPOS, GNEG, AP2, AN2, AMAX, S_G, INV_G = cols
    with ExitStack() as ph:
        Wh, Wl = W
        xr = [sb(ph, f"xr{n}", [P, 4, H], F32) for n in range(2)]
        xq = [sb(ph, f"gxq{n}", [P, KT, 512], I16) for n in range(2)]
        xh = [sb(ph, f"gxh{n}", [P, KT, 512], F32R) for n in range(2)]
        xl = [sb(ph, f"gxl{n}", [P, KT, 512], F32R) for n in range(2)]
        NS = 4
        stage = [sb(ph, f"gst{n}", [P, 512], F32) for n in range(NS)]
        JR = 6
        J = Jobs(mk, ph, "gj", JR, 1)
        pX = [pb(ph, f"gpX{n}") for n in range(4)]
        pG = [pb(ph, f"gpG{n}") for n in range(3)]
        xr_in = [sem(f"g_xr_in{n}") for n in range(2)]
        xq_out = [sem(f"g_xq_out{n}", 16) for n in range(2)]
        st_out = [sem(f"g_st_out{n}", 16) for n in range(NS)]
        xT_ps, xq_done, xh_done, xl_done, g_ps, g_neg = (sem(f"g_{n}") for n in ("xT_ps", "xq", "xh", "xl", "ps", "neg"))
        g_sb, g_pos = sem("g_sb", 4), sem("g_pos", NS)
        red, all_, scl = sem("g_red"), sem("g_all"), sem("g_scl")
        block = ph.enter_context(nc.Block())

        def job_src(i, q):
            r = i + q // JR
            q = q % JR
            if isinstance(r, int):
                return w_src[1 + q // 3][r, q % 3, :, :]
            return w_src[1 + q // 3][bass.ds(r, 1), q % 3, :, :].rearrange("a p k -> (a p) k")

        def job_dst(i, q):
            if q < 3:
                return by_input(wsc[1], i, q)
            return [d.rearrange("p (i h) -> p i h", h=H)[:, 4 * (q - 3):4 * (q - 3) + 4, bass.ds(i * P, P)] for d in wsc[2]]

        def rows(T):
            return xn_d[bass.ds(T * 512, 512), :].rearrange("(q p) d -> p q d", p=P)

        def traffic(sp, i, last=False):
            for t in range(2):
                sp.wait_ge(*at(xq_done, 2 * KT * i, KT * t + KT))
                sp.dma_start(xq_d[bass.ds(2 * i + t, 1), :, :].rearrange("a p k -> (a p) k"),
                             xq[t][:, :, :].rearrange("p k n -> p (k n)")).then_inc(xq_out[t], 16)
                for it in range(IT):
                    m = IT * t + it
                    n = m % NS
                    sp.wait_ge(*at(g_sb, 2 * IT * i, m + 1))
                    sp.dma_start(gate_d[bass.ds(8 * i + 4 * t, 4), :, it * P:(it + 1) * P].rearrange("q p n -> p q n"),
                                 stage[n][:, :].rearrange("p (q n) -> p q n", q=4)).then_inc(st_out[n], 16)
                    if last and t == 1 and it in (2, 5, 8):
                        c = it // 3
                        for n in range(NJ):
                            sp.wait_ge(*at(J.stored[n], 0, 32 * (2 * c + 1)))
                        load_w[1](sp, c)
                    if it == 6 and not last:
                        src = rows((2 * i + (t + 3)) % FT)
                        sp.wait_ge(*at(xT_ps, 2 * KT * i, KT * t + 2 * KT))
                        sp.dma_start(xr[(t + 1) % 2][:, :, :], src).then_inc(xr_in[(t + 1) % 2], 16)
                    if it in (2, 6, 10) and not (last and 3 * t + it // 4 + 2 >= JR):
                        q = 3 * t + it // 4
                        job_load(sp, J, i, q + 2, job_src(i, q + 2))
                    if it in (5, 9, 11):
                        q = 3 * t + (5, 9, 11).index(it)
                        job_store(sp, J, i, q, job_dst(i, q))

        @block.sync
        def _(sp):
            sp.dma_start(xr[0][:, :, :], rows(0)).then_inc(xr_in[0], 16)
            for c in range(4):
                load_w[0](sp, c)
                if c == 1:
                    for q in range(2):
                        job_load(sp, J, 0, q, job_src(0, q))
                if c == 2:
                    sp.dma_start(xr[1][:, :, :], rows(1)).then_inc(xr_in[1], 16)
            sp.wait_ge(*at(xT_ps, 0, KT))
            sp.dma_start(xr[0][:, :, :], rows(2)).then_inc(xr_in[0], 16)
            with sp.Fori(0, FT // 2 - 1) as i:
                traffic(sp, i)
            traffic(sp, FT // 2 - 1, last=True)
            sp.wait_ge(*at(xq_out[0], 0, 16 * FT // 2))
            sp.dma_start(uxq[:, :, :].rearrange("p k n -> p (k n)"), xq_d[0, :, :]).then_inc(uxq_in, 16)
            for n in range(NS):
                sp.wait_ge(*at(st_out[n], 0, 16 * FT * IT // NS))
            for n in range(2):
                sp.wait_ge(*at(xq_out[n], 0, 16 * FT // 2))
                sp.wait_ge(*at(xr_in[n], 0, 16 * (FT // 2 + (n == 0))))
            for n in range(NJ):
                sp.wait_ge(*at(J.stored[n], 0, 32 * JR * ROUNDS // NJ))
                sp.wait_ge(*at(J.loaded[n], 0, 16 * (JR * ROUNDS // NJ)))

        @block.scalar
        def _(act):
            def parts(i, T):
                n = T % 2
                for kt in range(KT):
                    act.wait_ge(*at(xT_ps, 2 * KT * i, KT * T + kt + 1))
                    if kt == 0:
                        act.wait_ge(*at(xq_out[n], 16 * i, 16 * (T // 2)))
                    act.activation(xq[n][:, kt, :], pX[kt][:, :], ACT.Copy, scale=INV_X).then_inc(xq_done, 1)

            def high(i, T, kt):
                act.wait_ge(*at(xq_done, 2 * KT * i, KT * T + kt + 1))
                act.activation(xh[T % 2][:, kt, :], xq[T % 2][:, kt, :], ACT.Copy).then_inc(xh_done, 1)

            parts(0, 0)
            for kt in range(KT):
                high(0, 0, kt)
            with act.Fori(0, FT // 2) as i:
                for t in range(2):
                    for it in range(IT):
                        m = IT * t + it
                        n = m % NS
                        act.wait_ge(*at(g_ps, 2 * IT * i, m + 1))
                        act.wait_ge(*at(st_out[n], 32 * IT // NS * i, 16 * (m // NS)))
                        act.wait_ge(*at(g_pos, 2 * IT * i, m - NS + 1))
                        act.activation(stage[n][:, :], pG[m % 3][:, :], ACT.Copy, scale=S_X).then_inc(g_sb, 1)
                        if it == 4:
                            parts(i, t + 1)
                        if it in range(5, 5 + KT):
                            high(i, t + 1, it - 5)
                        if it in (3, 7, 11):
                            job_hi(act, J, i, 3 * t + it // 4)

        @block.vector
        def _(dve):
            def low(i, T, kt):
                n = T % 2
                dve.wait_ge(*at(xh_done, 2 * KT * i, KT * T + kt + 1))
                dve.tensor_tensor(xl[n][:, kt, :], xq[n][:, kt, :], xh[n][:, kt, :].bitcast(F32), ALU.subtract).then_inc(xl_done, 1)

            for kt in range(KT):
                low(0, 0, kt)
            with dve.Fori(0, FT // 2) as i:
                for t in range(2):
                    for it in range(IT):
                        m = IT * t + it
                        dve.wait_ge(*at(g_sb, 2 * IT * i, m + 1))
                        dve.tensor_reduce(gmx[:, 1, bass.ds(2 * IT * i + m, 1)], stage[m % NS][:, :], X, ALU.min).then_inc(g_neg, 1)
                        dve.tensor_reduce(gmx[:, 0, bass.ds(2 * IT * i + m, 1)], stage[m % NS][:, :], X, ALU.max).then_inc(g_pos, 1)
                        if it in range(6, 6 + KT):
                            low(i, t + 1, it - 6)
                        q = 3 * t + it // 4
                        if it % 4 == 0:
                            job_scale(dve, J, i, q)
                        if it % 4 == 1:
                            job_integer(dve, J, i, q)
                        if it % 4 == 3:
                            job_lo(dve, J, i, q)
            dve.wait_ge(*at(g_pos, 0, FT * IT))
            dve.wait_ge(g_neg, FT * IT)
            dve.tensor_reduce(GPOS, gmx[:, 0, :], X, ALU.max).then_inc(red, 1)
            dve.tensor_reduce(GNEG, gmx[:, 1, :], X, ALU.min, negate=True).then_inc(red, 1)
            dve.wait_ge(all_, 2)
            dve.tensor_tensor(AMAX, AP2, AN2, ALU.max).then_inc(scl, 1)
            dve.wait_ge(scl, 1)
            dve.tensor_scalar(S_G, AMAX, 1.0 / QMAX, TINY, ALU.mult, ALU.max).then_inc(scl, 1)
            dve.wait_ge(scl, 2)
            dve.reciprocal(INV_G, S_G).then_inc(scl, 1)
            dve.wait_ge(scl, 3)

        @block.gpsimd
        def _(pool):
            head_starts(pool, sems)
            with pool.Fori(0, FT // 2) as i:
                for q in range(JR):
                    job_divide(pool, J, i, q)
            pool.wait_ge(red, 2)
            pool.partition_all_reduce(AP2, GPOS, P, RMAX).then_inc(all_, 1)
            pool.partition_all_reduce(AN2, GNEG, P, RMAX).then_inc(all_, 1)

        @block.tensor
        def _(pe):
            def transposes(i, T):
                n = T % 2
                pe.wait_ge(*at(xr_in[n], 16 * i, 16 * (T // 2 + 1)))
                for kt in range(KT):
                    if T:
                        pe.wait_ge(*at(xq_done, 2 * KT * i, KT * (T - 1) + kt + 1))
                    for q in range(4):
                        mm = pe.transpose(pX[kt][:, q * P:(q + 1) * P], xr[n][:, q, kt * P:(kt + 1) * P], ident[:, :])
                    mm.then_inc(xT_ps, 1)

            transposes(0, 0)
            with pe.Fori(0, FT // 2) as i:
                for t in range(2):
                    for it in range(IT):
                        m = IT * t + it
                        if it % 3 == 0:
                            pe.wait_ge(w_in[it // 3], 32)
                        pe.wait_ge(*at(g_sb, 2 * IT * i, m - 2))
                        if it == 0:
                            ready = lambda kt: pe.wait_ge(*at(xl_done, 2 * KT * i, KT * t + kt + 1))
                        else:
                            ready = None
                        product(pe, pG[m % 3], Wh, Wl, xh[t], xl[t], it, ready).then_inc(g_ps, 1)
                        if it == 3:
                            transposes(i, t + 1)
                        if it % 4 == 3:
                            job_turn(pe, J, i, 3 * t + it // 4, ident)


def product(pe, ps, Wh, Wl, xh, xl, it, ready):
    for kt in range(KT):
        if ready:
            ready(kt)
        for Ws, xs in ((Wh, xh), (Wh, xl), (Wl, xh)):
            mm = pe.matmul(ps[:, :], Ws[:, it, kt * P:(kt + 1) * P], xs[:, kt, :],
                           start=(kt == 0 and Ws is Wh and xs is xh), stop=(kt == KT - 1 and Ws is Wl))
    return mm


def up_phase(mk, xq_d, xq, xq_in, gate_d, up_d, W, w_in, load_w, nq, umx, fmx, sci, scu, S_X, cols, tmp):
    nc, sb, pb, sem, sems = mk
    S_G, INV_G, GMAX, S_F2, C_F, S_U, INV_U = cols
    T0, T1, T2, T3, T4 = tmp
    with ExitStack() as ph:
        Wh, Wl = W
        xh = [sb(ph, f"uxh{n}", [P, KT, 512], F32R) for n in range(2)]
        xl = [sb(ph, f"uxl{n}", [P, KT, 512], F32R) for n in range(2)]
        NS = 3
        stage = [sb(ph, f"ust{n}", [P, 512], F32) for n in range(NS)]
        GA = 3
        GW = I // GA
        NG, NN, NM = 6, 4, 3
        gb = [sb(ph, f"gb{n}", [P, GW], F32) for n in range(NG)]
        nb = [sb(ph, f"nb{n}", [P, GW], I16) for n in range(NN)]
        mb = [sb(ph, f"mb{n}", [P, GW], U16) for n in range(NM)]
        pU = [pb(ph, f"pU{n}") for n in range(4)]
        HT = FT // 2
        SPLIT_AT = (1, 3, 5, 7)
        GROUPS = QT * I // GW
        GR = GROUPS // HT
        g_in = [sem(f"u_g_in{n}") for n in range(NG)]
        st_out = [sem(f"u_st_out{n}", 16) for n in range(NS)]
        xh_done, xl_done, u_ps = (sem(f"u_{n}") for n in ("xh", "xl", "ps"))
        u_sb, u_max = sem("u_sb", 4), sem("u_max", NS)
        n_done, sig_done = sem("u_n"), sem("u_sig")
        m_done, f_done, kept = sem("u_m", NG), sem("u_f", NG), sem("u_kept", NG)
        link_s, red, all_, pos_n, pos_sig, pos_m, fmx_set, apart_p, apart_v = (sem(f"u_{n}") for n in
            ("link", "red", "all", "pos_n", "pos_sig", "pos_m", "fmx_set", "apart_p", "apart_v"))
        block = ph.enter_context(nc.Block())
        sig_at = {it: [gr for gr in range(GR) if gr * (IT - 1) // GR == it] for it in range(IT)}
        end_at = {it: sig_at.get(it - 1, []) for it in range(IT)}
        gate_g = gate_d.rearrange("q p (a k) -> q p a k", a=GA)

        def group(i, t, gr):
            return nq[:, bass.ds(2 * GR // GA * i + (GR // GA * t + gr // GA), 1), (gr % GA) * GW:(gr % GA + 1) * GW].rearrange("p a k -> p (a k)")

        def traffic(sp, h, i, last=False):
            for t in range(2):
                T = t + HT * h
                src = xq_d[bass.ds((2 * i + (T + 1)) % FT, 1), :, :].rearrange("a p k -> (a p) k")
                sp.wait_ge(*at(xl_done, 2 * KT * i, KT * (T + 1)))
                sp.dma_start(xq[:, :, :].rearrange("p k n -> p (k n)"), src).then_inc(xq_in, 16)
                for it in range(IT):
                    n = it % NS
                    sp.wait_ge(*at(u_sb, 2 * IT * i, IT * T + it + 1))
                    sp.dma_start(up_d[bass.ds(8 * i + 4 * T, 4), :, it * P:(it + 1) * P].rearrange("q p n -> p q n"),
                                 stage[n][:, :].rearrange("p (q n) -> p q n", q=4)).then_inc(st_out[n], 16)
                    for gr in end_at[it] if h == 0 else ():
                        refill(sp, i, t, gr)
                    if last and t == 1 and it in (2, 5, 8):
                        load_w[2](sp, it // 3)

        def refill(sp, i, t, gr):
            src = gate_g[bass.ds((2 * GR // GA * i + (GR // GA * t + (gr + NG) // GA)) % QT, 1), :, gr % GA, :].rearrange("a p k -> (a p) k")
            sp.wait_ge(*at(f_done, 2 * GR * i, GR * t + gr + 1))
            sp.dma_start(gb[gr % NG][:, :], src)\
              .then_inc(g_in[gr % NG], 16)

        @block.sync
        def _(sp):
            for n in range(NG):
                sp.dma_start(gb[n][:, :], gate_g[n // GA, :, n % GA, :]).then_inc(g_in[n], 16)
            load_w[1](sp, 3)
            with sp.Fori(0, HT // 2) as i:
                traffic(sp, 0, i)
            with sp.Fori(0, HT // 2 - 1) as i:
                traffic(sp, 1, i)
            traffic(sp, 1, HT // 2 - 1, last=True)
            for n in range(NS):
                sp.wait_ge(*at(st_out[n], 0, 16 * FT * IT // NS))
            sp.wait_ge(xq_in, 16 * (FT + 1))
            for n in range(NG):
                sp.wait_ge(g_in[n], 16 * (GROUPS // NG + 1))

        @block.gpsimd
        def _(pool):
            head_starts(pool, sems)

            def integer(i, t, gr):
                n = gr % NG
                pool.wait_ge(*at(kept, 2 * GR * i, GR * t + gr - NN + 1))
                pool.wait_ge(*at(g_in[n], 32 * GR // NG * i, 16 * GR // NG * t + 16 * (gr // NG) + 16))
                pool.sem_inc(apart_p, 1)
                pool.tensor_scalar(nb[gr % NN][:, :], gb[n][:, :], INV_G, 0.0, ALU.mult, ALU.add).then_inc(n_done, 1)

            def sigmoid_int(h, i, t, gr):
                g0 = GR * t + gr + GROUPS * h
                pool.wait_ge(*at(f_done, 2 * GR * i, g0 - NM + 1))
                pool.wait_ge(*at(sig_done, 2 * GR * i, g0 + 1))
                pool.sem_inc(apart_p, 1)
                pool.tensor_scalar(mb[gr % NM][:, :], gb[gr % NG][:, :], SIG_ONE, 0.0, ALU.mult, ALU.add).then_inc(m_done, 1)

            for h in range(2):
                with pool.Fori(0, HT // 2) as i:
                    for t in range(2):
                        for gr in range(GR):
                            if h == 0:
                                integer(i, t, gr)
                            if gr >= 1:
                                sigmoid_int(h, i, t, gr - 1)
                        sigmoid_int(h, i, t, GR - 1)
                if h == 0:
                    pool.wait_ge(red, 1)
                    pool.partition_all_reduce(T1, T0, P, RMAX).then_inc(all_, 1)
            pool.wait_ge(red, 2)
            pool.partition_all_reduce(T1, T0, P, RMAX).then_inc(all_, 1)

        @block.scalar
        def _(act):
            act.wait_ge(xq_in, 16)
            for kt in range(KT):
                act.activation(xh[0][:, kt, :], xq[:, kt, :], ACT.Copy).then_inc(xh_done, 1)
            act.wait_ge(pos_n, 1)
            act.activation(T3, sci[:, 0:1], ACT.Sigmoid, scale=S_G).then_inc(pos_sig, 1)
            for h in range(2):
                if h == 1:
                    for n in range(NG):
                        act.wait_ge(g_in[n], 16 * (GROUPS // NG + 1))
                with act.Fori(0, HT // 2) as i:
                    for t in range(2):
                        T = t + HT * h
                        for it in range(IT):
                            n = it % NS
                            m = IT * T + it
                            act.wait_ge(*at(u_ps, 2 * IT * i, m + 1))
                            act.wait_ge(*at(st_out[n], 32 * IT // NS * i, 16 * (m // NS)))
                            act.wait_ge(*at(u_max, 2 * IT * i, m - NS + 1))
                            act.activation(stage[n][:, :], pU[it % 4][:, :], ACT.Copy, scale=S_X).then_inc(u_sb, 1)
                            for gr in sig_at[it]:
                                g0 = GR * t + gr + GROUPS * h
                                if h == 0:
                                    act.wait_ge(*at(n_done, 2 * GR * i, g0 + 1))
                                    src = nb[gr % NN][:, :]
                                else:
                                    act.wait_ge(*at(m_done, 2 * GR * i, g0 - NG + 1))
                                    src = group(i, t, gr)
                                act.activation(gb[gr % NG][:, :], src, ACT.Sigmoid, scale=S_G).then_inc(sig_done, 1)
                            if it in SPLIT_AT:
                                kt = SPLIT_AT.index(it)
                                act.wait_ge(*at(xq_in, 32 * i, 16 * T + 32))
                                act.activation(xh[(t + 1) % 2][:, kt, :], xq[:, kt, :], ACT.Copy).then_inc(xh_done, 1)

        @block.vector
        def _(dve):
            seq = [0]

            def link(ins):
                seq[0] += 1
                ins.then_inc(link_s, 1)
                dve.wait_ge(link_s, seq[0])

            dve.memset(fmx[:, 0:NG], 0.0).then_inc(fmx_set, 1)
            dve.wait_ge(fmx_set, 1)
            dve.tensor_scalar(sci[:, 0:1], GMAX, INV_G, None, ALU.mult).then_inc(pos_n, 1)
            for kt in range(KT):
                dve.wait_ge(xh_done, kt + 1)
                dve.tensor_tensor(xl[0][:, kt, :], xq[:, kt, :], xh[0][:, kt, :].bitcast(F32), ALU.subtract).then_inc(xl_done, 1)
            dve.wait_ge(pos_sig, 1)
            dve.tensor_scalar(scu[:, 0:1], T3, SIG_ONE, None, ALU.mult).then_inc(pos_m, 1)
            for h in range(2):
                with dve.Fori(0, HT // 2) as i:
                    for t in range(2):
                        T = t + HT * h
                        for it in range(IT):
                            m = IT * T + it
                            for gr in end_at[it]:
                                g0 = GR * t + gr + GROUPS * h
                                dve.wait_ge(*at(m_done, 2 * GR * i, g0 + 1))
                                if h == 0:
                                    dve.wait_ge(*at(kept, 2 * GR * i, g0 - 1))
                                    dve.sem_inc(apart_v, 1)
                                    dve.tensor_tensor_reduce(out=gb[gr % NG][:, :], in0=nb[gr % NN][:, :], in1=mb[gr % NM][:, :],
                                                             scale=-1.0, scalar=fmx[:, gr % NG:gr % NG + 1], op0=ALU.mult, op1=ALU.max,
                                                             accum_out=fmx[:, gr % NG:gr % NG + 1]).then_inc(f_done, 1)
                                    dve.tensor_copy(group(i, t, gr), nb[gr % NN][:, :]).then_inc(kept, 1)
                                else:
                                    dve.scalar_tensor_tensor(out=group(i, t, gr), in0=group(i, t, gr), scalar=C_F, in1=mb[gr % NM][:, :],
                                                             op0=ALU.mult, op1=ALU.mult).then_inc(f_done, 1)
                            dve.wait_ge(*at(u_sb, 2 * IT * i, m + 1))
                            dve.tensor_reduce(umx[:, bass.ds(2 * IT * i + m, 1)], stage[it % NS][:, :], X, ALU.max,
                                              apply_absolute_value=True).then_inc(u_max, 1)
                            if it - 1 in SPLIT_AT:
                                kt = SPLIT_AT.index(it - 1)
                                dve.wait_ge(*at(xh_done, 2 * KT * i, KT * (T + 1) + kt + 1))
                                dve.tensor_tensor(xl[(t + 1) % 2][:, kt, :], xq[:, kt, :], xh[(t + 1) % 2][:, kt, :].bitcast(F32),
                                                  ALU.subtract).then_inc(xl_done, 1)
                if h == 0:
                    dve.wait_ge(*at(f_done, 0, GROUPS))
                    dve.tensor_reduce(T0, fmx[:, 0:NG], X, ALU.max).then_inc(red, 1)
                    dve.wait_ge(all_, 1)
                    dve.wait_ge(pos_m, 1)
                    link(dve.tensor_copy(T2, sci[:, 0:1]))
                    link(dve.tensor_copy(T3, scu[:, 0:1]))
                    link(dve.tensor_tensor(T4, T2, T3, ALU.mult))
                    link(dve.tensor_tensor(T2, T4, T1, ALU.max))
                    link(dve.tensor_scalar(T3, S_G, 1.0 / SIG_ONE, None, ALU.mult))
                    link(dve.tensor_tensor(T4, T2, T3, ALU.mult))
                    link(dve.tensor_scalar(S_F2, T4, 1.0 / QMAX, TINY, ALU.mult, ALU.max))
                    link(dve.reciprocal(T2, S_F2))
                    link(dve.tensor_tensor(C_F, T2, T3, ALU.mult))
            dve.wait_ge(*at(u_max, 0, FT * IT))
            dve.tensor_reduce(T0, umx[:, :], X, ALU.max).then_inc(red, 1)
            dve.wait_ge(all_, 2)
            link(dve.tensor_scalar(S_U, T1, 1.0 / QMAX, TINY, ALU.mult, ALU.max))
            link(dve.reciprocal(INV_U, S_U))

        @block.tensor
        def _(pe):
            for h in range(2):
                with pe.Fori(0, HT // 2) as i:
                    for t in range(2):
                        T = t + HT * h
                        for it in range(IT):
                            if it % 3 == 0:
                                pe.wait_ge(w_in[it // 3], 32)
                            pe.wait_ge(*at(u_sb, 2 * IT * i, IT * T + it - 3))
                            if it == 0:
                                ready = lambda kt: pe.wait_ge(*at(xl_done, 2 * KT * i, KT * T + kt + 1))
                            else:
                                ready = None
                            product(pe, pU[it % 4], Wh, Wl, xh[t], xl[t], it, ready).then_inc(u_ps, 1)


def down_phase(mk, up_d, x1_d, of, W, w_in, load_w, nq, pmx, cols, tmp):
    nc, sb, pb, sem, sems = mk
    S_F2, S_U, INV_U, S_O, C_O, C_OUT, TG_F = cols
    T0, T1, T2, T3 = tmp
    with ExitStack() as dn:
        Wh, Wl = W

        NU = 4
        ub = [sb(dn, f"dub{n}", [P, I], F32) for n in range(2)]
        ui = [sb(dn, f"dui{n}", [P, I], I16) for n in range(2)]
        u_in = [sem(f"d_u_in{n}") for n in range(2)]
        x_in = [sem(f"d_x_in{n}") for n in range(2)]
        y_out = [sem(f"d_y_out{n}", 16) for n in range(2)]
        ui_done, o_done, oh_done, ol_done, d_ps, y_done = (sem(f"d_{n}", 4) for n in ("ui", "o", "oh", "ol", "ps", "y"))
        d_sems = [*y_out, ui_done, o_done, oh_done, ol_done, d_ps, y_done]

        def load_up(sp, i, g):
            src = up_d[bass.ds(NU * i + g, 1), :, :].rearrange("a p k -> (a p) k")
            sp.wait_ge(*at(ui_done, NU * i, g - 1))
            sp.dma_start(ub[g % 2][:, :], src).then_inc(u_in[g % 2], 16)

        def integers(act, i, g):
            act.wait_ge(*at(u_in[g % 2], 16 * NU // 2 * i, 16 * (g // 2 + 1)))
            act.wait_ge(*at(o_done, NU * i, g - 1))
            act.activation(ui[g % 2][:, :], ub[g % 2][:, :], ACT.Copy, scale=INV_U).then_inc(ui_done, 1)

        def row_tile(g):
            return nq[:, bass.ds(g, 1), :].rearrange("p a k -> p (a k)")

        with ExitStack() as ph:
            NB = 4
            BY_ABS = 3
            xub = ub + [sb(ph, f"xub{n}", [P, I], F32) for n in range(2, NB)]
            xui = ui + [sb(ph, f"xui{n}", [P, I], I16) for n in range(2, NB)]
            ga = [sb(ph, f"xga{n}", [P, I], I16) for n in range(BY_ABS)]
            pp = [sb(ph, f"xpp{n}", [P, I], F32) for n in range(2)]
            xu_in = [sem(f"x_u_in{n}") for n in range(NB)]
            xui_done, us_done, p_done = sem("x_ui", BY_ABS), sem("x_us", 1), sem("x_p", NB)
            ga_done, prod, pmx_set, apart, apart_p, link_s, red, all_ = (sem(f"x_{n}") for n in
                ("ga", "prod", "pmx_set", "apart", "apart_p", "link", "red", "all"))
            x_sems = [xui_done, us_done, p_done]
            block = ph.enter_context(nc.Block())

            @block.sync
            def _(sp):
                with sp.Fori(0, QT // NB) as i:
                    for n in range(NB):
                        if n < BY_ABS:
                            sp.wait_ge(*at(xui_done, BY_ABS * i, n - BY_ABS + 1))
                        else:
                            sp.wait_ge(*at(us_done, i, 0))
                        sp.dma_start(xub[n][:, :], up_d[bass.ds(NB * i + n, 1), :, :].rearrange("a p k -> (a p) k")).then_inc(xu_in[n], 16)
                sp.wait_ge(*at(xui_done, 0, BY_ABS * QT // NB))
                for g in range(2):
                    load_up(sp, 0, g)
                load_w(sp, 3)

            @block.scalar
            def _(act):
                with act.Fori(0, QT // NB) as i:
                    for n in range(NB):
                        if n < BY_ABS:
                            act.wait_ge(*at(p_done, NB * i, n - NB + 1))
                            act.wait_ge(*at(xu_in[n], 16 * i, 16))
                            act.activation(xui[n][:, :], xub[n][:, :], ACT.Abs, scale=INV_U).then_inc(xui_done, 1)
                            act.activation(ga[n][:, :], row_tile(NB * i + n), ACT.Abs).then_inc(ga_done, 1)
                act.wait_ge(*at(p_done, 0, QT - 2))
                for g in range(2):
                    integers(act, 0, g)

            @block.vector
            def _(dve):
                seq = [0]

                def link(ins):
                    seq[0] += 1
                    ins.then_inc(link_s, 1)
                    dve.wait_ge(link_s, seq[0])

                dve.memset(pmx[:, :], 0.0).then_inc(pmx_set, 1)
                dve.wait_ge(pmx_set, 1)
                with dve.Fori(0, QT // NB) as i:
                    for n in range(NB):
                        dve.wait_ge(*at(p_done, NB * i, n - 1))
                        if n < BY_ABS:
                            dve.wait_ge(*at(ga_done, BY_ABS * i, n + 1))
                            dve.sem_inc(apart, 1)
                            dve.tensor_tensor_reduce(out=pp[n % 2][:, :], in0=ga[n][:, :], in1=xui[n][:, :], scale=1.0,
                                                     scalar=pmx[:, n:n + 1], op0=ALU.mult, op1=ALU.max,
                                                     accum_out=pmx[:, n:n + 1]).then_inc(p_done, 1)
                        else:
                            dve.wait_ge(*at(us_done, i, 1))
                            dve.tensor_tensor(pp[n % 2][:, :], row_tile(NB * i + n), xui[n][:, :], ALU.mult).then_inc(prod, 1)
                            dve.wait_ge(*at(prod, i, 1))
                            dve.tensor_reduce(pmx[:, bass.ds(i + NB, 1)], pp[n % 2][:, :], X, ALU.max,
                                              apply_absolute_value=True).then_inc(p_done, 1)
                dve.wait_ge(*at(p_done, 0, QT))
                dve.tensor_reduce(T0, pmx[:, :], X, ALU.max).then_inc(red, 1)
                dve.wait_ge(all_, 1)
                link(dve.tensor_tensor(T2, S_F2, S_U, ALU.mult))
                link(dve.tensor_tensor(T3, T1, T2, ALU.mult))
                link(dve.tensor_scalar(S_O, T3, 1.0 / QMAX, TINY, ALU.mult, ALU.max))
                link(dve.reciprocal(T0, S_O))
                link(dve.tensor_tensor(C_O, T0, T2, ALU.mult))
                link(dve.tensor_tensor(C_OUT, S_O, TG_F, ALU.mult))

            @block.gpsimd
            def _(pool):
                head_starts(pool, [*x_sems, *d_sems])
                with pool.Fori(0, QT // NB) as i:
                    n = BY_ABS
                    pool.wait_ge(*at(p_done, NB * i, n - NB + 1))
                    pool.wait_ge(*at(xu_in[n], 16 * i, 16))
                    pool.sem_inc(apart_p, 1)
                    pool.tensor_scalar(xui[n][:, :], xub[n][:, :], INV_U, 0.0, ALU.mult, ALU.add).then_inc(us_done, 1)
                pool.wait_ge(red, 1)
                pool.partition_all_reduce(T1, T0, P, RMAX).then_inc(all_, 1)

        with ExitStack() as ph:
            oq = [sb(ph, f"doq{n}", [P, I], I16) for n in range(2)]
            oh = [sb(ph, f"doh{n}", [P, I], F32R) for n in range(2)]
            ol = [sb(ph, f"dol{n}", [P, I], F32R) for n in range(2)]
            xr = [sb(ph, f"dxr{n}", [P, H], F32) for n in range(2)]
            yo = [sb(ph, f"dyo{n}", [P, H], F32) for n in range(2)]
            pD = [pb(ph, f"pD{n}") for n in range(4)]
            block = ph.enter_context(nc.Block())

            def load_x(sp, i, g):
                src = x1_d[bass.ds(NU * P * i + g * P, P), :]
                sp.wait_ge(*at(y_done, NU * i, g - 1))
                sp.dma_start(xr[g % 2][:, :], src).then_inc(x_in[g % 2], 16)

            def output(sp, i, g):
                y_dst = of[bass.ds(NU * P * i + g * P, P), :]
                sp.wait_ge(*at(y_done, NU * i, g + 1))
                sp.dma_start(y_dst, yo[g % 2][:, :]).then_inc(y_out[g % 2], 16)

            @block.sync
            def _(sp):
                for g in range(2):
                    load_x(sp, 0, g)
                load_up(sp, 0, 2)
                with sp.Fori(0, QT // NU - 1) as i:
                    for g in range(NU):
                        load_up(sp, i, g + 3)
                        output(sp, i, g)
                        load_x(sp, i, g + 2)
                for g in range(NU):
                    if g < 1:
                        load_up(sp, QT // NU - 1, g + 3)
                    output(sp, QT // NU - 1, g)
                    if g < 2:
                        load_x(sp, QT // NU - 1, g + 2)
                for n in range(2):
                    sp.wait_ge(*at(y_out[n], 0, 16 * QT // 2))

            @block.scalar
            def _(act):
                def high(i, g):
                    act.wait_ge(*at(o_done, NU * i, g + 1))
                    act.wait_ge(*at(d_ps, NU * i, g - 1))
                    act.activation(oh[g % 2][:, :], oq[g % 2][:, :], ACT.Copy).then_inc(oh_done, 1)

                high(0, 0)
                high(0, 1)
                with act.Fori(0, QT // NU - 1) as i:
                    for g in range(NU):
                        integers(act, i, g + 2)
                        high(i, g + 2)
                for g in range(2):
                    integers(act, QT // NU - 1, g + 2)
                    high(QT // NU - 1, g + 2)

            @block.vector
            def _(dve):
                def finish(i, g):
                    n = g % 2
                    dve.wait_ge(*at(d_ps, NU * i, g + 1))
                    dve.wait_ge(*at(x_in[n], 16 * NU // 2 * i, 16 * (g // 2 + 1)))
                    dve.wait_ge(*at(y_out[n], 16 * NU // 2 * i, 16 * (g // 2)))
                    dve.scalar_tensor_tensor(out=yo[n][:, :], in0=pD[g % 4][:, :], scalar=C_OUT, in1=xr[n][:, :],
                                             op0=ALU.mult, op1=ALU.add).then_inc(y_done, 1)

                def quantize(i, g):
                    n = g % 2
                    dve.wait_ge(*at(ui_done, NU * i, g + 1))
                    dve.wait_ge(*at(ol_done, NU * i, g - 1))
                    dve.scalar_tensor_tensor(out=oq[n][:, :], in0=row_tile(NU * i + g), scalar=C_O,
                                             in1=ui[n][:, :], op0=ALU.mult, op1=ALU.mult).then_inc(o_done, 1)

                def low(i, g):
                    n = g % 2
                    dve.wait_ge(*at(oh_done, NU * i, g + 1))
                    dve.tensor_tensor(ol[n][:, :], oq[n][:, :], oh[n][:, :].bitcast(F32), ALU.subtract).then_inc(ol_done, 1)

                for g in range(2):
                    quantize(0, g)
                    low(0, g)
                with dve.Fori(0, QT // NU - 1) as i:
                    for g in range(NU):
                        quantize(i, g + 2)
                        finish(i, g)
                        low(i, g + 2)
                for g in range(NU):
                    if g < 2:
                        quantize(QT // NU - 1, g + 2)
                    finish(QT // NU - 1, g)
                    if g < 2:
                        low(QT // NU - 1, g + 2)

            @block.tensor
            def _(pe):
                for c in range(4):
                    pe.wait_ge(w_in[c], 32)
                with pe.Fori(0, QT // NU) as i:
                    for g in range(NU):
                        n = g % 2
                        pe.wait_ge(*at(ol_done, NU * i, g + 1))
                        pe.wait_ge(*at(y_done, NU * i, g - 3))
                        for it in range(IT):
                            cs = slice(it * P, (it + 1) * P)
                            for os_, Ws in ((oh[n], Wh), (oh[n], Wl), (ol[n], Wh)):
                                mm = pe.matmul(pD[g % 4][:, :], os_[:, cs], Ws[:, it, :],
                                               start=(it == 0 and os_ is oh[n] and Ws is Wh),
                                               stop=(it == IT - 1 and os_ is ol[n]))
                        mm.then_inc(d_ps, 1)


_INS = ["x", "ctx_1024", "g_xattn", "g_ffn", "L0_xattn_w_q", "L0_xattn_w_k", "L0_xattn_w_v", "L0_xattn_w_o",
        "L0_ffn_w_gate", "L0_ffn_w_up", "L0_ffn_w_down"]


def kernel(**inputs):
    import numpy as _np
    import concourse.bacc as _bacc
    from concourse import mybir as _mybir
    from concourse.bass_utils import run_bass_kernel_spmd as _run

    nc = _bacc.Bacc("TRN2", target_bir_lowering=False, num_devices=1)
    arrays, args = {}, []
    for name in _INS:
        a = _np.ascontiguousarray(inputs[name])
        arrays[f"in_{name}"] = a
        args.append(nc.dram_tensor(f"in_{name}", a.shape, _mybir.dt.from_np(a.dtype), kind="ExternalInput").ap())
    out = nc.dram_tensor("out_0", (B, S, H), F32, kind="ExternalOutput").ap()
    flamingo_block(nc, *args, out)
    r = _run(nc, [arrays], core_ids=[0])
    return r.results[0]["out_0"]
```
